# Optimizing a Trainium2 kernel written in Bass

```python
import numpy as np
import jax
import jax.numpy as jnp

def _softmax(x, axis=-1):
    return jax.nn.softmax(x, axis=axis)

def _gelu(x):
    return jax.nn.gelu(x, approximate=True)

def _silu(x):
    return jax.nn.silu(x)

def _sigmoid(x):
    return jax.nn.sigmoid(x)

def _layernorm(x, axis=-1, eps=1e-05):
    m = jnp.mean(x, axis=axis, keepdims=True)
    v = jnp.var(x, axis=axis, keepdims=True)
    return (x - m) / jnp.sqrt(v + eps)

def _scatter_add(tgt, idx, src, axis=0):
    return tgt.at[idx].add(src)

def _segment_sum(src, seg, n):
    return jax.ops.segment_sum(src, seg, n)
kernel_name = 'mk_flamingo_gated_d2_seqx_r8_edef43'

def setup_inputs(seed: int=0):
    np.random.seed(seed)
    _w = jnp.asarray

    def _rec_inputs():
        import jax
        import jax.numpy as jnp
        _rk = jax.random.key(seed)
        x = -0.0002928 + 1 * jax.random.normal(jax.random.fold_in(_rk, 1), (16, 256, 128), jnp.float32)
        _lenS = 256 - jax.random.randint(jax.random.fold_in(_rk, 7), (16,), 0, max(1, 256 // 4) + 1, jnp.int32)
        _lenS2 = 64 - jax.random.randint(jax.random.fold_in(_rk, 8), (16,), 0, max(1, 64 // 4) + 1, jnp.int32)
        _ctx_512P = jax.random.normal(jax.random.fold_in(_rk, 11), (16, 16, 64), jnp.float32)
        _ctx_512c = jax.random.dirichlet(jax.random.fold_in(_rk, 511), 0.3 * jnp.ones((16,), jnp.float32), (16, 64))
        _ctx_512t = jnp.einsum('bsk,bkd->bsd', _ctx_512c, _ctx_512P)
        _ctx_512t = _ctx_512t * jax.lax.rsqrt(jnp.mean(jnp.square(_ctx_512t)) + 1e-12) * 0.953939
        ctx_512 = 0.00222621 + 0.99962 * (_ctx_512t + 0.3 * jax.random.normal(jax.random.fold_in(_rk, 611), (16, 64, 64), jnp.float32))
        _g = jax.random.normal(jax.random.fold_in(_rk, 9001), (2, 2), jnp.float32)
        _g = jnp.sign(_g) * jnp.maximum(jnp.abs(_g), 1.0) + (_g == 0) * 1.0
        g_xattn = _g[0]
        g_ffn = _g[1]
        return (x, ctx_512, g_xattn, g_ffn)
    x, ctx_512, g_xattn, g_ffn = _rec_inputs()

    def _L0_xattn_setup():
        import jax, jax.numpy as jnp
        import numpy as np
        B, T, TC, C, CC, H = (2, 256, 64, 128, 64, 16)
        D = C // H

        def _heads(t):
            b, l, _ = t.shape
            return t.reshape(b, l, H, D).transpose(0, 2, 1, 3)
        key = jax.random.key(seed)
        ks = jax.random.split(key, 18)
        w = lambda k, i, o: jax.random.normal(k, (i, o), jnp.float32) / np.sqrt(i).astype(np.float32)
        return {'x': jax.random.normal(ks[0], (B, T, C), jnp.float32), 'cross_input': jax.random.normal(ks[1], (B, TC, CC), jnp.float32), 'Wk': w(ks[2], C, C), 'bk': jnp.zeros((C,), jnp.float32), 'Wq': w(ks[3], C, C), 'bq': jnp.zeros((C,), jnp.float32), 'Wv': w(ks[4], C, C), 'bv': jnp.zeros((C,), jnp.float32), 'Wck': w(ks[5], CC, C), 'bck': jnp.zeros((C,), jnp.float32), 'Wcq': w(ks[6], C, C), 'bcq': jnp.zeros((C,), jnp.float32), 'Wcv': w(ks[7], CC, C), 'bcv': jnp.zeros((C,), jnp.float32), 'Wp': w(ks[8], C, C), 'bp': jnp.zeros((C,), jnp.float32)}
    _L0_xattn_all = _L0_xattn_setup()
    _L0_xattn_in = {k: v for k, v in _L0_xattn_all.items() if k in ('Wk', 'bk', 'Wq', 'bq', 'Wv', 'bv', 'Wck', 'bck', 'Wcq', 'bcq', 'Wcv', 'bcv', 'Wp', 'bp')}
    del _L0_xattn_all

    def _L0_ffn_setup():
        import jax, jax.numpy as jnp
        import numpy as np
        BITS = 8
        LORA_RANK = 16
        LORA_ALPHA = 32
        SCALING = LORA_ALPHA / LORA_RANK

        def fake_quant_weight(w, bits=BITS):
            qmax = 2.0 ** (bits - 1) - 1
            scale = jnp.max(jnp.abs(w)) / qmax
            wq = jnp.clip(jnp.round(w / scale), -qmax - 1, qmax) * scale
            return w + jax.lax.stop_gradient(wq - w)

        def qat_lora_linear(x, W, b, A, B):
            Wq = fake_quant_weight(W)
            base = jnp.einsum('bsi,oi->bso', x, Wq) + b
            lora = jnp.einsum('bsr,or->bso', jnp.einsum('bsi,ri->bsr', x, A), B)
            return base + SCALING * lora
        key = jax.random.key(seed)
        ks = jax.random.split(key, 9)
        d, f = (128, 512)
        s_in = 1.0 / np.sqrt(d)
        s_ff = 1.0 / np.sqrt(f)
        return {'hidden_states': jax.random.normal(ks[0], (4, 256, d), jnp.float32), 'W_fc': jax.random.normal(ks[1], (f, d), jnp.float32) * s_in, 'b_fc': jnp.zeros((f,), jnp.float32), 'A_fc': jax.random.normal(ks[2], (LORA_RANK, d), jnp.float32) * s_in, 'B_fc': jnp.zeros((f, LORA_RANK), jnp.float32), 'W_proj': jax.random.normal(ks[3], (d, f), jnp.float32) * s_ff, 'b_proj': jnp.zeros((d,), jnp.float32), 'A_proj': jax.random.normal(ks[4], (LORA_RANK, f), jnp.float32) * s_ff, 'B_proj': jnp.zeros((d, LORA_RANK), jnp.float32)}
    _L0_ffn_all = _L0_ffn_setup()
    _L0_ffn_in = {k: v for k, v in _L0_ffn_all.items() if k in ('W_fc', 'b_fc', 'A_fc', 'B_fc', 'W_proj', 'b_proj', 'A_proj', 'B_proj')}
    del _L0_ffn_all

    def _L1_xattn_setup():
        import jax, jax.numpy as jnp
        import numpy as np
        H, D, C1, C2, S, M, B, W = (16, 32, 128, 64, 256, 64, 2, 4)

        def _ln(x, g, b):
            m = jnp.mean(x, -1, keepdims=True)
            v = jnp.var(x, -1, keepdims=True)
            return (x - m) * jax.lax.rsqrt(v + 1e-05) * g + b

        def _mha(x, y, wq, wk, wv, li1_w, li1_b, lnx_g, lnx_b, lny_g, lny_b, ln3_g, ln3_b, li2_w, li2_b, li3_w, li3_b, causal):
            xn = _ln(x, lnx_g, lnx_b)
            yn = _ln(y, lny_g, lny_b)
            q = jnp.einsum('bsc,hcd->bhsd', xn, wq)
            k = jnp.einsum('btc,hcd->bhtd', yn, wk)
            v = jnp.einsum('btc,hcd->bhtd', yn, wv)
            a = jax.nn.softmax(jnp.einsum('bhsd,bhtd->bhst', q, k) * D ** (-0.5), axis=-1)
            if causal:
                s, t = (a.shape[-2], a.shape[-1])
                mask = (jnp.arange(t)[None, :] > jnp.arange(s)[:, None]).astype(a.dtype)
                a = a * mask
            o = jnp.einsum('bhst,bhtd->bhsd', a, v)
            o = o.transpose(0, 2, 1, 3).reshape(x.shape[0], x.shape[1], H * D)
            x_out = x + o @ li1_w + li1_b
            h = jax.nn.gelu(_ln(x_out, ln3_g, ln3_b) @ li2_w + li2_b, approximate=False)
            return x_out + h @ li3_w + li3_b
        key = jax.random.key(seed)
        ks = iter(jax.random.split(key, 64))

        def w(shape, scale=0.02):
            return jax.random.normal(next(ks), shape, jnp.float32) * scale
        inp = {'xx': jax.random.normal(next(ks), (B, S, C1), jnp.float32), 'ee': jax.random.normal(next(ks), (B, M, C2), jnp.float32), 'ln1_g': jnp.ones(C1, jnp.float32), 'ln1_b': jnp.zeros(C1, jnp.float32), 'ln2_g': jnp.ones(C1, jnp.float32), 'ln2_b': jnp.zeros(C1, jnp.float32)}
        for pfx, cy in (('a1', C1), ('a2', C2)):
            inp[pfx + '_wq'] = w((H, C1, D))
            inp[pfx + '_wk'] = w((H, cy, D))
            inp[pfx + '_wv'] = w((H, cy, D))
            inp[pfx + '_li1_w'] = w((H * D, C1))
            inp[pfx + '_li1_b'] = jnp.zeros(C1, jnp.float32)
            inp[pfx + '_lnx_g'] = jnp.ones(C1, jnp.float32)
            inp[pfx + '_lnx_b'] = jnp.zeros(C1, jnp.float32)
            inp[pfx + '_lny_g'] = jnp.ones(cy, jnp.float32)
            inp[pfx + '_lny_b'] = jnp.zeros(cy, jnp.float32)
            inp[pfx + '_ln3_g'] = jnp.ones(C1, jnp.float32)
            inp[pfx + '_ln3_b'] = jnp.zeros(C1, jnp.float32)
            inp[pfx + '_li2_w'] = w((C1, C1 * W))
            inp[pfx + '_li2_b'] = jnp.zeros(C1 * W, jnp.float32)
            inp[pfx + '_li3_w'] = w((C1 * W, C1))
            inp[pfx + '_li3_b'] = jnp.zeros(C1, jnp.float32)
        inp['training'] = 0
        return inp
    _L1_xattn_all = _L1_xattn_setup()
    _L1_xattn_in = {k: v for k, v in _L1_xattn_all.items() if k in ('ln1_g', 'ln1_b', 'ln2_g', 'ln2_b', 'a1_wq', 'a1_wk', 'a1_wv', 'a1_li1_w', 'a1_li1_b', 'a1_lnx_g', 'a1_lnx_b', 'a1_lny_g', 'a1_lny_b', 'a1_ln3_g', 'a1_ln3_b', 'a1_li2_w', 'a1_li2_b', 'a1_li3_w', 'a1_li3_b', 'a2_wq', 'a2_wk', 'a2_wv', 'a2_li1_w', 'a2_li1_b', 'a2_lnx_g', 'a2_lnx_b', 'a2_lny_g', 'a2_lny_b', 'a2_ln3_g', 'a2_ln3_b', 'a2_li2_w', 'a2_li2_b', 'a2_li3_w', 'a2_li3_b')}
    del _L1_xattn_all

    def _L1_ffn_setup():
        import jax, jax.numpy as jnp
        import numpy as np
        B, S, D, H, E = (4, 256, 128, 512, 8)
        key = jax.random.key(seed)
        ks = jax.random.split(key, 8)
        s_d = 1.0 / np.sqrt(D)
        s_h = 1.0 / np.sqrt(H)
        return {'x': jax.random.normal(ks[0], (B, S, D), dtype=jnp.float32), 'gate_w': jax.random.uniform(ks[1], (E, D), jnp.float32, -s_d, s_d), 'gate_b': jax.random.uniform(ks[2], (E,), jnp.float32, -s_d, s_d), 'w1': jax.random.uniform(ks[3], (E, H, D), jnp.float32, -s_d, s_d), 'b1': jax.random.uniform(ks[4], (E, H), jnp.float32, -s_d, s_d), 'w2': jax.random.uniform(ks[5], (E, D, H), jnp.float32, -s_h, s_h), 'b2': jax.random.uniform(ks[6], (E, D), jnp.float32, -s_h, s_h)}
    _L1_ffn_all = _L1_ffn_setup()
    _L1_ffn_in = {k: v for k, v in _L1_ffn_all.items() if k in ('gate_w', 'gate_b', 'w1', 'b1', 'w2', 'b2')}
    del _L1_ffn_all
    return {'x': x, 'ctx_512': ctx_512, 'g_xattn': g_xattn, 'g_ffn': g_ffn, 'L0_xattn_Wk': _L0_xattn_in['Wk'], 'L0_xattn_bk': _L0_xattn_in['bk'], 'L0_xattn_Wq': _L0_xattn_in['Wq'], 'L0_xattn_bq': _L0_xattn_in['bq'], 'L0_xattn_Wv': _L0_xattn_in['Wv'], 'L0_xattn_bv': _L0_xattn_in['bv'], 'L0_xattn_Wck': _L0_xattn_in['Wck'], 'L0_xattn_bck': _L0_xattn_in['bck'], 'L0_xattn_Wcq': _L0_xattn_in['Wcq'], 'L0_xattn_bcq': _L0_xattn_in['bcq'], 'L0_xattn_Wcv': _L0_xattn_in['Wcv'], 'L0_xattn_bcv': _L0_xattn_in['bcv'], 'L0_xattn_Wp': _L0_xattn_in['Wp'], 'L0_xattn_bp': _L0_xattn_in['bp'], 'L0_ffn_W_fc': _L0_ffn_in['W_fc'], 'L0_ffn_b_fc': _L0_ffn_in['b_fc'], 'L0_ffn_A_fc': _L0_ffn_in['A_fc'], 'L0_ffn_B_fc': _L0_ffn_in['B_fc'], 'L0_ffn_W_proj': _L0_ffn_in['W_proj'], 'L0_ffn_b_proj': _L0_ffn_in['b_proj'], 'L0_ffn_A_proj': _L0_ffn_in['A_proj'], 'L0_ffn_B_proj': _L0_ffn_in['B_proj'], 'L1_xattn_ln1_g': _L1_xattn_in['ln1_g'], 'L1_xattn_ln1_b': _L1_xattn_in['ln1_b'], 'L1_xattn_ln2_g': _L1_xattn_in['ln2_g'], 'L1_xattn_ln2_b': _L1_xattn_in['ln2_b'], 'L1_xattn_a1_wq': _L1_xattn_in['a1_wq'], 'L1_xattn_a1_wk': _L1_xattn_in['a1_wk'], 'L1_xattn_a1_wv': _L1_xattn_in['a1_wv'], 'L1_xattn_a1_li1_w': _L1_xattn_in['a1_li1_w'], 'L1_xattn_a1_li1_b': _L1_xattn_in['a1_li1_b'], 'L1_xattn_a1_lnx_g': _L1_xattn_in['a1_lnx_g'], 'L1_xattn_a1_lnx_b': _L1_xattn_in['a1_lnx_b'], 'L1_xattn_a1_lny_g': _L1_xattn_in['a1_lny_g'], 'L1_xattn_a1_lny_b': _L1_xattn_in['a1_lny_b'], 'L1_xattn_a1_ln3_g': _L1_xattn_in['a1_ln3_g'], 'L1_xattn_a1_ln3_b': _L1_xattn_in['a1_ln3_b'], 'L1_xattn_a1_li2_w': _L1_xattn_in['a1_li2_w'], 'L1_xattn_a1_li2_b': _L1_xattn_in['a1_li2_b'], 'L1_xattn_a1_li3_w': _L1_xattn_in['a1_li3_w'], 'L1_xattn_a1_li3_b': _L1_xattn_in['a1_li3_b'], 'L1_xattn_a2_wq': _L1_xattn_in['a2_wq'], 'L1_xattn_a2_wk': _L1_xattn_in['a2_wk'], 'L1_xattn_a2_wv': _L1_xattn_in['a2_wv'], 'L1_xattn_a2_li1_w': _L1_xattn_in['a2_li1_w'], 'L1_xattn_a2_li1_b': _L1_xattn_in['a2_li1_b'], 'L1_xattn_a2_lnx_g': _L1_xattn_in['a2_lnx_g'], 'L1_xattn_a2_lnx_b': _L1_xattn_in['a2_lnx_b'], 'L1_xattn_a2_lny_g': _L1_xattn_in['a2_lny_g'], 'L1_xattn_a2_lny_b': _L1_xattn_in['a2_lny_b'], 'L1_xattn_a2_ln3_g': _L1_xattn_in['a2_ln3_g'], 'L1_xattn_a2_ln3_b': _L1_xattn_in['a2_ln3_b'], 'L1_xattn_a2_li2_w': _L1_xattn_in['a2_li2_w'], 'L1_xattn_a2_li2_b': _L1_xattn_in['a2_li2_b'], 'L1_xattn_a2_li3_w': _L1_xattn_in['a2_li3_w'], 'L1_xattn_a2_li3_b': _L1_xattn_in['a2_li3_b'], 'L1_ffn_gate_w': _L1_ffn_in['gate_w'], 'L1_ffn_gate_b': _L1_ffn_in['gate_b'], 'L1_ffn_w1': _L1_ffn_in['w1'], 'L1_ffn_b1': _L1_ffn_in['b1'], 'L1_ffn_w2': _L1_ffn_in['w2'], 'L1_ffn_b2': _L1_ffn_in['b2']}

def reference(x, ctx_512, g_xattn, g_ffn, L0_xattn_Wk, L0_xattn_bk, L0_xattn_Wq, L0_xattn_bq, L0_xattn_Wv, L0_xattn_bv, L0_xattn_Wck, L0_xattn_bck, L0_xattn_Wcq, L0_xattn_bcq, L0_xattn_Wcv, L0_xattn_bcv, L0_xattn_Wp, L0_xattn_bp, L0_ffn_W_fc, L0_ffn_b_fc, L0_ffn_A_fc, L0_ffn_B_fc, L0_ffn_W_proj, L0_ffn_b_proj, L0_ffn_A_proj, L0_ffn_B_proj, L1_xattn_ln1_g, L1_xattn_ln1_b, L1_xattn_ln2_g, L1_xattn_ln2_b, L1_xattn_a1_wq, L1_xattn_a1_wk, L1_xattn_a1_wv, L1_xattn_a1_li1_w, L1_xattn_a1_li1_b, L1_xattn_a1_lnx_g, L1_xattn_a1_lnx_b, L1_xattn_a1_lny_g, L1_xattn_a1_lny_b, L1_xattn_a1_ln3_g, L1_xattn_a1_ln3_b, L1_xattn_a1_li2_w, L1_xattn_a1_li2_b, L1_xattn_a1_li3_w, L1_xattn_a1_li3_b, L1_xattn_a2_wq, L1_xattn_a2_wk, L1_xattn_a2_wv, L1_xattn_a2_li1_w, L1_xattn_a2_li1_b, L1_xattn_a2_lnx_g, L1_xattn_a2_lnx_b, L1_xattn_a2_lny_g, L1_xattn_a2_lny_b, L1_xattn_a2_ln3_g, L1_xattn_a2_ln3_b, L1_xattn_a2_li2_w, L1_xattn_a2_li2_b, L1_xattn_a2_li3_w, L1_xattn_a2_li3_b, L1_ffn_gate_w, L1_ffn_gate_b, L1_ffn_w1, L1_ffn_b1, L1_ffn_w2, L1_ffn_b2):
    import jax
    import jax.numpy as jnp

    def _L0_xattn_ref(x, cross_input, Wk, bk, Wq, bq, Wv, bv, Wck, bck, Wcq, bcq, Wcv, bcv, Wp, bp):
        import jax, jax.numpy as jnp
        import numpy as np
        B, T, TC, C, CC, H = (2, 256, 64, 128, 64, 16)
        D = C // H

        def _heads(t):
            b, l, _ = t.shape
            return t.reshape(b, l, H, D).transpose(0, 2, 1, 3)
        scale = np.float32(1.0 / np.sqrt(D))
        q = _heads(x @ Wq + bq)
        k = _heads(x @ Wk + bk)
        v = _heads(x @ Wv + bv)
        att = jnp.einsum('bhqd,bhkd->bhqk', q, k) * scale
        causal = jnp.tril(jnp.ones((T, T), bool))
        att = jnp.where(causal[None, None], att, -jnp.inf)
        y = jnp.einsum('bhqk,bhkd->bhqd', jax.nn.softmax(att, axis=-1), v)
        qc = _heads(x @ Wcq + bcq)
        kc = _heads(cross_input @ Wck + bck)
        vc = _heads(cross_input @ Wcv + bcv)
        attc = jnp.einsum('bhqd,bhkd->bhqk', qc, kc) * scale
        y = y + jnp.einsum('bhqk,bhkd->bhqd', jax.nn.softmax(attc, axis=-1), vc)
        y = y.transpose(0, 2, 1, 3).reshape(x.shape[0], T, C)
        return y @ Wp + bp

    def _L0_ffn_ref(hidden_states, W_fc, b_fc, A_fc, B_fc, W_proj, b_proj, A_proj, B_proj):
        import jax, jax.numpy as jnp
        import numpy as np
        BITS = 8
        LORA_RANK = 16
        LORA_ALPHA = 32
        SCALING = LORA_ALPHA / LORA_RANK

        def fake_quant_weight(w, bits=BITS):
            qmax = 2.0 ** (bits - 1) - 1
            scale = jnp.max(jnp.abs(w)) / qmax
            wq = jnp.clip(jnp.round(w / scale), -qmax - 1, qmax) * scale
            return w + jax.lax.stop_gradient(wq - w)

        def qat_lora_linear(x, W, b, A, B):
            Wq = fake_quant_weight(W)
            base = jnp.einsum('bsi,oi->bso', x, Wq) + b
            lora = jnp.einsum('bsr,or->bso', jnp.einsum('bsi,ri->bsr', x, A), B)
            return base + SCALING * lora
        h = qat_lora_linear(hidden_states, W_fc, b_fc, A_fc, B_fc)
        h = jax.nn.gelu(h, approximate=False)
        h = qat_lora_linear(h, W_proj, b_proj, A_proj, B_proj)
        return h

    def _L1_xattn_ref(xx, ee, ln1_g, ln1_b, ln2_g, ln2_b, a1_wq, a1_wk, a1_wv, a1_li1_w, a1_li1_b, a1_lnx_g, a1_lnx_b, a1_lny_g, a1_lny_b, a1_ln3_g, a1_ln3_b, a1_li2_w, a1_li2_b, a1_li3_w, a1_li3_b, a2_wq, a2_wk, a2_wv, a2_li1_w, a2_li1_b, a2_lnx_g, a2_lnx_b, a2_lny_g, a2_lny_b, a2_ln3_g, a2_ln3_b, a2_li2_w, a2_li2_b, a2_li3_w, a2_li3_b, training):
        import jax, jax.numpy as jnp
        import numpy as np
        H, D, C1, C2, S, M, B, W = (16, 32, 128, 64, 256, 64, 2, 4)

        def _ln(x, g, b):
            m = jnp.mean(x, -1, keepdims=True)
            v = jnp.var(x, -1, keepdims=True)
            return (x - m) * jax.lax.rsqrt(v + 1e-05) * g + b

        def _mha(x, y, wq, wk, wv, li1_w, li1_b, lnx_g, lnx_b, lny_g, lny_b, ln3_g, ln3_b, li2_w, li2_b, li3_w, li3_b, causal):
            xn = _ln(x, lnx_g, lnx_b)
            yn = _ln(y, lny_g, lny_b)
            q = jnp.einsum('bsc,hcd->bhsd', xn, wq)
            k = jnp.einsum('btc,hcd->bhtd', yn, wk)
            v = jnp.einsum('btc,hcd->bhtd', yn, wv)
            a = jax.nn.softmax(jnp.einsum('bhsd,bhtd->bhst', q, k) * D ** (-0.5), axis=-1)
            if causal:
                s, t = (a.shape[-2], a.shape[-1])
                mask = (jnp.arange(t)[None, :] > jnp.arange(s)[:, None]).astype(a.dtype)
                a = a * mask
            o = jnp.einsum('bhst,bhtd->bhsd', a, v)
            o = o.transpose(0, 2, 1, 3).reshape(x.shape[0], x.shape[1], H * D)
            x_out = x + o @ li1_w + li1_b
            h = jax.nn.gelu(_ln(x_out, ln3_g, ln3_b) @ li2_w + li2_b, approximate=False)
            return x_out + h @ li3_w + li3_b
        x = _ln(xx, ln1_g, ln1_b)
        x = x + _mha(x, x, a1_wq, a1_wk, a1_wv, a1_li1_w, a1_li1_b, a1_lnx_g, a1_lnx_b, a1_lny_g, a1_lny_b, a1_ln3_g, a1_ln3_b, a1_li2_w, a1_li2_b, a1_li3_w, a1_li3_b, causal=True)
        x = _ln(x, ln2_g, ln2_b)
        return x + _mha(x, ee, a2_wq, a2_wk, a2_wv, a2_li1_w, a2_li1_b, a2_lnx_g, a2_lnx_b, a2_lny_g, a2_lny_b, a2_ln3_g, a2_ln3_b, a2_li2_w, a2_li2_b, a2_li3_w, a2_li3_b, causal=False)

    def _L1_ffn_ref(x, gate_w, gate_b, w1, b1, w2, b2):
        import jax, jax.numpy as jnp
        import numpy as np
        B, S, D, H, E = (4, 256, 128, 512, 8)
        b, s, d = x.shape
        xf = x.reshape(-1, d)
        logits = xf @ gate_w.T + gate_b
        top1 = jnp.argmax(logits, axis=-1)
        out = jnp.zeros_like(xf)
        n_experts = w1.shape[0]
        for e in range(n_experts):
            h = jax.nn.relu(xf @ w1[e].T + b1[e])
            y = h @ w2[e].T + b2[e]
            out = out + jnp.where((top1 == e)[:, None], y, jnp.zeros((), y.dtype))
        return out.reshape(b, s, d)
    x = x + jnp.tanh(g_xattn[0]) * _L0_xattn_ref(_layernorm(x, axis=-1), ctx_512, L0_xattn_Wk, L0_xattn_bk, L0_xattn_Wq, L0_xattn_bq, L0_xattn_Wv, L0_xattn_bv, L0_xattn_Wck, L0_xattn_bck, L0_xattn_Wcq, L0_xattn_bcq, L0_xattn_Wcv, L0_xattn_bcv, L0_xattn_Wp, L0_xattn_bp)
    x = x + jnp.tanh(g_ffn[0]) * _L0_ffn_ref(_layernorm(x, axis=-1), L0_ffn_W_fc, L0_ffn_b_fc, L0_ffn_A_fc, L0_ffn_B_fc, L0_ffn_W_proj, L0_ffn_b_proj, L0_ffn_A_proj, L0_ffn_B_proj)
    x = x + jnp.tanh(g_xattn[1]) * _L1_xattn_ref(_layernorm(x, axis=-1), ctx_512, L1_xattn_ln1_g, L1_xattn_ln1_b, L1_xattn_ln2_g, L1_xattn_ln2_b, L1_xattn_a1_wq, L1_xattn_a1_wk, L1_xattn_a1_wv, L1_xattn_a1_li1_w, L1_xattn_a1_li1_b, L1_xattn_a1_lnx_g, L1_xattn_a1_lnx_b, L1_xattn_a1_lny_g, L1_xattn_a1_lny_b, L1_xattn_a1_ln3_g, L1_xattn_a1_ln3_b, L1_xattn_a1_li2_w, L1_xattn_a1_li2_b, L1_xattn_a1_li3_w, L1_xattn_a1_li3_b, L1_xattn_a2_wq, L1_xattn_a2_wk, L1_xattn_a2_wv, L1_xattn_a2_li1_w, L1_xattn_a2_li1_b, L1_xattn_a2_lnx_g, L1_xattn_a2_lnx_b, L1_xattn_a2_lny_g, L1_xattn_a2_lny_b, L1_xattn_a2_ln3_g, L1_xattn_a2_ln3_b, L1_xattn_a2_li2_w, L1_xattn_a2_li2_b, L1_xattn_a2_li3_w, L1_xattn_a2_li3_b, 0)
    x = x + jnp.tanh(g_ffn[1]) * _L1_ffn_ref(_layernorm(x, axis=-1), L1_ffn_gate_w, L1_ffn_gate_b, L1_ffn_w1, L1_ffn_b1, L1_ffn_w2, L1_ffn_b2)
    return x

_drawn_inputs = setup_inputs


def setup_inputs(seed=0):
    import zlib

    import numpy as np

    out = dict(_drawn_inputs(seed))
    spreads = {'g_ffn': (-1.0, 0.2),
     'L0_xattn_bk': (0.0, 0.8),
     'L0_xattn_bq': (0.0, 0.1),
     'L0_xattn_bv': (0.0, 0.1),
     'L0_xattn_bck': (0.0, 0.8),
     'L0_xattn_bcq': (0.0, 0.1),
     'L0_xattn_bcv': (0.0, 0.1),
     'L0_xattn_bp': (0.0, 0.1),
     'L0_ffn_b_fc': (0.0, 0.1),
     'L0_ffn_B_fc': (0.0, 0.1),
     'L0_ffn_b_proj': (0.0, 0.1),
     'L0_ffn_B_proj': (0.0, 0.1),
     'L1_xattn_ln1_g': (1.0, 0.2),
     'L1_xattn_ln1_b': (0.0, 0.1),
     'L1_xattn_ln2_g': (1.0, 0.2),
     'L1_xattn_ln2_b': (0.0, 0.1),
     'L1_xattn_a1_li1_b': (0.0, 0.1),
     'L1_xattn_a1_lnx_g': (1.0, 0.6),
     'L1_xattn_a1_lnx_b': (0.0, 0.8),
     'L1_xattn_a1_lny_g': (1.0, 0.6),
     'L1_xattn_a1_lny_b': (0.0, 0.385),
     'L1_xattn_a1_ln3_g': (1.0, 0.2),
     'L1_xattn_a1_ln3_b': (0.0, 0.317),
     'L1_xattn_a1_li2_b': (0.0, 0.1),
     'L1_xattn_a1_li3_b': (0.0, 0.1),
     'L1_xattn_a2_li1_b': (0.0, 0.1),
     'L1_xattn_a2_lnx_g': (1.0, 0.6),
     'L1_xattn_a2_lnx_b': (0.0, 0.8),
     'L1_xattn_a2_lny_g': (1.0, 0.2),
     'L1_xattn_a2_lny_b': (0.0, 0.318),
     'L1_xattn_a2_ln3_g': (1.0, 0.2),
     'L1_xattn_a2_ln3_b': (0.0, 0.267),
     'L1_xattn_a2_li2_b': (0.0, 0.1),
     'L1_xattn_a2_li3_b': (0.0, 0.1)}
    factors = {'L1_xattn_a1_wq': 7.946,
     'L1_xattn_a1_wk': 8.0,
     'L1_xattn_a2_wq': 7.414,
     'L1_xattn_a2_wk': 6.71,
     'L1_ffn_b1': 2.714}
    for name, (base, spread) in spreads.items():
        noise = np.random.default_rng([zlib.crc32(name.encode()), seed]).standard_normal(out[name].shape)
        drawn = base * np.exp(spread * noise) if base else spread * noise
        out[name] = jnp.asarray(drawn.astype(out[name].dtype))
    for name, factor in factors.items():
        out[name] = (out[name] * factor).astype(out[name].dtype)
    return out
```

```python
from contextlib import ExitStack

import concourse.bass as bass
from concourse import mybir

P = 128
B, S, C = 16, 256, 128
TC, CC = 64, 64
H = 16
SB = S // P
UNITS = H // 2
QUADS = H // 4
EPS = 1e-5
MASKED = -1e30
EXPERTS, HID = 8, 512
MT = 512
MB = MT // P
MSTEPS = B * S // MT
FC = HID // P
RANK, LORA_SCALE = 16, 2.0
QMAX = 127.0
ROUND = 12582912.0
SPACE = 26000

F32 = mybir.dt.float32
BF16 = mybir.dt.bfloat16
ALU = mybir.AluOpType
ACT = mybir.ActivationFunctionType
AX = mybir.AxisListType


class Count:

    def __init__(self, sem):
        self.sem, self.n = sem, 0

    def inc(self, ins, by=1):
        ins.then_inc(self.sem, by)
        self.n += by


class Step:

    def __init__(self, n, reg=None, start=0):
        self.n, self.reg, self.start = n, reg, start

    def __add__(self, k):
        return Step(self.n + k, self.reg, self.start)

    @property
    def parity(self):
        return self.n % 2

    def count(self, fn):
        if self.reg is None:
            v = fn(self.n)
            return v if v > 0 else None
        n = self.n + 2 * self.start
        first, slope = fn(n), fn(n + 2) - fn(n)
        assert slope > 0 and fn(n + 4) - fn(n + 2) == slope
        assert first > 0, "a wait below one"
        return self.reg * slope + (first - slope * self.start)

    def row(self, eng):
        return self.n if self.reg is None else eng.snap(self.reg * 2 + self.n)


class Signal:

    def __init__(self, sem, base):
        self.sem, self.base = sem, base

    def due(self, step, fn):
        v = step.count(fn)
        return None if v is None else v + self.base

    def at(self, step, fn):
        v = self.due(step, fn)
        assert v is not None
        return v


def apart(eng, k, step):
    if step.reg is not None:
        eng.sem_inc(k.through)


def pipeline(eng, steps, body):
    for n in range(4):
        body(Step(n))
    with eng.Fori(2, steps // 2 - 1) as i:
        body(Step(0, i, 2))
        body(Step(1, i, 2))
    body(Step(steps - 2))
    body(Step(steps - 1))


class Attention:

    SLOTS = {
        ("self", 1): [["T0+"], ["R0-"], ["Q0+"], ["V0+"], ["Y0-"], [], [], []],
        ("self", 4): [["T0+"], ["Q0+"], ["Q1+", "R0-"], ["Q2+", "R1-"], ["Q3+", "R2-"], ["V0+", "R3-"], ["V1+"], ["Y0-"]],
        ("cross", 1): [["T0+", "R0-"], ["Q0+", "V0+"], ["Y0-"], []],
        ("cross", 4): [["T0+", "R0-", "R1-"], ["Q0+", "Q1+", "R2-", "R3-"], ["Q2+", "Q3+", "Y0-"], ["V0+"]],
    }

    def __init__(self, k, name, kind, D, mask, src, base, dst, ctx, ctx_norm, w):
        self.name, self.kind, self.D, self.mask = name, kind, D, mask
        self.src, self.base, self.dst, self.ctx, self.ctx_norm = src, base, dst, ctx, ctx_norm
        self.w = w
        self.scale = float(D) ** -0.5
        self.G = H * D // P
        self.HG = H // self.G
        self.T = S if kind == "self" else TC
        self.KC = C if kind == "self" else CC
        self.one_side = kind == "self" and w["q_gain"] is None
        self.nv = 2 if kind == "self" and self.G == 4 else 1
        self.slots = self.SLOTS[(kind, self.G)]
        self.nslots = len(self.slots)
        self.regions = QUADS if self.G == 4 else 1
        self.k = k
        self.weights_ahead, self.loaded_ahead = [], None
        U, G = (UNITS, self.G) if kind == "self" else (4, self.G)
        turned = H if kind == "self" else 4
        each = dict(x_in=16, base_in=16, stored=16, stats=1, aggr=1, eps_in=1, rstd=1, wn=1, t_full=1, side=1, qk_full=G,
                    q_ready=G, km_ready=G, v_full=self.nv, v_ready=self.nv, s_full=U, max_ready=U, exp_done=U,
                    tr_full=turned, pt_ready=turned, pv_done=QUADS if kind == "self" else 2, num_saved=self.regions,
                    rden=1, rx=1, r_full=G, ot=G, y_full=1, res=1, biased=1)
        if mask == "after":
            each.update(masked=U)
        if kind == "cross":
            each.update(ctx_in=16)
        if ctx_norm:
            each.update(cstats=1, caggr=1, ceps=1, crstd=1, cn=1)
        self.s = k.signals(each, B)

    def pieces(self, t):
        out = []
        for u, names in enumerate(self.slots):
            for n in names:
                b = t + (1 if n[2] == "+" else -1)
                if 0 <= b < B:
                    out.append((u, n[0], int(n[1]), b))
        return out

    def in_slot(self, step, u):
        at = 5 if step.reg is not None else step.n
        return [(kind, i, step + (b - at)) for (v, kind, i, b) in self.pieces(at) if v == u]

    def before(self, step, u, kind, i):
        at = 5 if step.reg is not None else step.n
        order = [p for t in range(-1, at + 1) for p in self.pieces(t) if self.same_bank(kind, i, p[1], p[2])]
        here = [n for n, p in enumerate(order) if p[1:3] == (kind, i) and p[0] == u][-1]
        if here == 0:
            return None
        _, kind, i, b = order[here - 1]
        return kind, i, b - at

    def bank(self, kind, i):
        if self.kind == "cross" and kind in "QR":
            return self.k.scores[1][:, i % 2 * 512:(i % 2 + 1) * 512]
        return self.k.misc

    def same_bank(self, kind, i, other, j):
        pair = self.kind == "cross" and kind in "QR", self.kind == "cross" and other in "QR"
        return pair == (True, True) and i % 2 == j % 2 or pair == (False, False)

    def emptied(self, kind, i):
        return {
            "T": [("side", 1, 1)],
            "Q": [("q_ready", self.G, i + 1), ("km_ready", self.G, i + 1)],
            "V": [("v_ready", self.nv, i + 1)],
            "R": [("ot", self.G, i + 1)],
            "Y": [("res", 1, 1)],
        }[kind]

    def head(self, n):
        return 4 * (n % 4) + n // 4 if self.G == 1 else n



def sync_attention(sp, a):
    k, s = a.k, a.s

    def load_x(b):
        row = b.row(sp)
        if (due := s["x_in"].due(b, lambda t: 16 * t)) is not None:
            sp.wait_ge(s["x_in"].sem, due)
            apart(sp, k, b)
        if (due := s["wn"].due(b, lambda t: t - 1)) is not None:
            sp.wait_ge(s["wn"].sem, due)
            apart(sp, k, b)
        sp.dma_start(k.x_in[:, b.parity], a.src[row].rearrange("(k p) c -> p k c", p=P)).then_inc(s["x_in"].sem, 16)
        if a.ctx is not None:
            if (due := s["ctx_in"].due(b, lambda t: 16 * t)) is not None:
                sp.wait_ge(s["ctx_in"].sem, due)
                apart(sp, k, b)
            if a.ctx_norm:
                if (due := s["cn"].due(b, lambda t: t - 1)) is not None:
                    sp.wait_ge(s["cn"].sem, due)
                    apart(sp, k, b)
            else:
                if (due := s["t_full"].due(b, lambda t: t - 1)) is not None:
                    sp.wait_ge(s["t_full"].sem, due)
                    apart(sp, k, b)
            sp.dma_start(k.ctx_in[:, b.parity], a.ctx[row]).then_inc(s["ctx_in"].sem, 16)

    def load_base(b):
        row = b.row(sp)
        if (due := s["base_in"].due(b, lambda t: 16 * t)) is not None:
            sp.wait_ge(s["base_in"].sem, due)
            apart(sp, k, b)
        if (due := s["res"].due(b, lambda t: t - 1)) is not None:
            sp.wait_ge(s["res"].sem, due)
            apart(sp, k, b)
        sp.dma_start(k.base_in[:, b.parity], a.base[row].rearrange("(k p) c -> p k c", p=P)).then_inc(s["base_in"].sem, 16)

    def store(b):
        row = b.row(sp)
        if (due := s["stored"].due(b, lambda t: 16 * t)) is not None:
            sp.wait_ge(s["stored"].sem, due)
            apart(sp, k, b)
        sp.wait_ge(s["res"].sem, s["res"].at(b, lambda t: t + 1))
        apart(sp, k, b)
        sp.dma_start(a.dst[row].rearrange("(k p) c -> p k c", p=P), k.res[:, b.parity]).then_inc(s["stored"].sem, 16)

    load_x(Step(0))
    load_x(Step(1))

    def body(t):
        if t.n < B - 2 or t.reg is not None:
            load_x(t + 2)
        load_base(t)
        if t.reg is None and t.n < 4:
            for dst, src in a.weights_ahead[t.n::4]:
                sp.dma_start(dst, src).then_inc(a.loaded_ahead, 16)
        if t.n > 0 or t.reg is not None:
            store(t + -1)

    pipeline(sp, B, body)
    store(Step(B - 1))
    sp.wait_ge(s["stored"].sem, s["stored"].base + 16 * B)



def tensor_attention(pe, a):
    k, s, w = a.k, a.s, a.w

    def piece(t, u, kind, i, b):
        bank = a.bank(kind, i)
        was = a.before(t, u, kind, i)
        if was is not None:
            for name, per, n in a.emptied(*was[:2]):
                if (due := s[name].due(t, lambda x: (x + was[2]) * per + n)) is not None:
                    pe.wait_ge(s[name].sem, due)
        if kind == "T":
            if a.ctx_norm:
                pe.wait_ge(s["cn"].sem, s["cn"].at(b, lambda x: x + 1))
            elif a.kind == "cross":
                pe.wait_ge(s["ctx_in"].sem, s["ctx_in"].at(b, lambda x: 16 * (x + 1)))
            pe.wait_ge(s["wn"].sem, s["wn"].at(b, lambda x: x + 1))
            for blk in range(SB):
                last = pe.transpose(bank[:, blk * P:(blk + 1) * P], k.wn[:, b.parity, blk], k.ident[:, :])
            if a.kind == "cross":
                src = k.cn if a.ctx_norm else k.ctx_in
                last = pe.transpose(bank[0:CC, 256:256 + TC], src[:, b.parity], k.ident[0:TC, 0:TC])
            last.then_inc(s["t_full"].sem, 1)
        if kind == "Q":
            pe.wait_ge(s["side"].sem, s["side"].at(b, lambda x: x + 1))
            pe.matmul(bank[:, 0:S], w["wq"][:, i * P:(i + 1) * P], k.xq[:, b.parity], start=True, stop=True)
            keys = k.xq[:, b.parity] if a.one_side else k.xk[:, b.parity] if a.kind == "self" else k.xc[:, b.parity, 0]
            pe.matmul(bank[:, S:S + a.T], w["wk"][:, i * P:(i + 1) * P], keys, start=True, stop=True)\
              .then_inc(s["qk_full"].sem, 1)
        if kind == "V":
            pe.wait_ge(s["side"].sem, s["side"].at(b, lambda x: x + 1))
            keys = k.xq if a.one_side else k.xk
            if a.kind == "cross":
                last = pe.matmul(bank[:, 0:a.G * P], k.xc[:, b.parity].rearrange("c h t -> c (h t)"), w["wv"][:, :],
                                 start=True, stop=True)
            elif a.G == 4:
                last = pe.matmul(bank[:, :], keys[:, b.parity, i * P:(i + 1) * P], w["wv"][:, :], start=True, stop=True)
            else:
                for blk in range(SB):
                    last = pe.matmul(bank[:, blk * P:(blk + 1) * P], keys[:, b.parity, blk * P:(blk + 1) * P],
                                     w["wv"][:, :], start=True, stop=True)
            last.then_inc(s["v_full"].sem, 1)
        if kind == "R":
            pe.wait_ge(s["rx"].sem, s["rx"].at(b, lambda x: x + 1))
            for blk in range(SB):
                last = pe.transpose(bank[:, blk * P:(blk + 1) * P], k.rx[:, blk, i * P:(i + 1) * P], k.ident[:, :])
            last.then_inc(s["r_full"].sem, 1)
        if kind == "Y":
            pe.wait_ge(s["ot"].sem, s["ot"].at(b, lambda x: a.G * (x + 1)))
            for blk in range(SB):
                for g in range(a.G):
                    last = pe.matmul(bank[:, blk * P:(blk + 1) * P], k.ot[:, g, blk * P:(blk + 1) * P],
                                     w["wo"][:, g], start=(g == 0), stop=(g == a.G - 1))
            last.then_inc(s["y_full"].sem, 1)

    def pieces(t, u):
        for kind, i, b in a.in_slot(t, u):
            piece(t, u, kind, i, b)

    def self_scores(b, u):
        U = lambda x: UNITS * x + u
        if (due := s["exp_done"].due(b, lambda x: U(x) - 1)) is not None:
            pe.wait_ge(s["exp_done"].sem, due)
        g0 = a.head(2 * u) // a.HG
        pe.wait_ge(s["q_ready"].sem, s["q_ready"].at(b, lambda x: a.G * x + g0 + 1))
        pe.wait_ge(s["km_ready"].sem, s["km_ready"].at(b, lambda x: a.G * x + g0 + 1))
        for n in range(2):
            h = a.head(2 * u + n)
            bank = k.scores[u % 2][:, n * 512:(n + 1) * 512]
            for blk in range(SB):
                q = k.qT[:, b.parity, h // a.HG, blk * P:(blk + 1) * P]
                if a.mask == "before":
                    cols = (0, P) if blk == 0 else (P, 3 * P)
                    pe.matmul(bank[:, cols[0]:cols[1]], q, k.km[:, b.parity, h, 0:cols[1] - cols[0]],
                              start=True, stop=False, skip_group_check=True)
                    last = pe.matmul(bank[:, cols[1] - P:cols[1]], k.identb[:, :], k.above[:, :],
                                     start=False, stop=True, skip_group_check=True)
                else:
                    last = pe.matmul(bank[:, blk * S:(blk + 1) * S], q, k.km[:, b.parity, h], start=True, stop=True)
        last.then_inc(s["s_full"].sem, 1)

    def self_turn(b, u):
        pe.wait_ge(s["masked" if a.mask == "after" else "exp_done"].sem, s["masked" if a.mask == "after" else "exp_done"].at(b, lambda x: UNITS * x + u + 1))
        for n in range(2):
            hd = 2 * u + n
            if (due := s["pt_ready"].due(b, lambda x: H * x + hd - 1)) is not None:
                pe.wait_ge(s["pt_ready"].sem, due)
            blocks = (0, 1, 3) if a.mask == "after" else (0, 1, 2)
            for o, blk in enumerate(blocks):
                last = pe.transpose(k.turned[hd % 2][:, o * P:(o + 1) * P], k.probs[:, u % 2, n, blk * P:(blk + 1) * P],
                                    k.ident[:, :])
            last.then_inc(s["tr_full"].sem, 1)

    def self_values(b, q):
        pe.wait_ge(s["pt_ready"].sem, s["pt_ready"].at(b, lambda x: H * x + 4 * q + 4))
        pe.wait_ge(s["v_ready"].sem, s["v_ready"].at(b, lambda x: a.nv * (x + 1)))
        r = a.regions
        reg = q if r > 1 else 0
        if (due := s["num_saved"].due(b, lambda x: r * x + reg)) is not None:
            pe.wait_ge(s["num_saved"].sem, due)
        half = (q % 2 if r > 1 else b.parity) * S
        pt = lambda n, lo, hi: k.pt[:, 4 * (q % 2) + n, lo * P:hi * P]
        first = r > 1 or q == 0
        for part in range(2):
            for n in range(4):
                h = a.head(4 * q + n)
                out = k.num[32 * n:32 * n + 32]
                tb = part if a.mask == "before" else 1 - part
                v = k.val[:, b.parity, tb, 32 * h:32 * h + 32]
                if a.mask == "before":
                    out, p = (out[:, half:half + S], pt(n, 0, 2)) if part == 0 else (out[:, half + P:half + S], pt(n, 2, 3))
                else:
                    out, p = (out[:, half:half + S], pt(n, 1, 3)) if part == 0 else (out[:, half:half + P], pt(n, 0, 1))
                last = pe.matmul(out, v, p, start=(first and part == 0), stop=(part == 1), skip_group_check=True)
        last.then_inc(s["pv_done"].sem, 1)

    def cross_scores(b, c):
        if (due := s["exp_done"].due(b, lambda x: 4 * x + c - 1)) is not None:
            pe.wait_ge(s["exp_done"].sem, due)
        half, blk = c // 2, c % 2
        g1 = min(a.G - 1, 2 * half + 1)
        pe.wait_ge(s["q_ready"].sem, s["q_ready"].at(b, lambda x: a.G * x + g1 + 1))
        pe.wait_ge(s["km_ready"].sem, s["km_ready"].at(b, lambda x: a.G * x + g1 + 1))
        bank = k.scores[0][:, (c % 2) * 512:(c % 2 + 1) * 512]
        for i in range(2 if a.G == 4 else 1):
            g = 2 * half + i if a.G == 4 else 0
            hs = 4 if a.G == 4 else 8
            h0 = 8 * half + hs * i
            last = pe.matmul(bank[:, i * hs * TC:(i + 1) * hs * TC], k.qT[:, b.parity, g, blk * P:(blk + 1) * P],
                             k.km_cross[:, b.parity, h0 * TC:(h0 + hs) * TC], start=True, stop=True)
        last.then_inc(s["s_full"].sem, 1)

    def cross_turn(b, c):
        pe.wait_ge(s["exp_done"].sem, s["exp_done"].at(b, lambda x: 4 * x + c + 1))
        if (due := s["pt_ready"].due(b, lambda x: 4 * x + c - 1)) is not None:
            pe.wait_ge(s["pt_ready"].sem, due)
        for p in range(4):
            last = pe.transpose(k.turned[c % 2][:, p * P:(p + 1) * P], k.pc[:, c % 2, p * P:(p + 1) * P], k.ident[:, :])
        last.then_inc(s["tr_full"].sem, 1)

    def cross_values(b, half):
        pe.wait_ge(s["pt_ready"].sem, s["pt_ready"].at(b, lambda x: 4 * x + 2 * half + 2))
        pe.wait_ge(s["v_ready"].sem, s["v_ready"].at(b, lambda x: x + 1))
        if a.G == 4:
            if (due := s["num_saved"].due(b, lambda x: 4 * x + 2 * half)) is not None:
                pe.wait_ge(s["num_saved"].sem, due)
            for g in range(2):
                for p in range(2):
                    pair = 4 * half + 2 * g + p
                    last = pe.matmul(k.num[:, g * S:(g + 1) * S], k.vb[:, b.parity, pair], k.ptc[:, half, 2 * g + p],
                                     start=(p == 0), stop=(p == 1), skip_group_check=True)
        else:
            if (due := s["num_saved"].due(b, lambda x: x)) is not None:
                pe.wait_ge(s["num_saved"].sem, due)
            for p in range(4):
                last = pe.matmul(k.num[:, b.parity * S:(b.parity + 1) * S], k.vb[:, b.parity, 4 * half + p],
                                 k.ptc[:, half, p], start=(half == 0 and p == 0), stop=(half == 1 and p == 3),
                                 skip_group_check=True)
        last.then_inc(s["pv_done"].sem, 1)

    for _, kind, i, b in a.pieces(-1):
        piece(Step(-1), _, kind, i, Step(b))
    scores, turn, values = ((self_scores, self_turn, self_values) if a.kind == "self" else
                            (cross_scores, cross_turn, cross_values))
    n = a.nslots
    for u in range(2):
        scores(Step(0), u)

    def body(t):
        last = t.reg is None and t.n == B - 1
        first = t.reg is None and t.n == 0
        for u in range(n):
            turn(t, u)
            if u + 2 < n:
                scores(t, u + 2)
            elif not last:
                scores(t + 1, u + 2 - n)
            if u % 2 == 0 and not (first and u == 0):
                values(t + (-1 if u == 0 else 0), (u // 2 - 1) % (n // 2))
            pieces(t, u)

    pipeline(pe, B, body)
    values(Step(B - 1), n // 2 - 1)
    for u in range(n):
        pieces(Step(B), u)



def scalar_attention(act, a):
    k, s, w = a.k, a.s, a.w

    def piece(kind, i, b):
        bank = a.bank(kind, i)
        if kind == "Q":
            act.wait_ge(s["qk_full"].sem, s["qk_full"].at(b, lambda x: a.G * x + i + 1))
            last_use = (lambda x: UNITS * (x - 1)) if a.kind == "self" else (lambda x: 4 * (x - 1))
            if (due := s["s_full"].due(b, last_use)) is not None:
                act.wait_ge(s["s_full"].sem, due)
            act.wait_ge(s["km_ready"].sem, s["km_ready"].at(b, lambda x: a.G * x + i + 1))
            act.activation(k.qT[:, b.parity, i], bank[:, 0:S], ACT.Identity, bias=w["q_bias"] if w["q_bias"] is not None else 0.0,
                           scale=a.scale).then_inc(s["q_ready"].sem, 1)
        if kind == "V" and a.kind == "self" and a.G == 4:
            act.wait_ge(s["v_full"].sem, s["v_full"].at(b, lambda x: 2 * x + i + 1))
            if (due := s["pv_done"].due(b, lambda x: QUADS * (x - 1))) is not None:
                act.wait_ge(s["pv_done"].sem, due)
            act.copy(k.val[:, b.parity, i], bank[:, :]).then_inc(s["v_ready"].sem, 1)

    def self_exp(b, u):
        act.wait_ge(s["max_ready"].sem, s["max_ready"].at(b, lambda x: UNITS * x + u + 1))
        if (due := s["tr_full"].due(b, lambda x: H * x + 2 * (u - 1))) is not None:
            act.wait_ge(s["tr_full"].sem, due)
        if (due := s["rden"].due(b, lambda x: x - 1)) is not None:
            act.wait_ge(s["rden"].sem, due)
        for n in range(2):
            h = a.head(2 * u + n)
            for blk in range(SB):
                if a.mask == "before":
                    lo, hi = (0, P) if blk == 0 else (P, 3 * P)
                else:
                    lo, hi = blk * S, (blk + 1) * S
                last = act.activation(k.probs[:, u % 2, n, lo:hi], k.scores[u % 2][:, n * 512 + lo:n * 512 + hi], ACT.Exp,
                                      bias=k.nmax[:, u % 2, 2 * n + blk:2 * n + blk + 1], scale=1.0,
                                      accum_out=k.sums[:, b.parity, blk, h:h + 1])
        last.then_inc(s["exp_done"].sem, 1)

    def cross_exp(b, c):
        act.wait_ge(s["max_ready"].sem, s["max_ready"].at(b, lambda x: 4 * x + c + 1))
        if (due := s["tr_full"].due(b, lambda x: 4 * x + c - 1)) is not None:
            act.wait_ge(s["tr_full"].sem, due)
        if (due := s["rden"].due(b, lambda x: x - 1)) is not None:
            act.wait_ge(s["rden"].sem, due)
        for h in range(8):
            at = c % 2 * 512 + h * TC
            last = act.activation(k.pc[:, c % 2, h * TC:(h + 1) * TC], k.scores[0][:, at:at + TC], ACT.Exp,
                                  bias=k.cmax[:, c % 2, h:h + 1], scale=1.0,
                                  accum_out=k.sums[:, b.parity, c % 2, 8 * (c // 2) + h:8 * (c // 2) + h + 1])
        last.then_inc(s["exp_done"].sem, 1)

    def save(b, q):
        if a.regions > 1:
            n, per = (1, 4) if a.kind == "self" else (2, 2)
            act.wait_ge(s["pv_done"].sem, s["pv_done"].at(b, lambda x: per * x + q + 1))
            if (due := s["ot"].due(b, lambda x: 4 * (x - 1))) is not None:
                act.wait_ge(s["ot"].sem, due)
            half = (q % 2) * S if a.kind == "self" else 0
            act.copy(k.numS[:, b.parity, n * q:n * (q + 1)], k.num[:, half:half + n * S].rearrange("p (g t) -> p g t", g=n))\
               .then_inc(s["num_saved"].sem, n)
        elif q == (3 if a.kind == "self" else 1):
            act.wait_ge(s["pv_done"].sem, s["pv_done"].at(b, lambda x: (q + 1) * (x + 1)))
            if (due := s["ot"].due(b, lambda x: x - 1)) is not None:
                act.wait_ge(s["ot"].sem, due)
            act.copy(k.numS[:, b.parity, 0], k.num[:, b.parity * S:(b.parity + 1) * S]).then_inc(s["num_saved"].sem, 1)

    exps = self_exp if a.kind == "self" else cross_exp
    n = a.nslots
    for _, kind, i, b in a.pieces(-1):
        piece(kind, i, Step(b))
    for u in range(2):
        exps(Step(0), u)

    def body(t):
        last = t.reg is None and t.n == B - 1
        first = t.reg is None and t.n == 0
        for u in range(n):
            if u + 2 < n:
                exps(t, u + 2)
            elif not last:
                exps(t + 1, u + 2 - n)
            if u % 2 == 0 and not (first and u == 0):
                save(t + (-1 if u == 0 else 0), (u // 2 - 1) % (n // 2))
            for kind, i, b in a.in_slot(t, u):
                piece(kind, i, b)

    pipeline(act, B, body)
    save(Step(B - 1), n // 2 - 1)
    for u in range(n):
        for kind, i, b in a.in_slot(Step(B), u):
            piece(kind, i, b)



def vector_norm_stats(dve, k, s, x, stats, aggr, names, b, blocks):
    for blk in range(blocks):
        last = dve.bn_stats(stats[:, blk], x[:, blk])
    last.then_inc(s[names[0]].sem, 1)
    dve.wait_ge(s[names[0]].sem, s[names[0]].at(b, lambda t: t + 1))
    apart(dve, k, b)
    for blk in range(blocks):
        last = dve.bn_aggr(aggr[:, blk], stats[:, blk])
    last.then_inc(s[names[1]].sem, 1)


def vector_attention(dve, a):
    k, s, w = a.k, a.s, a.w

    def norm_stats(b):
        dve.wait_ge(s["x_in"].sem, s["x_in"].at(b, lambda t: 16 * (t + 1)))
        vector_norm_stats(dve, k, s, k.x_in[:, b.parity], k.stats[:, b.parity], k.aggr[:, b.parity], ("stats", "aggr"), b, SB)
        if a.ctx_norm:
            dve.wait_ge(s["ctx_in"].sem, s["ctx_in"].at(b, lambda t: 16 * (t + 1)))
            vector_norm_stats(dve, k, s, k.ctx_in[:, b.parity].unsqueeze(1), k.cstats[:, b.parity], k.caggr[:, b.parity],
                              ("cstats", "caggr"), b, 1)

    def norm(b):
        dve.wait_ge(s["rstd"].sem, s["rstd"].at(b, lambda t: t + 1))
        if (due := s["t_full"].due(b, lambda t: t - 1)) is not None:
            dve.wait_ge(s["t_full"].sem, due)
        for blk in range(SB):
            last = dve.tensor_scalar(k.wn[:, b.parity, blk], k.x_in[:, b.parity, blk], k.aggr[:, b.parity, blk, 0:1],
                                     k.rstd[:, b.parity, blk:blk + 1], ALU.subtract, ALU.mult)
        last.then_inc(s["wn"].sem, 1)
        if a.ctx_norm:
            dve.wait_ge(s["crstd"].sem, s["crstd"].at(b, lambda t: t + 1))
            dve.tensor_scalar(k.cn[:, b.parity], k.ctx_in[:, b.parity], k.caggr[:, b.parity, 0, 0:1],
                              k.crstd[:, b.parity, 0:1], ALU.subtract, ALU.mult).then_inc(s["cn"].sem, 1)

    def piece(kind, i, b):
        bank = a.bank(kind, i)
        if kind == "T":
            dve.wait_ge(s["t_full"].sem, s["t_full"].at(b, lambda x: x + 1))
            if (due := s["qk_full"].due(b, lambda x: a.G * (x - 1))) is not None:
                dve.wait_ge(s["qk_full"].sem, due)
            if (due := s["v_full"].due(b, lambda x: a.nv * (x - 1))) is not None:
                dve.wait_ge(s["v_full"].sem, due)
            if w["q_gain"] is None:
                last = dve.tensor_copy(k.xq[:, b.parity], bank[:, 0:S])
            else:
                last = dve.tensor_scalar(k.xq[:, b.parity], bank[:, 0:S], w["q_gain"], w["q_shift"], ALU.mult, ALU.add)
            if a.kind == "self" and not a.one_side:
                last = dve.tensor_scalar(k.xk[:, b.parity], bank[:, 0:S], w["k_gain"], w["k_shift"], ALU.mult, ALU.add)
            if a.kind == "cross":
                both = bank[0:CC, S:S + TC].unsqueeze(1).to_broadcast([CC, 2, TC])
                if w["k_gain"] is None:
                    last = dve.tensor_copy(k.xc[:, b.parity], both)
                else:
                    last = dve.tensor_scalar(k.xc[:, b.parity], both, w["k_gain"], w["k_shift"], ALU.mult, ALU.add)
            last.then_inc(s["side"].sem, 1)
        if kind == "Q":
            dve.wait_ge(s["qk_full"].sem, s["qk_full"].at(b, lambda x: a.G * x + i + 1))
            last_use = (lambda x: UNITS * (x - 1)) if a.kind == "self" else (lambda x: 4 * (x - 1))
            if (due := s["s_full"].due(b, last_use)) is not None:
                dve.wait_ge(s["s_full"].sem, due)
            n = min(a.HG, 1024 // a.T)
            for j in range(0, a.HG, n):
                h0 = a.HG * i + j
                out = (k.km[:, b.parity, h0:h0 + n] if a.kind == "self" else
                       k.km_cross[:, b.parity, h0 * TC:(h0 + n) * TC].rearrange("p (h t) -> p h t", t=TC))
                keys = bank[:, S:S + a.T].unsqueeze(1).to_broadcast([P, n, a.T])
                own = w["own"][:, j:j + n].unsqueeze(2).to_broadcast([P, n, a.T])
                if w["k_bias"] is None:
                    last = dve.tensor_tensor(out, keys, own, ALU.mult)
                else:
                    last = dve.scalar_tensor_tensor(out=out, in0=keys, scalar=w["k_bias"], in1=own, op0=ALU.add, op1=ALU.mult)
            last.then_inc(s["km_ready"].sem, 1)
        if kind == "V" and a.kind == "self" and a.G == 1:
            dve.wait_ge(s["v_full"].sem, s["v_full"].at(b, lambda x: x + 1))
            if (due := s["pv_done"].due(b, lambda x: QUADS * (x - 1))) is not None:
                dve.wait_ge(s["pv_done"].sem, due)
            for blk in range(SB):
                last = dve.tensor_tensor(
                    k.val[:, b.parity, blk].rearrange("p (r j c) -> p r j c", r=4, c=32),
                    bank[:, blk * P:(blk + 1) * P].rearrange("p (r c) -> p r c", r=4).unsqueeze(2).to_broadcast([P, 4, 4, 32]),
                    k.own_columns[:, :, :].unsqueeze(1).to_broadcast([P, 4, 4, 32]), ALU.mult)
            last.then_inc(s["v_ready"].sem, 1)
        if kind == "V" and a.kind == "cross":
            dve.wait_ge(s["v_full"].sem, s["v_full"].at(b, lambda x: x + 1))
            if (due := s["pv_done"].due(b, lambda x: 2 * (x - 1))) is not None:
                dve.wait_ge(s["pv_done"].sem, due)
            if a.G == 1:
                last = dve.tensor_tensor(k.vb[:, b.parity], bank[:, 0:P].unsqueeze(1).to_broadcast([P, 8, P]),
                                         w["own_pair"], ALU.mult)
            else:
                last = dve.tensor_tensor(k.vb[:, b.parity].rearrange("p (g j) c -> p g j c", g=4),
                                         bank[:, :].rearrange("p (g c) -> p g c", g=4).unsqueeze(2).to_broadcast([P, 4, 2, P]),
                                         w["own_pair"].rearrange("p (g j) c -> p g j c", g=4), ALU.mult)
            last.then_inc(s["v_ready"].sem, 1)
        if kind == "R":
            dve.wait_ge(s["r_full"].sem, s["r_full"].at(b, lambda x: a.G * x + i + 1))
            if (due := s["num_saved"].due(b, lambda x: a.regions * x + min(i, a.regions - 1) + 1)) is not None:
                dve.wait_ge(s["num_saved"].sem, due)
            if (due := s["y_full"].due(b, lambda x: x)) is not None:
                dve.wait_ge(s["y_full"].sem, due)
            dve.tensor_tensor(k.ot[:, i], bank[:, 0:S], k.numS[:, b.parity, i], ALU.mult).then_inc(s["ot"].sem, 1)
        if kind == "Y":
            dve.wait_ge(s["y_full"].sem, s["y_full"].at(b, lambda x: x + 1))
            dve.wait_ge(s["biased"].sem, s["biased"].at(b, lambda x: x + 1))
            if (due := s["stored"].due(b, lambda x: 16 * (x - 1))) is not None:
                dve.wait_ge(s["stored"].sem, due)
            dve.tensor_tensor(k.res[:, b.parity].rearrange("p k c -> p (k c)"), bank[:, 0:S],
                              k.base_sum[:, b.parity].rearrange("p k c -> p (k c)"), ALU.add).then_inc(s["res"].sem, 1)

    def self_max(b, u):
        dve.wait_ge(s["s_full"].sem, s["s_full"].at(b, lambda x: UNITS * x + u + 1))
        if (due := s["exp_done"].due(b, lambda x: UNITS * x + u - 1)) is not None:
            dve.wait_ge(s["exp_done"].sem, due)
        bank = k.scores[u % 2][:, :].rearrange("p (n t) -> p n t", n=2)
        out = k.nmax[:, u % 2].rearrange("p (n k) -> p n k", n=2)
        if a.mask == "before":
            dve.tensor_reduce(out[:, :, 0:1], bank[:, :, 0:P], AX.X, ALU.max, negate=True)
            last = dve.tensor_reduce(out[:, :, 1:2], bank[:, :, P:3 * P], AX.X, ALU.max, negate=True)
        else:
            last = dve.tensor_reduce(k.nmax[:, u % 2], k.scores[u % 2][:, :].rearrange("p (n t) -> p n t", n=4),
                                     AX.X, ALU.max, negate=True)
        last.then_inc(s["max_ready"].sem, 1)

    def self_copy(b, u):
        for n in range(2):
            hd = 2 * u + n
            dve.wait_ge(s["tr_full"].sem, s["tr_full"].at(b, lambda x: H * x + hd + 1))
            if (due := s["pv_done"].due(b, lambda x: QUADS * x + hd // 4 - 1)) is not None:
                dve.wait_ge(s["pv_done"].sem, due)
            dve.tensor_copy(k.pt[:, hd % 8], k.turned[hd % 2][:, 0:3 * P]).then_inc(s["pt_ready"].sem, 1)

    def cross_max(b, c):
        dve.wait_ge(s["s_full"].sem, s["s_full"].at(b, lambda x: 4 * x + c + 1))
        if (due := s["exp_done"].due(b, lambda x: 4 * x + c - 1)) is not None:
            dve.wait_ge(s["exp_done"].sem, due)
        scores = k.scores[0][:, (c % 2) * 512:(c % 2 + 1) * 512].rearrange("p (h t) -> p h t", t=TC)
        dve.tensor_reduce(k.cmax[:, c % 2], scores, AX.X, ALU.max, negate=True).then_inc(s["max_ready"].sem, 1)

    def cross_copy(b, c):
        dve.wait_ge(s["tr_full"].sem, s["tr_full"].at(b, lambda x: 4 * x + c + 1))
        if (due := s["pv_done"].due(b, lambda x: 2 * (x - 1) + c // 2 + 1)) is not None:
            dve.wait_ge(s["pv_done"].sem, due)
        dve.tensor_copy(k.ptc[:, c // 2, :, (c % 2) * P:(c % 2 + 1) * P],
                        k.turned[c % 2][:, :].rearrange("p (j t) -> p j t", j=4)).then_inc(s["pt_ready"].sem, 1)

    def reciprocals(b):
        dve.wait_ge(s["exp_done"].sem, s["exp_done"].at(b, lambda x: a.nslots * (x + 1)))
        dve.reciprocal(k.rsum[:, b.parity], k.sums[:, b.parity]).then_inc(s["rden"].sem, 1)
        dve.wait_ge(s["rden"].sem, s["rden"].at(b, lambda x: x + 1))
        if (due := s["r_full"].due(b, lambda x: a.G * x)) is not None:
            dve.wait_ge(s["r_full"].sem, due)
        for blk in range(SB):
            last = dve.tensor_copy(k.rx[:, blk, 0:H * a.D].rearrange("p (h d) -> p h d", d=a.D),
                                   k.rsum[:, b.parity, blk].unsqueeze(2).to_broadcast([P, H, a.D]))
        last.then_inc(s["rx"].sem, 1)

    exists = lambda t, ahead: t.reg is not None or t.n + ahead < B
    for b in range(2):
        norm_stats(Step(b))
        norm(Step(b))
    for _, kind, i, b in a.pieces(-1):
        piece(kind, i, Step(b))
    top = self_max if a.kind == "self" else cross_max
    for u in range(2):
        top(Step(0), u)

    def body(t):
        n = a.nslots
        for u in range(n):
            if a.kind == "self":
                self_copy(t, u)
            else:
                cross_copy(t, u)
            if u + 2 < n or exists(t, 1):
                b, v = (t, u + 2) if u + 2 < n else (t + 1, u + 2 - n)
                top(b, v)
            for kind, i, b in a.in_slot(t, u):
                piece(kind, i, b)
            if u == n - 2 and exists(t, 2):
                norm_stats(t + 2)
            if u == n - 1:
                reciprocals(t)
                if exists(t, 2):
                    norm(t + 2)

    pipeline(dve, B, body)
    for u in range(a.nslots):
        for kind, i, b in a.in_slot(Step(B), u):
            piece(kind, i, b)



def gpsimd_attention(pool, a):
    k, s, w = a.k, a.s, a.w

    def rstd(b):
        pool.wait_ge(s["aggr"].sem, s["aggr"].at(b, lambda t: t + 1))
        if (due := s["wn"].due(b, lambda t: t - 1)) is not None:
            pool.wait_ge(s["wn"].sem, due)
        pool.tensor_tensor(k.vareps[:, b.parity], k.aggr[:, b.parity, :, 1], k.eps[0:k.vareps.shape[0], 0:k.vareps.shape[2]], ALU.add).then_inc(s["eps_in"].sem, 1)
        pool.wait_ge(s["eps_in"].sem, s["eps_in"].at(b, lambda t: t + 1))
        pool.tensor_tensor(k.rstd[:, b.parity], k.vareps[:, b.parity], k.minus_half[:, 0:SB], ALU.pow).then_inc(s["rstd"].sem, 1)
        if a.ctx_norm:
            pool.wait_ge(s["caggr"].sem, s["caggr"].at(b, lambda t: t + 1))
            if (due := s["cn"].due(b, lambda t: t - 1)) is not None:
                pool.wait_ge(s["cn"].sem, due)
            pool.tensor_tensor(k.cvareps[:, b.parity], k.caggr[:, b.parity, :, 1], k.eps[0:k.cvareps.shape[0], 0:k.cvareps.shape[2]], ALU.add).then_inc(s["ceps"].sem, 1)
            pool.wait_ge(s["ceps"].sem, s["ceps"].at(b, lambda t: t + 1))
            pool.tensor_tensor(k.crstd[:, b.parity], k.cvareps[:, b.parity], k.minus_half[0:TC, 0:1], ALU.pow)\
                .then_inc(s["crstd"].sem, 1)

    def bias(b):
        pool.wait_ge(s["base_in"].sem, s["base_in"].at(b, lambda t: 16 * (t + 1)))
        if (due := s["res"].due(b, lambda t: t - 1)) is not None:
            pool.wait_ge(s["res"].sem, due)
        pool.tensor_tensor(k.base_sum[:, b.parity], k.base_in[:, b.parity],
                           w["o_bias"].unsqueeze(1).to_broadcast([P, SB, C]), ALU.add).then_inc(s["biased"].sem, 1)

    def mask(b, u):
        pool.wait_ge(s["exp_done"].sem, s["exp_done"].at(b, lambda x: UNITS * x + u + 1))
        apart(pool, k, b)
        for n in range(2):
            blocks = k.probs[:, u % 2, n].rearrange("p (q t) -> p q t", t=P)[:, 0:4:3]
            last = pool.affine_select(out=blocks, in_=blocks, compare_op=ALU.is_ge, fill=0.0, base=-1,
                                      pattern=[[0, 2], [1, P]], channel_multiplier=-1)
        last.then_inc(s["masked"].sem, 1)

    exists = lambda t, ahead: t.reg is not None or t.n + ahead < B
    rstd(Step(0))
    rstd(Step(1))
    if a.mask == "after":
        for u in range(2):
            mask(Step(0), u)

    def body(t):
        n = a.nslots
        bias(t)
        for u in range(n):
            if a.mask == "after" and (u + 2 < n or exists(t, 1)):
                mask(t if u + 2 < n else t + 1, u + 2 if u + 2 < n else u + 2 - n)
            if u == n - 2 and exists(t, 2):
                rstd(t + 2)

    pipeline(pool, B, body)



class Mlp:

    def __init__(self, k, name, src, also, after, dst, keep, start, w):
        self.k, self.name, self.src, self.also, self.after = k, name, src, also, after
        self.dst, self.keep, self.start, self.w = dst, keep, start, w
        each = dict(x_in=16, stored=16, stats=1, aggr=1, eps_in=1, rstd=1, wn=1, t_full=1, xt=1, h_full=FC, gelu=FC,
                    y_full=1, biased=1, r=1, out=1)
        if after == "norm":
            each.update(rstats=1, raggr=1, reps=1, rrstd=1, rn=1, gained=1)
        if keep is not None:
            each.update(kept=16)
        if also is not None:
            each.update(both=1, also_in=16)
        if start is not None:
            each.update(start_in=16)
        self.s = k.signals(each, MSTEPS)


def mlp_rows(x, row):
    return x.rearrange("(m n) s c -> m (n s) c", n=MT // S)[row].rearrange("(k p) c -> p k c", p=P)


def sync_mlp(sp, m):
    k, s = m.k, m.s

    def load(t):
        row = t.row(sp)
        if (due := s["x_in"].due(t, lambda x: 16 * x)) is not None:
            sp.wait_ge(s["x_in"].sem, due)
            apart(sp, k, t)
        if (due := s["biased"].due(t, lambda x: x - 1)) is not None:
            sp.wait_ge(s["biased"].sem, due)
            apart(sp, k, t)
        if (due := s["wn"].due(t, lambda x: x - 1)) is not None:
            sp.wait_ge(s["wn"].sem, due)
            apart(sp, k, t)
        sp.dma_start(k.mx[:, t.parity], mlp_rows(m.src, row)).then_inc(s["x_in"].sem, 16)
        if m.also is not None:
            if (due := s["also_in"].due(t, lambda x: 16 * x)) is not None:
                sp.wait_ge(s["also_in"].sem, due)
                apart(sp, k, t)
            sp.dma_start(k.malso[:, t.parity], mlp_rows(m.also, row)).then_inc(s["also_in"].sem, 16)

    def load_start(t):
        row = t.row(sp)
        if (due := s["start_in"].due(t, lambda x: 16 * x)) is not None:
            sp.wait_ge(s["start_in"].sem, due)
            apart(sp, k, t)
        if (due := s["out"].due(t, lambda x: x - 1)) is not None:
            sp.wait_ge(s["out"].sem, due)
            apart(sp, k, t)
        sp.dma_start(k.mstart[:, t.parity], mlp_rows(m.start, row)).then_inc(s["start_in"].sem, 16)

    def store(t):
        row = t.row(sp)
        if m.keep is not None:
            if (due := s["kept"].due(t, lambda x: 16 * x)) is not None:
                sp.wait_ge(s["kept"].sem, due)
                apart(sp, k, t)
            sp.wait_ge(s["r"].sem, s["r"].at(t, lambda x: x + 1))
            apart(sp, k, t)
            sp.dma_start(mlp_rows(m.keep, row), k.mr[:, t.parity]).then_inc(s["kept"].sem, 16)
        if (due := s["stored"].due(t, lambda x: 16 * x)) is not None:
            sp.wait_ge(s["stored"].sem, due)
            apart(sp, k, t)
        sp.wait_ge(s["out"].sem, s["out"].at(t, lambda x: x + 1))
        apart(sp, k, t)
        sp.dma_start(mlp_rows(m.dst, row), k.mout[:, t.parity]).then_inc(s["stored"].sem, 16)

    load(Step(0))
    load(Step(1))

    def body(t):
        if m.start is not None:
            load_start(t)
        if t.reg is not None or t.n + 2 < MSTEPS:
            load(t + 2)
        if t.reg is not None or t.n > 0:
            store(t + -1)

    pipeline(sp, MSTEPS, body)
    store(Step(MSTEPS - 1))
    if m.keep is not None:
        sp.wait_ge(s["kept"].sem, s["kept"].base + 16 * MSTEPS)
    sp.wait_ge(s["stored"].sem, s["stored"].base + 16 * MSTEPS)


def tensor_mlp(pe, m):
    k, s, w = m.k, m.s, m.w

    def turn(t):
        pe.wait_ge(s["wn"].sem, s["wn"].at(t, lambda x: x + 1))
        if (due := s["xt"].due(t, lambda x: x)) is not None:
            pe.wait_ge(s["xt"].sem, due)
        for blk in range(MB):
            last = pe.transpose(k.misc[:, blk * P:(blk + 1) * P], k.mwn[:, t.parity, blk], k.ident[:, :])
        last.then_inc(s["t_full"].sem, 1)

    def body(t):
        pe.wait_ge(s["xt"].sem, s["xt"].at(t, lambda x: x + 1))
        for f in range(FC):
            if (due := s["gelu"].due(t, lambda x: FC * (x - 1) + f + 1)) is not None:
                pe.wait_ge(s["gelu"].sem, due)
            pe.matmul(k.scores[f // 2][:, (f % 2) * 512:(f % 2 + 1) * 512], w["w1"][:, f * P:(f + 1) * P], k.mxt[:, t.parity],
                      start=True, stop=True).then_inc(s["h_full"].sem, 1)
        if t.reg is not None or t.n + 1 < MSTEPS:
            turn(t + 1)
        if (due := s["r"].due(t, lambda x: x - 1)) is not None:
            pe.wait_ge(s["r"].sem, due)
        for blk in range(MB):
            for f in range(FC):
                if blk == 0:
                    pe.wait_ge(s["gelu"].sem, s["gelu"].at(t, lambda x: FC * x + f + 1))
                last = pe.matmul(k.turned[t.parity][:, blk * P:(blk + 1) * P], k.mh[:, t.parity, f, blk * P:(blk + 1) * P],
                                 w["w2"][:, f], start=(f == 0), stop=(f == FC - 1))
        last.then_inc(s["y_full"].sem, 1)

    turn(Step(0))
    pipeline(pe, MSTEPS, body)


def scalar_mlp(act, m):
    k, s, w = m.k, m.s, m.w

    def body(t):
        if (due := s["y_full"].due(t, lambda x: x - 1)) is not None:
            act.wait_ge(s["y_full"].sem, due)
        for f in range(FC):
            act.wait_ge(s["h_full"].sem, s["h_full"].at(t, lambda x: FC * x + f + 1))
            act.activation(k.mh[:, t.parity, f], k.scores[f // 2][:, (f % 2) * 512:(f % 2 + 1) * 512], ACT.Gelu,
                           bias=w["b1"][:, f:f + 1], scale=1.0).then_inc(s["gelu"].sem, 1)

    pipeline(act, MSTEPS, body)


def vector_mlp(dve, m):
    k, s, w = m.k, m.s, m.w

    def norm_stats(t):
        dve.wait_ge(s["x_in"].sem, s["x_in"].at(t, lambda x: 16 * (x + 1)))
        vector_norm_stats(dve, k, s, k.mx[:, t.parity], k.mstats[:, t.parity], k.maggr[:, t.parity], ("stats", "aggr"), t, MB)

    def norm(t):
        dve.wait_ge(s["rstd"].sem, s["rstd"].at(t, lambda x: x + 1))
        if (due := s["t_full"].due(t, lambda x: x - 1)) is not None:
            dve.wait_ge(s["t_full"].sem, due)
        for blk in range(MB):
            last = dve.tensor_scalar(k.mwn[:, t.parity, blk], k.mx[:, t.parity, blk], k.maggr[:, t.parity, blk, 0:1],
                                     k.mrstd[:, t.parity, blk:blk + 1], ALU.subtract, ALU.mult)
        last.then_inc(s["wn"].sem, 1)

    def gain(t):
        dve.wait_ge(s["t_full"].sem, s["t_full"].at(t, lambda x: x + 1))
        if (due := s["h_full"].due(t, lambda x: FC * (x - 1))) is not None:
            dve.wait_ge(s["h_full"].sem, due)
        if w["gain"] is None:
            last = dve.tensor_copy(k.mxt[:, t.parity], k.misc[:, :])
        else:
            last = dve.tensor_scalar(k.mxt[:, t.parity], k.misc[:, :], w["gain"], w["shift"], ALU.mult, ALU.add)
        last.then_inc(s["xt"].sem, 1)

    def finish(t):
        dve.wait_ge(s["y_full"].sem, s["y_full"].at(t, lambda x: x + 1))
        dve.wait_ge(s["biased"].sem, s["biased"].at(t, lambda x: x + 1))
        if m.keep is not None:
            if (due := s["kept"].due(t, lambda x: 16 * (x - 1))) is not None:
                dve.wait_ge(s["kept"].sem, due)
        if m.after == "norm":
            if (due := s["rn"].due(t, lambda x: x - 1)) is not None:
                dve.wait_ge(s["rn"].sem, due)
        else:
            if (due := s["out"].due(t, lambda x: x - 1)) is not None:
                dve.wait_ge(s["out"].sem, due)
        dve.tensor_tensor(k.mr[:, t.parity].rearrange("p k c -> p (k c)"), k.turned[t.parity][:, :],
                          k.msum[:, t.parity].rearrange("p k c -> p (k c)"), ALU.add).then_inc(s["r"].sem, 1)
        dve.wait_ge(s["r"].sem, s["r"].at(t, lambda x: x + 1))
        if m.after == "norm":
            vector_norm_stats(dve, k, s, k.mr[:, t.parity], k.mrstats[:, t.parity], k.mraggr[:, t.parity],
                              ("rstats", "raggr"), t, MB)
        else:
            dve.wait_ge(s["start_in"].sem, s["start_in"].at(t, lambda x: 16 * (x + 1)))
            if (due := s["stored"].due(t, lambda x: 16 * (x - 1))) is not None:
                dve.wait_ge(s["stored"].sem, due)
            dve.scalar_tensor_tensor(out=k.mout[:, t.parity].rearrange("p k c -> p (k c)"),
                                     in0=k.mr[:, t.parity].rearrange("p k c -> p (k c)"), scalar=w["gate"],
                                     in1=k.mstart[:, t.parity].rearrange("p k c -> p (k c)"), op0=ALU.mult, op1=ALU.add)\
               .then_inc(s["out"].sem, 1)

    def normed(t):
        dve.wait_ge(s["rrstd"].sem, s["rrstd"].at(t, lambda x: x + 1))
        if (due := s["gained"].due(t, lambda x: x - 1)) is not None:
            dve.wait_ge(s["gained"].sem, due)
        for blk in range(MB):
            last = dve.tensor_scalar(k.mrn[:, t.parity, blk], k.mr[:, t.parity, blk], k.mraggr[:, t.parity, blk, 0:1],
                                     k.mrrstd[:, t.parity, blk:blk + 1], ALU.subtract, ALU.mult)
        last.then_inc(s["rn"].sem, 1)

    for b in range(2):
        norm_stats(Step(b))
        norm(Step(b))
    gain(Step(0))

    def body(t):
        if t.reg is not None or t.n + 2 < MSTEPS:
            norm_stats(t + 2)
        if t.reg is not None or t.n + 1 < MSTEPS:
            gain(t + 1)
        if t.reg is not None or t.n + 2 < MSTEPS:
            norm(t + 2)
        if m.after == "norm" and (t.reg is not None or t.n > 0):
            normed(t + -1)
        finish(t)

    pipeline(dve, MSTEPS, body)
    if m.after == "norm":
        normed(Step(MSTEPS - 1))


def gpsimd_mlp(pool, m):
    k, s, w = m.k, m.s, m.w

    def power(aggr, eps, out, names, t):
        pool.wait_ge(s[names[0]].sem, s[names[0]].at(t, lambda x: x + 1))
        if (due := s[names[3]].due(t, lambda x: x - 1)) is not None:
            pool.wait_ge(s[names[3]].sem, due)
        pool.tensor_tensor(eps[:, t.parity], aggr[:, t.parity, :, 1], k.eps[:, 0:MB], ALU.add).then_inc(s[names[1]].sem, 1)
        pool.wait_ge(s[names[1]].sem, s[names[1]].at(t, lambda x: x + 1))
        pool.tensor_tensor(out[:, t.parity], eps[:, t.parity], k.minus_half[:, 0:MB], ALU.pow).then_inc(s[names[2]].sem, 1)

    def rstd(t):
        power(k.maggr, k.meps, k.mrstd, ("aggr", "eps_in", "rstd", "wn"), t)

    def bias(t):
        pool.wait_ge(s["x_in"].sem, s["x_in"].at(t, lambda x: 16 * (x + 1)))
        if (due := s["r"].due(t, lambda x: x - 1)) is not None:
            pool.wait_ge(s["r"].sem, due)
        x = k.mx[:, t.parity]
        if m.also is not None:
            pool.wait_ge(s["also_in"].sem, s["also_in"].at(t, lambda x: 16 * (x + 1)))
            pool.tensor_tensor(k.mboth[:, t.parity], x, k.malso[:, t.parity], ALU.add).then_inc(s["both"].sem, 1)
            pool.wait_ge(s["both"].sem, s["both"].at(t, lambda x: x + 1))
            x = k.mboth[:, t.parity]
        pool.tensor_tensor(k.msum[:, t.parity], x, w["bias"].unsqueeze(1).to_broadcast([P, MB, C]), ALU.add)\
            .then_inc(s["biased"].sem, 1)

    def after(t):
        power(k.mraggr, k.mreps, k.mrrstd, ("raggr", "reps", "rrstd", "rn"), t)

    def gains(t):
        pool.wait_ge(s["rn"].sem, s["rn"].at(t, lambda x: x + 1))
        if (due := s["out"].due(t, lambda x: x - 1)) is not None:
            pool.wait_ge(s["out"].sem, due)
        if (due := s["stored"].due(t, lambda x: 16 * (x - 1))) is not None:
            pool.wait_ge(s["stored"].sem, due)
        pool.tensor_tensor(k.mrg[:, t.parity], k.mrn[:, t.parity], w["out_gain"].unsqueeze(1).to_broadcast([P, MB, C]),
                           ALU.mult).then_inc(s["gained"].sem, 1)
        pool.wait_ge(s["gained"].sem, s["gained"].at(t, lambda x: x + 1))
        pool.tensor_tensor(k.mout[:, t.parity], k.mrg[:, t.parity], w["out_shift"].unsqueeze(1).to_broadcast([P, MB, C]),
                           ALU.add).then_inc(s["out"].sem, 1)

    rstd(Step(0))
    rstd(Step(1))

    def body(t):
        if t.reg is not None or t.n + 2 < MSTEPS:
            bias(t)
            rstd(t + 2)
        else:
            bias(t)
        if m.after == "norm":
            after(t)
            if t.reg is not None or t.n > 0:
                gains(t + -1)

    pipeline(pool, MSTEPS, body)
    if m.after == "norm":
        gains(Step(MSTEPS - 1))



class Experts:
    def __init__(self, k, name, src, dst, w):
        self.k, self.name, self.src, self.dst, self.w = k, name, src, dst, w
        E = EXPERTS
        self.s = k.signals(dict(
            x_in=16, stored=16, stats=1, aggr=1, eps_in=1, rstd=1, wn=1, t_full=1, xt=1, g_full=1, logits=1, best=1, eq=1,
            rank=1, first=1, chosen=1, c_full=1, chosen_t=1, b_full=1, acc=E + 1, h_full=E * FC, relu=E * FC, y_full=E,
            out=1), MSTEPS)


def sync_experts(sp, m):
    k, s = m.k, m.s

    def load(t):
        row = t.row(sp)
        if (due := s["x_in"].due(t, lambda x: 16 * x)) is not None:
            sp.wait_ge(s["x_in"].sem, due)
            apart(sp, k, t)
        if (due := s["out"].due(t, lambda x: x - 1)) is not None:
            sp.wait_ge(s["out"].sem, due)
            apart(sp, k, t)
        sp.dma_start(k.mx[:, t.parity], mlp_rows(m.src, row)).then_inc(s["x_in"].sem, 16)

    def store(t):
        row = t.row(sp)
        if (due := s["stored"].due(t, lambda x: 16 * x)) is not None:
            sp.wait_ge(s["stored"].sem, due)
            apart(sp, k, t)
        sp.wait_ge(s["out"].sem, s["out"].at(t, lambda x: x + 1))
        apart(sp, k, t)
        sp.dma_start(mlp_rows(m.dst, row), k.mout[:, t.parity]).then_inc(s["stored"].sem, 16)

    load(Step(0))
    load(Step(1))

    def body(t):
        store(t)
        if t.reg is not None or t.n + 2 < MSTEPS:
            load(t + 2)

    pipeline(sp, MSTEPS, body)
    sp.wait_ge(s["stored"].sem, s["stored"].base + 16 * MSTEPS)


def tensor_experts(pe, m):
    k, s, w = m.k, m.s, m.w
    E = EXPERTS

    def body(t):
        pe.wait_ge(s["wn"].sem, s["wn"].at(t, lambda x: x + 1))
        if (due := s["xt"].due(t, lambda x: x)) is not None:
            pe.wait_ge(s["xt"].sem, due)
        for blk in range(MB):
            last = pe.transpose(k.misc[:, blk * P:(blk + 1) * P], k.mwn[:, t.parity, blk], k.ident[:, :])
        last.then_inc(s["t_full"].sem, 1)
        pe.wait_ge(s["xt"].sem, s["xt"].at(t, lambda x: x + 1))
        if (due := s["acc"].due(t, lambda x: (E + 1) * x)) is not None:
            pe.wait_ge(s["acc"].sem, due)
        for blk in range(MB):
            last = pe.matmul(k.num[:, blk * E:(blk + 1) * E], k.mxt[:, t.parity, blk * P:(blk + 1) * P], w["gate_w"],
                             start=True, stop=True)
        last.then_inc(s["g_full"].sem, 1)

        def hidden(e):
            for f in range(FC):
                if (due := s["relu"].due(t, lambda x: FC * (E * x + e - 1) + f + 1)) is not None:
                    pe.wait_ge(s["relu"].sem, due)
                pe.matmul(k.scores[f // 2][:, (f % 2) * 512:(f % 2 + 1) * 512], w["w1"][:, e, f * P:(f + 1) * P],
                          k.mxt[:, t.parity], start=True, stop=True).then_inc(s["h_full"].sem, 1)

        hidden(0)
        pe.wait_ge(s["chosen"].sem, s["chosen"].at(t, lambda x: x + 1))
        for blk in range(MB):
            last = pe.transpose(k.misc[0:E, blk * P:(blk + 1) * P], k.mchosen[:, t.parity, blk], k.ident[:, :])
        last.then_inc(s["c_full"].sem, 1)
        pe.wait_ge(s["chosen_t"].sem, s["chosen_t"].at(t, lambda x: x + 1))
        for blk in range(MB):
            last = pe.matmul(k.num[:, blk * P:(blk + 1) * P], k.mchosen_t[:, blk * P:(blk + 1) * P], w["b2"],
                             start=True, stop=True)
        last.then_inc(s["b_full"].sem, 1)
        for e in range(E):
            if e + 1 < E:
                hidden(e + 1)
            if (due := s["acc"].due(t, lambda x: (E + 1) * x + e)) is not None:
                pe.wait_ge(s["acc"].sem, due)
            for blk in range(MB):
                for f in range(FC):
                    if blk == 0:
                        pe.wait_ge(s["relu"].sem, s["relu"].at(t, lambda x: FC * (E * x + e) + f + 1))
                    last = pe.matmul(k.turned[e % 2][:, blk * P:(blk + 1) * P], k.mh[:, e % 2, f, blk * P:(blk + 1) * P],
                                     w["w2"][:, e, f], start=(f == 0), stop=(f == FC - 1))
            last.then_inc(s["y_full"].sem, 1)

    pipeline(pe, MSTEPS, body)


def scalar_experts(act, m):
    k, s, w = m.k, m.s, m.w

    def body(t):
        for e in range(EXPERTS):
            if (due := s["y_full"].due(t, lambda x: EXPERTS * x + e - 1)) is not None:
                act.wait_ge(s["y_full"].sem, due)
            for f in range(FC):
                act.wait_ge(s["h_full"].sem, s["h_full"].at(t, lambda x: FC * (EXPERTS * x + e) + f + 1))
                act.activation(k.mh[:, e % 2, f], k.scores[f // 2][:, (f % 2) * 512:(f % 2 + 1) * 512], ACT.Relu,
                               bias=w["b1"][:, e, f:f + 1], scale=1.0).then_inc(s["relu"].sem, 1)

    pipeline(act, MSTEPS, body)


def vector_experts(dve, m):
    k, s, w = m.k, m.s, m.w
    E = EXPERTS

    def norm_in(t):
        dve.wait_ge(s["x_in"].sem, s["x_in"].at(t, lambda x: 16 * (x + 1)))
        vector_norm_stats(dve, k, s, k.mx[:, t.parity], k.mstats[:, t.parity], k.maggr[:, t.parity], ("stats", "aggr"), t, MB)
        dve.wait_ge(s["rstd"].sem, s["rstd"].at(t, lambda x: x + 1))
        if (due := s["t_full"].due(t, lambda x: x - 1)) is not None:
            dve.wait_ge(s["t_full"].sem, due)
        for blk in range(MB):
            last = dve.tensor_scalar(k.mwn[:, t.parity, blk], k.mx[:, t.parity, blk], k.maggr[:, t.parity, blk, 0:1],
                                     k.mrstd[:, t.parity, blk:blk + 1], ALU.subtract, ALU.mult)
        last.then_inc(s["wn"].sem, 1)

    def body(t):
        norm_in(t)
        dve.wait_ge(s["t_full"].sem, s["t_full"].at(t, lambda x: x + 1))
        dve.tensor_copy(k.mxt[:, t.parity], k.misc[:, :]).then_inc(s["xt"].sem, 1)
        one = lambda x: x.unsqueeze(2).to_broadcast([P, MB, E])
        rows = lambda x: x.unsqueeze(1).to_broadcast([P, MB, E])
        dve.wait_ge(s["g_full"].sem, s["g_full"].at(t, lambda x: x + 1))
        dve.tensor_tensor(k.mlogits[:, :, :], k.num[:, 0:MB * E].rearrange("p (k e) -> p k e", e=E), rows(w["gate_b"]),
                          ALU.add).then_inc(s["logits"].sem, 1)
        dve.wait_ge(s["logits"].sem, s["logits"].at(t, lambda x: x + 1))
        dve.tensor_reduce(k.mbest[:, :], k.mlogits[:, :, :], AX.X, ALU.max).then_inc(s["best"].sem, 1)
        dve.wait_ge(s["best"].sem, s["best"].at(t, lambda x: x + 1))
        dve.tensor_tensor(k.meq[:, :, :], k.mlogits[:, :, :], one(k.mbest[:, :]), ALU.is_equal).then_inc(s["eq"].sem, 1)
        dve.wait_ge(s["eq"].sem, s["eq"].at(t, lambda x: x + 1))
        dve.tensor_tensor(k.mrank[:, :, :], k.meq[:, :, :], rows(k.falling[:, :]), ALU.mult).then_inc(s["rank"].sem, 1)
        dve.wait_ge(s["rank"].sem, s["rank"].at(t, lambda x: x + 1))
        dve.tensor_reduce(k.mfirst[:, :], k.mrank[:, :, :], AX.X, ALU.max).then_inc(s["first"].sem, 1)
        dve.wait_ge(s["first"].sem, s["first"].at(t, lambda x: x + 1))
        if (due := s["c_full"].due(t, lambda x: x - 1)) is not None:
            dve.wait_ge(s["c_full"].sem, due)
        dve.tensor_tensor(k.mchosen[:, t.parity], k.mrank[:, :, :], one(k.mfirst[:, :]), ALU.is_equal).then_inc(s["chosen"].sem, 1)
        dve.wait_ge(s["c_full"].sem, s["c_full"].at(t, lambda x: x + 1))
        dve.tensor_copy(k.mchosen_t[:, :], k.misc[0:E, :]).then_inc(s["chosen_t"].sem, 1)
        dve.wait_ge(s["b_full"].sem, s["b_full"].at(t, lambda x: x + 1))
        dve.tensor_copy(k.macc[:, 0].rearrange("p k c -> p (k c)"), k.num[:, :]).then_inc(s["acc"].sem, 1)
        for e in range(E):
            dve.wait_ge(s["acc"].sem, s["acc"].at(t, lambda x: (E + 1) * x + e + 1))
            dve.wait_ge(s["y_full"].sem, s["y_full"].at(t, lambda x: E * x + e + 1))
            for blk in range(MB):
                last = dve.scalar_tensor_tensor(out=k.macc[:, (e + 1) % 2, blk], in0=k.turned[e % 2][:, blk * P:(blk + 1) * P],
                                                scalar=k.mchosen[:, t.parity, blk, e:e + 1], in1=k.macc[:, e % 2, blk],
                                                op0=ALU.mult, op1=ALU.add)
            last.then_inc(s["acc"].sem, 1)
        dve.wait_ge(s["acc"].sem, s["acc"].at(t, lambda x: (E + 1) * (x + 1)))
        if (due := s["stored"].due(t, lambda x: 16 * (x - 1))) is not None:
            dve.wait_ge(s["stored"].sem, due)
        dve.scalar_tensor_tensor(out=k.mout[:, t.parity], in0=k.macc[:, E % 2], scalar=w["gate"], in1=k.mx[:, t.parity],
                                 op0=ALU.mult, op1=ALU.add).then_inc(s["out"].sem, 1)

    pipeline(dve, MSTEPS, body)


def gpsimd_experts(pool, m):
    k, s = m.k, m.s

    def body(t):
        pool.wait_ge(s["aggr"].sem, s["aggr"].at(t, lambda x: x + 1))
        if (due := s["wn"].due(t, lambda x: x - 1)) is not None:
            pool.wait_ge(s["wn"].sem, due)
        pool.tensor_tensor(k.meps[:, t.parity], k.maggr[:, t.parity, :, 1], k.eps[0:k.meps.shape[0], 0:k.meps.shape[2]], ALU.add).then_inc(s["eps_in"].sem, 1)
        pool.wait_ge(s["eps_in"].sem, s["eps_in"].at(t, lambda x: x + 1))
        pool.tensor_tensor(k.mrstd[:, t.parity], k.meps[:, t.parity], k.minus_half[:, 0:MB], ALU.pow).then_inc(s["rstd"].sem, 1)

    pipeline(pool, MSTEPS, body)



class Core:

    def __init__(self, nc, ctx):
        self.nc, self.ctx, self.counts = nc, ctx, {}
        self.scores = [ctx.enter_context(nc.psum_tensor(f"scores{i}", [P, 1024], F32)) for i in range(2)]
        self.turned = [ctx.enter_context(nc.psum_tensor(f"turned{i}", [P, 512], F32)) for i in range(2)]
        self.num = ctx.enter_context(nc.psum_tensor("num", [P, 512], F32))
        self.misc = ctx.enter_context(nc.psum_tensor("misc", [P, 512], F32))
        self.ident = self.sb("ident", [P, P])
        self.identb = self.sb("identb", [P, P], BF16)
        self.above = self.sb("above", [P, P], BF16)
        self.own8 = self.sb("own8", [P, 16])
        self.own32 = self.sb("own32", [P, 4])
        self.own_columns = self.sb("own_columns", [P, 4, 32])
        self.own_pair8 = self.sb("own_pair8", [P, 8, P])
        self.own_pair32 = self.sb("own_pair32", [P, 8, P])
        self.minus_half = self.sb("minus_half", [P, 4])
        self.eps = self.sb("eps", [P, 4])
        self.falling = self.sb("falling", [P, EXPERTS])
        self.ones = self.sb("ones", [P, P])
        self.space = self.sb("space", [P, SPACE])
        self.at = 0
        t = self.take
        self.through = self.sem("through")
        self.km, self.qT, self.val = t(2, 16, 256), t(2, 4, 256), t(2, 2, 512)
        self.probs, self.pt = t(2, 2, 512), t(8, 384)
        self.numS, self.rx, self.ot = t(2, 4, 256), t(2, 512), t(4, 256)
        self.xq, self.xk, self.wn, self.x_in = t(2, 256), t(2, 256), t(2, 2, 128), t(2, 2, 128)
        self.base_in, self.base_sum, self.res = t(2, 2, 128), t(2, 2, 128), t(2, 2, 128)
        self.nmax, self.sums, self.rsum = t(2, 4), t(2, 2, 16), t(2, 2, 16)
        self.stats, self.aggr, self.vareps, self.rstd = t(2, 2, 6), t(2, 2, 2), t(2, 2), t(2, 2)
        self.cstats, self.caggr, self.cvareps, self.crstd = t(2, 1, 6)[0:TC], t(2, 1, 2)[0:TC], t(2, 1)[0:TC], t(2, 1)[0:TC]
        self.cmax = t(2, 8)
        self.ctx_in, self.cn, self.xc = t(2, 64)[0:TC], t(2, 64)[0:TC], t(2, 2, 64)[0:TC]
        mark = self.at
        self.at = 0
        self.km_cross, self.vb, self.ptc = t(2, 1024), t(2, 8, 128), t(2, 4, 256)
        self.pc = t(2, 512)
        assert self.at <= 2 * 16 * 256, self.at
        self.at = 0
        self.mx, self.malso, self.mstart, self.mwn = t(2, 4, 128), t(2, 4, 128), t(2, 4, 128), t(2, 4, 128)
        self.mxt, self.msum, self.mboth, self.mr = t(2, 512), t(2, 4, 128), t(2, 4, 128), t(2, 4, 128)
        self.mrn, self.mrg, self.mout, self.mh = t(2, 4, 128), t(2, 4, 128), t(2, 4, 128), t(2, 4, 512)
        self.macc = t(2, 4, 128)
        self.mstats, self.maggr, self.meps, self.mrstd = t(2, 4, 6), t(2, 4, 2), t(2, 4), t(2, 4)
        self.mrstats, self.mraggr, self.mreps, self.mrrstd = t(2, 4, 6), t(2, 4, 2), t(2, 4), t(2, 4)
        self.mlogits, self.mbest, self.meq, self.mrank = t(4, 8), t(4), t(4, 8), t(4, 8)
        self.mfirst, self.mchosen, self.mchosen_t = t(4), t(2, 4, 8), t(512)[0:EXPERTS]
        mark = max(mark, self.at)
        self.at = 0
        self.quant, self.quant_round, self.quant_out, self.proj_sum = t(1024), t(1024), t(1024), t(512)
        self.fc_t, self.proj_t, self.bfc_t, self.bproj_t = t(512), t(512), t(512)[0:RANK], t(128)[0:RANK]
        self.amax, self.amax_t, self.amax_d, self.amax_b = t(2), t(1)[0:2], t(2)[0:2], t(2)
        self.qscale, self.qinv = t(2), t(2)
        self.bv_b, self.bcv_b, self.bp_g, self.value_rows = t(128), t(128), t(128), t(256)
        mark = max(mark, self.at)
        assert mark <= SPACE, mark

    def sb(self, name, shape, dt=F32):
        return self.ctx.enter_context(self.nc.sbuf_tensor(name, shape, dt))

    def sem(self, name):
        return self.ctx.enter_context(self.nc.semaphore(name))

    def signals(self, each, steps):
        out = {}
        for name, n in each.items():
            if name not in self.counts:
                self.counts[name] = (self.sem(name), 0)
            sem, base = self.counts[name]
            out[name] = Signal(sem, base)
            self.counts[name] = (sem, base + n * steps)
        return out

    def take(self, *shape):
        n = 1
        for x in shape:
            n *= x
        flat = self.space[:, self.at:self.at + n]
        self.at += n
        if len(shape) == 1:
            return flat
        if len(shape) == 2:
            return flat.rearrange("p (a b) -> p a b", b=shape[1])
        return flat.rearrange("p (a b c) -> p a b c", b=shape[1], c=shape[2])


class Weights:

    FIRST_ROWS = ("bk", "bq", "bck", "bcq", "bv", "bcv")
    LATER_ROWS = tuple(f"{a}_{n}" for a in ("a1", "a2") for n in ("lnx_g", "lnx_b", "lny_g", "lny_b", "ln3_g", "ln3_b"))

    def __init__(self, k):
        self.k = k
        t = lambda name, *shape: k.sb("w_" + name, list(shape))
        self.first_rows, self.first_cols = t("first_rows", 8, P), t("first_cols", P, 8)
        self.later_rows, self.later_cols = t("later_rows", 64, P), t("later_cols", P, 64)
        self.scaled = t("scaled", P, 2)
        self.raw_gates, self.gates = t("raw_gates", P, 4), t("gates", P, 4)
        self.Wq, self.Wk, self.Wv, self.Wcq = (t(n, C, C) for n in ("Wq", "Wk", "Wv", "Wcq"))
        self.Wck, self.Wcv = t("Wck", CC, C), t("Wcv", CC, C)
        self.raw_wp, self.wp, self.bp = t("raw_wp", C, C), t("wp", P, 1, C), t("bp", P, C)
        self.o_bias1, self.o_bias2 = t("o_bias1", P, C), t("o_bias2", P, C)
        self.fc, self.proj = t("fc", P, HID), t("proj", P, FC, C)
        self.raw_bfc, self.raw_bproj = t("raw_bfc", P, FC, RANK), t("raw_bproj", P, RANK)
        self.a_fc, self.a_proj = t("a_fc", RANK, C), t("a_proj", RANK, HID)
        self.proj_b, self.proj_bg = t("proj_b", P, C), t("proj_bg", P, C)
        self.ln = {n: t(n, P, C) for n in ("ln1_g", "ln1_b", "ln2_g", "ln2_b")}
        self.attn = {}
        for a, cy in (("a1", C), ("a2", CC)):
            self.attn[a] = dict(wq=t(a + "_wq", C, H, 32), wk=t(a + "_wk", cy, H, 32), wv=t(a + "_wv", cy, H, 32),
                                li1_w=t(a + "_li1_w", P, 4, C), li2_w=t(a + "_li2_w", C, HID), li3_w=t(a + "_li3_w", P, FC, C),
                                li1_b=t(a + "_li1_b", P, C), li3_b=t(a + "_li3_b", P, C))
        self.raw_gate, self.gate_w, self.gate_b = t("raw_gate", EXPERTS, C), t("gate_w", C, EXPERTS), t("gate_b", P, EXPERTS)
        self.w1, self.w2 = t("w1", P, EXPERTS, HID), t("w2", P, EXPERTS, FC, C)
        self.b2 = t("b2", EXPERTS, C)

    def col(self, name):
        if name in self.FIRST_ROWS:
            i = self.FIRST_ROWS.index(name)
            return self.first_cols[:, i:i + 1]
        i = self.LATER_ROWS.index(name)
        return self.later_cols[0:CC if name[0:6] == "a2_lny" else P, i:i + 1]

    def hidden_bias(self, i):
        n = len(self.LATER_ROWS) + FC * i
        return self.later_cols[:, n:n + FC]

    @property
    def expert_bias(self):
        return self.later_cols[:, 32:64].rearrange("p (e f) -> p e f", f=FC)


def on_every_partition(v):
    return v.rearrange("(a n) -> a n", a=1).to_broadcast([P, v.shape[0]])


def first_loads(w, g_xattn, g_ffn, A):
    rows = [(w.first_rows[i:i + 1, :], A[n].rearrange("(a n) -> a n", a=1)) for i, n in enumerate(w.FIRST_ROWS)]
    return rows + [
        (w.raw_gates[:, 0:2], on_every_partition(g_xattn)), (w.raw_gates[:, 2:4], on_every_partition(g_ffn)),
        (w.raw_wp[:, :], A["Wp"]), (w.Wq[:, :], A["Wq"]), (w.Wk[:, :], A["Wk"]), (w.Wv[:, :], A["Wv"]),
        (w.Wcq[:, :], A["Wcq"]), (w.Wck[:, :], A["Wck"]), (w.Wcv[:, :], A["Wcv"]), (w.bp[:, :], on_every_partition(A["bp"]))]


def later_loads(w, F, X, M):
    out = []
    for i, n in enumerate(w.LATER_ROWS):
        out.append((w.later_rows[i:i + 1, 0:X[n].shape[0]], X[n].rearrange("(a n) -> a n", a=1)))
    for i, v in enumerate((F["b_fc"], X["a1_li2_b"], X["a2_li2_b"])):
        n = len(w.LATER_ROWS) + FC * i
        out.append((w.later_rows[n:n + FC, :], v.rearrange("(f p) -> f p", p=P)))
    out += [
        (w.later_rows[32:64, :], M["b1"].rearrange("e (f p) -> (e f) p", p=P)),
        (w.fc[:, :].rearrange("p (f c) -> p f c", f=FC), F["W_fc"].rearrange("(f p) c -> p f c", p=P)),
        (w.proj[:, :, :].rearrange("p f c -> p (f c)"), F["W_proj"]),
        (w.raw_bfc[:, :, :], F["B_fc"].rearrange("(f p) r -> p f r", p=P)), (w.raw_bproj[:, :], F["B_proj"]),
        (w.a_fc[:, :], F["A_fc"]), (w.a_proj[:, :], F["A_proj"]), (w.proj_b[:, :], on_every_partition(F["b_proj"])),
        (w.raw_gate[:, :], M["gate_w"]), (w.gate_b[:, :], on_every_partition(M["gate_b"])), (w.b2[:, :], M["b2"]),
        (w.w1[:, :, :].rearrange("p e (f c) -> p (e f) c", c=C), M["w1"].rearrange("e (f p) c -> p (e f) c", p=P)),
        (w.w2[:, :, :, :].rearrange("p e f c -> p e (f c)"), M["w2"].rearrange("e p h -> p e h"))]
    for a, t in w.attn.items():
        out += [(t[n][:, :, :], X[f"{a}_{n}"].rearrange("h c d -> c h d")) for n in ("wq", "wk", "wv")]
        out += [(t[n][:, :, :], X[f"{a}_{n}"].rearrange("(g p) c -> p g c", p=P)) for n in ("li1_w", "li3_w")]
        out += [(t["li2_w"][:, :], X[f"{a}_li2_w"])]
        out += [(t[n][:, :], on_every_partition(X[f"{a}_{n}"])) for n in ("li1_b", "li3_b")]
    return out + [(w.ln[n][:, :], on_every_partition(X[n])) for n in w.ln]



class Ready:

    FILLED_FIRST, RESULTS_FIRST = 2, 5

    def __init__(self, k):
        self.made, self.loaded_first, self.loaded_later = k.sem("made"), k.sem("loaded_first"), k.sem("loaded_later")
        self.gated, self.filled, self.result = k.sem("gated"), k.sem("filled"), k.sem("result")
        self.turned, self.emptied = k.sem("turned"), k.sem("emptied")


def tensor_first(pe, k, w, r):
    pe.transpose(k.num[:, 0:8], w.first_rows[:, :], k.ident[0:8, 0:8]).then_inc(r.filled, 1)
    pe.wait_ge(r.result, 3)
    pe.matmul(k.misc[:, 0:P], k.bv_b, w.raw_wp[:, :], start=True, stop=True)
    pe.matmul(k.misc[:, P:2 * P], k.bcv_b, w.raw_wp[:, :], start=True, stop=True).then_inc(r.filled, 1)


def vector_first(dve, k, w, r):
    result = Count(r.result)
    dve.wait_ge(r.filled, 1)
    result.inc(dve.tensor_copy(w.first_cols[:, :], k.num[:, 0:8]))
    dve.wait_ge(r.result, result.n)
    result.inc(dve.tensor_scalar(k.bv_b, k.ones[:, :], w.col("bv"), None, ALU.mult))
    result.inc(dve.tensor_scalar(k.bcv_b, k.ones[:, :], w.col("bcv"), None, ALU.mult))
    dve.tensor_scalar(w.scaled[:, 0:1], w.col("bq"), 8.0 ** -0.5, None, ALU.mult)
    dve.tensor_scalar(w.scaled[:, 1:2], w.col("bcq"), 8.0 ** -0.5, None, ALU.mult)
    dve.wait_ge(r.gated, 1)
    dve.tensor_scalar(w.wp[:, 0], w.raw_wp[:, :], w.gates[:, 0:1], None, ALU.mult)
    dve.wait_ge(r.filled, 2)
    result.inc(dve.tensor_tensor(k.bp_g, w.bp[:, :], k.misc[:, 0:P], ALU.add))
    dve.wait_ge(r.result, result.n)
    dve.tensor_scalar(w.o_bias1[:, :], k.bp_g, w.gates[:, 0:1], None, ALU.mult)
    result.inc(dve.tensor_scalar(w.o_bias2[:, :], k.misc[:, P:2 * P], w.gates[:, 0:1], None, ALU.mult))
    assert result.n == Ready.RESULTS_FIRST



class Prepare:

    ROW_MAX, MAX, DIAGONAL, SCALE, INVERSE, QUANTISED = 1, 2, 3, 4, 5, 15

    def __init__(self, k, w, r, later):
        self.k, self.w, self.r, self.later = k, w, r, later


def nothing(eng, m):
    pass


def tensor_prepare(pe, m):
    k, w, r, n = m.k, m.w, m.r, Ready.RESULTS_FIRST
    turned, filled = Count(r.turned), Count(r.filled)

    def turn(bank, parts, rows):
        for f, part in enumerate(parts):
            last = pe.transpose(bank[0:part.shape[1], f * rows:(f + 1) * rows], part, k.ident[0:rows, 0:rows])
        return last

    def to_scalar(parts, rows):
        if turned.n >= 4:
            pe.wait_ge(r.emptied, turned.n - 3)
        half = turned.n % 2 * 512
        turned.inc(turn(k.scores[turned.n // 2 % 2][:, half:half + 512], parts, rows))

    pe.wait_ge(r.loaded_later, m.later)
    to_scalar([w.later_rows[:, :]], 64)
    to_scalar([w.raw_bfc[:, f] for f in range(FC)], P)
    to_scalar([w.raw_bproj[:, :]], P)
    to_scalar([w.raw_gate[:, :]], EXPERTS)
    pe.wait_ge(r.result, n + m.ROW_MAX)
    filled.inc(turn(k.num, [k.amax], P))
    for e in range(EXPERTS):
        to_scalar([w.w1[:, e, f * P:(f + 1) * P] for f in range(FC)], P)
        to_scalar([w.w2[:, e, f] for f in range(FC)], P)
        if e == 1:
            pe.wait_ge(r.result, n + m.DIAGONAL)
            filled.inc(pe.matmul(k.misc[:, 0:2], k.ones[0:2, :], k.amax_d, start=True, stop=True))
    pe.wait_ge(r.result, n + m.QUANTISED)
    q = k.quant_out
    filled.inc(turn(k.turned[0], [q[:, f * P:(f + 1) * P] for f in range(FC)], P))
    filled.inc(turn(k.turned[1], [q[:, HID + f * P:HID + (f + 1) * P] for f in range(FC)], P))
    pe.wait_ge(r.emptied, turned.n)
    filled.inc(pe.matmul(k.num[:, :], w.a_fc[:, :], k.bfc_t, start=True, stop=True))
    for f in range(FC):
        last = pe.matmul(k.misc[:, f * P:(f + 1) * P], w.a_proj[:, f * P:(f + 1) * P], k.bproj_t, start=True, stop=True)
    filled.inc(last)


def scalar_prepare(act, m):
    k, w, r = m.k, m.w, m.r
    emptied = Count(r.emptied)

    def empty(out, scale=None):
        act.wait_ge(r.turned, emptied.n + 1)
        half = emptied.n % 2 * 512
        bank = k.scores[emptied.n // 2 % 2][0:out.shape[0], half:half + out.shape[1]]
        emptied.inc(act.copy(out, bank) if scale is None else act.mul(out, bank, scale))

    empty(w.later_cols[:, :])
    empty(k.bfc_t, LORA_SCALE)
    empty(k.bproj_t, LORA_SCALE)
    empty(w.gate_w[:, :])
    for e in range(EXPERTS):
        empty(w.w1[:, e])
        empty(w.w2[:, e].rearrange("p f c -> p (f c)"))


def vector_prepare(dve, m):
    k, w, r = m.k, m.w, m.r
    n, filled = Ready.RESULTS_FIRST, Ready.FILLED_FIRST
    result = Count(r.result)
    result.n = n
    raws = (w.fc[:, :], w.proj[:, :, :].rearrange("p f c -> p (f c)"))
    dve.wait_ge(r.loaded_later, m.later)
    dve.tensor_reduce(k.amax[:, 0:1], raws[0], AX.X, ALU.max, apply_absolute_value=True)
    result.inc(dve.tensor_reduce(k.amax[:, 1:2], raws[1], AX.X, ALU.max, apply_absolute_value=True))
    dve.wait_ge(r.filled, filled + 1)
    result.inc(dve.tensor_reduce(k.amax_t, k.num[0:2, 0:P], AX.X, ALU.max))
    dve.wait_ge(r.result, result.n)
    result.inc(dve.tensor_scalar(k.amax_d, k.ident[0:2, 0:2], k.amax_t, None, ALU.mult))
    dve.wait_ge(r.filled, filled + 2)
    result.inc(dve.tensor_scalar(k.qscale, k.misc[:, 0:2], 1.0 / QMAX, None, ALU.mult))
    dve.wait_ge(r.result, result.n)
    result.inc(dve.reciprocal(k.qinv, k.qscale))
    assert result.n == n + m.INVERSE

    def quantise(step, j):
        half = slice(j * HID, (j + 1) * HID)
        q, rounded, raw = k.quant[:, half], k.quant_round[:, half], raws[j]
        if step == 0:
            return dve.tensor_scalar(q, raw, k.qinv[:, j:j + 1], ROUND, ALU.mult, ALU.add)
        if step == 1:
            return dve.tensor_scalar(rounded, q, ROUND, QMAX, ALU.subtract, ALU.min)
        if step == 2:
            return dve.tensor_scalar(q, rounded, -QMAX - 1.0, k.qscale[:, j:j + 1], ALU.max, ALU.mult)
        if step == 3:
            return dve.tensor_tensor(rounded, q, raw, ALU.subtract)
        return dve.tensor_tensor(k.quant_out[:, half], raw, rounded, ALU.add)

    for step in range(5):
        for j in range(2):
            dve.wait_ge(r.result, result.n - (1 if step else j))
            result.inc(quantise(step, j))
    assert result.n == n + m.QUANTISED
    dve.wait_ge(r.filled, filled + 3)
    dve.tensor_copy(k.fc_t, k.turned[0][:, :])
    dve.wait_ge(r.filled, filled + 4)
    result.inc(dve.tensor_copy(k.proj_t, k.turned[1][:, :]))
    dve.wait_ge(r.result, result.n)
    dve.wait_ge(r.filled, filled + 5)
    dve.tensor_tensor(w.fc[:, :], k.num[:, :], k.fc_t, ALU.add)
    dve.wait_ge(r.filled, filled + 6)
    result.inc(dve.tensor_tensor(k.proj_sum, k.misc[:, :], k.proj_t, ALU.add))
    dve.wait_ge(r.result, result.n)
    dve.tensor_scalar(raws[1], k.proj_sum, w.gates[:, 2:3], None, ALU.mult)
    result.inc(dve.tensor_scalar(w.proj_bg[:, :], w.proj_b[:, :], w.gates[:, 2:3], None, ALU.mult))


def gpsimd_constants(pool, k, w, made):
    def fill(t, v):
        made.inc(pool.memset(t, v))

    def keep(t, pattern, base, cm, op=ALU.is_ge, v=0.0):
        pool.wait_ge(made.sem, made.n)
        made.inc(pool.affine_select(out=t, in_=t, compare_op=op, fill=v, base=base, pattern=pattern, channel_multiplier=cm))

    fill(k.ident[:, :], 0.0)
    keep(k.ident[:, :], [[-1, P]], 0, 1, ALU.not_equal, 1.0)
    for t, v in ((k.identb, 0.0), (k.above, 0.0), (k.own8, 1.0), (k.own32, 1.0), (k.ones, 1.0), (k.minus_half, -0.5), (k.eps, EPS)):
        fill(t[:, :], v)
    for t in (k.own_columns, k.own_pair8, k.own_pair32):
        fill(t[:, :, :], 1.0)
    for e in range(EXPERTS):
        fill(k.falling[:, e:e + 1], float(EXPERTS - e))
    keep(k.identb[:, :], [[-1, P]], 0, 1, ALU.not_equal, 1.0)
    keep(k.above[:, :], [[-1, P]], 0, 1, ALU.is_ge, MASKED)
    for own, n in ((k.own8, 8), (k.own32, 32)):
        keep(own[:, :], [[-n, P // n]], 0, 1)
        keep(own[:, :], [[n, P // n]], n - 1, -1)
    keep(k.own_columns[:, :, :], [[-8, 4], [1, 32]], 0, 0)
    keep(k.own_columns[:, :, :], [[8, 4], [-1, 32]], 7, 0)
    for half in range(2):
        part = slice(64 * half, 64 * half + 64)
        keep(k.own_pair8[part], [[-16, 8], [1, P]], -8 * half, 0)
        keep(k.own_pair8[part], [[16, 8], [-1, P]], 8 * half + 7, 0)
        for j in range(2):
            four = k.own_pair32[part].rearrange("p (g j) c -> p g j c", j=2)[:, :, j]
            keep(four, [[0, 4], [1, P]], -(64 * j + 32 * half), 0)
            keep(four, [[0, 4], [-1, P]], 64 * j + 32 * half + 31, 0)


def network(nc, x, ctx_512, g_xattn, g_ffn, A, F, X, M, out, parts_run=None):
    with ExitStack() as stack:
        k = Core(nc, stack)
        w, r = Weights(k), Ready(k)
        made = Count(r.made)
        first, later = first_loads(w, g_xattn, g_ffn, A), later_loads(w, F, X, M)
        phase, cleared = k.sem("phase"), k.sem("cleared")
        made_all = 40

        def dram(name):
            return nc.dram_tensor(name, [B, S, C], F32, kind="Internal").ap()

        s1, s2, x2, xx, xo1, xm, xo2, x3 = (dram(n) for n in ("s1", "s2", "x2", "xx", "xo1", "xm", "xo2", "x3"))

        def second(a):
            t = w.attn[a]
            wide = {n: t[n][:, :, :].rearrange("c h d -> c (h d)") for n in ("wq", "wk", "wv")}
            return dict(wide, wo=t["li1_w"], q_gain=w.col(a + "_lnx_g"), q_shift=w.col(a + "_lnx_b"),
                        k_gain=w.col(a + "_lny_g"), k_shift=w.col(a + "_lny_b"), q_bias=None, k_bias=None,
                        o_bias=t["li1_b"][:, :], own=k.own32, own_pair=k.own_pair32[:, :, :])

        def first_layer(wq, wk, wv, q_bias, k_bias, o_bias):
            return dict(wq=wq, wk=wk, wv=wv, wo=w.wp, q_gain=None, q_shift=None, k_gain=None, k_shift=None, q_bias=q_bias,
                        k_bias=k_bias, o_bias=o_bias[:, :], own=k.own8, own_pair=k.own_pair8[:, :, :])

        def mlp(a, i):
            t = w.attn[a]
            return dict(gain=w.col(a + "_ln3_g"), shift=w.col(a + "_ln3_b"), w1=t["li2_w"], b1=w.hidden_bias(i), w2=t["li3_w"],
                        bias=t["li3_b"][:, :], out_gain=w.ln["ln2_g"][:, :], out_shift=w.ln["ln2_b"][:, :], gate=w.gates[:, 1:2])

        parts = [
            Attention(k, "a", "self", 8, "before", x, x, s1, None, False,
                      first_layer(w.Wq, w.Wk, w.Wv, w.scaled[:, 0:1], w.col("bk"), w.o_bias1)),
            Attention(k, "b", "cross", 8, None, x, s1, s2, ctx_512, False,
                      first_layer(w.Wcq, w.Wck, w.Wcv, w.scaled[:, 1:2], w.col("bck"), w.o_bias2)),
            Prepare(k, w, r, 16 * len(later)),
            Mlp(k, "c", s2, None, "norm", xx, x2, None, dict(
                gain=None, shift=None, w1=w.fc, b1=w.hidden_bias(0), w2=w.proj, bias=w.proj_bg[:, :],
                out_gain=w.ln["ln1_g"][:, :], out_shift=w.ln["ln1_b"][:, :])),
            Attention(k, "d", "self", 32, "after", xx, xx, xo1, None, False, second("a1")),
            Mlp(k, "e", xo1, xx, "norm", xm, None, None, mlp("a1", 1)),
            Attention(k, "f", "cross", 32, None, xm, xm, xo2, ctx_512, True, second("a2")),
            Mlp(k, "g", xo2, xm, "add", x3, None, x2, mlp("a2", 2)),
            Experts(k, "h", x3, out, dict(gate_w=w.gate_w[:, :], gate_b=w.gate_b[:, :], w1=w.w1, b1=w.expert_bias, w2=w.w2,
                                          b2=w.b2[:, :], gate=w.gates[:, 3:4])),
        ][0:parts_run]
        [p for p in parts if not isinstance(p, Prepare)][-1].dst = out
        parts[0].weights_ahead, parts[0].loaded_ahead = later, r.loaded_later
        block = stack.enter_context(nc.Block())

        def phases(eng, programs):
            for n, part in enumerate(parts):
                eng.drain().then_inc(phase, 1)
                eng.wait_ge(phase, 5 * (n + 1))
                programs[type(part)](eng, part)

        @block.sync
        def _(sp):
            sp.wait_ge(cleared, 1)
            for dst, src in first:
                sp.dma_start(dst, src).then_inc(r.loaded_first, 16)
            phases(sp, {Attention: sync_attention, Mlp: sync_mlp, Experts: sync_experts, Prepare: nothing})

        @block.gpsimd
        def _(pool):
            gpsimd_constants(pool, k, w, made)
            assert made.n == made_all, made.n
            pool.wait_ge(r.made, made_all)
            phases(pool, {Attention: gpsimd_attention, Mlp: gpsimd_mlp, Experts: gpsimd_experts, Prepare: nothing})

        @block.scalar
        def _(act):
            act.wait_ge(cleared, 1)
            act.wait_ge(r.loaded_first, 16 * len(first))
            act.activation(w.gates[:, :], w.raw_gates[:, :], ACT.Tanh).then_inc(r.gated, 1)
            phases(act, {Attention: scalar_attention, Mlp: scalar_mlp, Experts: scalar_experts, Prepare: scalar_prepare})

        @block.tensor
        def _(pe):
            pe.wait_ge(r.loaded_first, 16 * len(first))
            pe.wait_ge(r.made, made_all)
            tensor_first(pe, k, w, r)
            phases(pe, {Attention: tensor_attention, Mlp: tensor_mlp, Experts: tensor_experts, Prepare: tensor_prepare})

        @block.vector
        def _(dve):
            dve.memset(w.first_rows[:, :], 0.0)
            dve.memset(w.later_rows[:, :], 0.0).then_inc(cleared, 1)
            dve.wait_ge(r.loaded_first, 16 * len(first))
            dve.wait_ge(r.made, made_all)
            vector_first(dve, k, w, r)
            phases(dve, {Attention: vector_attention, Mlp: vector_mlp, Experts: vector_experts, Prepare: vector_prepare})


OUT = (B, S, C)


def kernel(**inputs):
    import numpy as np
    import concourse.bacc as bacc
    from concourse.bass_utils import run_bass_kernel_spmd

    nc = bacc.Bacc("TRN2", target_bir_lowering=False, num_devices=1)
    arrays, aps = {}, {}
    for name, value in inputs.items():
        a = np.ascontiguousarray(value)
        arrays[f"in_{name}"] = a
        aps[name] = nc.dram_tensor(f"in_{name}", a.shape, mybir.dt.from_np(a.dtype), kind="ExternalInput").ap()
    out = nc.dram_tensor("out", OUT, F32, kind="ExternalOutput").ap()

    def group(prefix):
        return {n[len(prefix):]: ap for n, ap in aps.items() if n.startswith(prefix)}

    network(nc, aps["x"], aps["ctx_512"], aps["g_xattn"], aps["g_ffn"], group("L0_xattn_"), group("L0_ffn_"),
            group("L1_xattn_"), group("L1_ffn_"), out)
    r = run_bass_kernel_spmd(nc, [arrays], core_ids=[0])
    return r.results[0]["out"]
```

```python
from contextlib import ExitStack

import concourse.bass as bass
from concourse import mybir

P = 128
B, S, C = 16, 256, 128
TC, CC = 64, 64
H = 16
SB = S // P
UNITS = H // 2
QUADS = H // 4
EPS = 1e-5
MASKED = -1e30
EXPERTS, HID = 8, 512
W1_COLS = HID + HID // P
MT = 512
MB = MT // P
MSTEPS = B * S // MT
FC = HID // P
RANK, LORA_SCALE = 16, 2.0
QMAX = 127.0
ROUND = 12582912.0
SPACE = 25600

F32 = mybir.dt.float32
BF16 = mybir.dt.bfloat16
I32 = mybir.dt.int32
ALU = mybir.AluOpType
ACT = mybir.ActivationFunctionType
AX = mybir.AxisListType


class Count:

    def __init__(self, sem):
        self.sem, self.n = sem, 0

    def inc(self, ins, by=1):
        ins.then_inc(self.sem, by)
        self.n += by


class Step:

    def __init__(self, n, reg=None, start=0):
        self.n, self.reg, self.start = n, reg, start

    def __add__(self, k):
        return Step(self.n + k, self.reg, self.start)

    @property
    def parity(self):
        return self.n % 2

    def count(self, fn):
        if self.reg is None:
            v = fn(self.n)
            return v if v > 0 else None
        n = self.n + 2 * self.start
        first, slope = fn(n), fn(n + 2) - fn(n)
        assert slope > 0 and fn(n + 4) - fn(n + 2) == slope
        assert first > 0, "a wait below one"
        return self.reg * slope + (first - slope * self.start)

    def row(self, eng):
        return self.n if self.reg is None else eng.snap(self.reg * 2 + self.n)


class Signal:

    def __init__(self, sem, base):
        self.sem, self.base = sem, base

    def due(self, step, fn):
        v = step.count(fn)
        return None if v is None else v + self.base

    def at(self, step, fn):
        v = self.due(step, fn)
        assert v is not None
        return v


def apart(eng, k, step):
    if step.reg is not None:
        eng.sem_inc(k.through)


def pipeline(eng, steps, body):
    for n in range(4):
        body(Step(n))
    with eng.Fori(2, steps // 2 - 1) as i:
        body(Step(0, i, 2))
        body(Step(1, i, 2))
    body(Step(steps - 2))
    body(Step(steps - 1))


class Attention:

    SLOTS = {
        ("self", 1): [["T0+"], ["R0-"], ["Q0+"], ["V0+"], ["Y0-"], [], [], []],
        ("self", 4): [["T0+"], ["Q0+"], ["R0-", "Q1+"], ["R1-", "Q2+"], ["R2-", "Q3+"], ["R3-", "V0+"], ["V1+"], ["Y0-"]],
        ("cross", 1): [["T0+"], ["Q0+"], ["R0-", "V0+"], ["Y0-"]],
        ("cross", 4): [["R0-", "R1-", "T0+"], ["Q0+", "Q1+"], ["R2-", "R3-", "V0+"], ["Q2+", "Q3+", "Y0-"]],
    }

    def __init__(self, k, name, kind, D, mask, src, base, dst, ctx, ctx_norm, w):
        self.name, self.kind, self.D, self.mask = name, kind, D, mask
        self.src, self.base, self.dst, self.ctx, self.ctx_norm = src, base, dst, ctx, ctx_norm
        self.w = w
        self.scale = float(D) ** -0.5
        self.G = H * D // P
        self.HG = H // self.G
        self.T = S if kind == "self" else TC
        self.KC = C if kind == "self" else CC
        self.one_side = kind == "self" and w["q_gain"] is None
        self.nv = 2 if kind == "self" and self.G == 4 else 1
        self.slots = self.SLOTS[(kind, self.G)]
        self.nslots = len(self.slots)
        self.regions = QUADS if self.G == 4 else 1
        self.k = k
        self.weights_ahead, self.loaded_ahead = [], None
        U, G = (UNITS, self.G) if kind == "self" else (4, self.G)
        turned = H if kind == "self" else 4
        copied = H // 2 if kind == "self" else 4
        each = dict(x_in=16, base_in=16, stored=16, stats=1, aggr=1, eps_in=1, rstd=1, wn=1, t_full=1, side=1, qk_full=G,
                    q_ready=G, km_ready=G, v_full=self.nv, v_ready=self.nv, s_full=U, max_ready=U, exp_done=U,
                    tr_full=turned, pt_ready=copied, pv_done=QUADS if kind == "self" else 2, num_saved=self.regions,
                    rden=1, rx=1, r_full=G, ot=G, y_full=1, res=1, biased=1)
        if kind == "self":
            each.update(odd_pt_ready=copied)
        if mask == "after":
            each.update(masked=U)
        if kind == "cross":
            each.update(ctx_in=16)
        if ctx_norm:
            each.update(cstats=1, caggr=1, ceps=1, crstd=1, cn=1)
        self.s = k.signals(each, B)

    def pieces(self, t):
        out = []
        for u, names in enumerate(self.slots):
            for n in names:
                b = t + (1 if n[2] == "+" else -1)
                if 0 <= b < B:
                    out.append((u, n[0], int(n[1]), b))
        return out

    def in_slot(self, step, u):
        at = 5 if step.reg is not None else step.n
        return [(kind, i, step + (b - at)) for (v, kind, i, b) in self.pieces(at) if v == u]

    def before(self, step, u, kind, i):
        at = 5 if step.reg is not None else step.n
        order = [p for t in range(-1, at + 1) for p in self.pieces(t) if self.same_bank(kind, i, p[1], p[2])]
        here = [n for n, p in enumerate(order) if p[1:3] == (kind, i) and p[0] == u][-1]
        if here == 0:
            return None
        _, kind, i, b = order[here - 1]
        return kind, i, b - at

    def bank(self, kind, i):
        if self.kind == "cross" and kind in "QR":
            return self.k.scores[1][:, i % 2 * 512:(i % 2 + 1) * 512]
        return self.k.misc

    def same_bank(self, kind, i, other, j):
        pair = self.kind == "cross" and kind in "QR", self.kind == "cross" and other in "QR"
        return pair == (True, True) and i % 2 == j % 2 or pair == (False, False)

    def emptied(self, kind, i):
        return {
            "T": [("side", 1, 1)],
            "Q": [("q_ready", self.G, i + 1), ("km_ready", self.G, i + 1)],
            "V": [("v_ready", self.nv, i + 1)],
            "R": [("ot", self.G, i + 1)],
            "Y": [("res", 1, 1)],
        }[kind]

    def head(self, n):
        return 4 * (n % 4) + n // 4 if self.G == 1 else n



def sync_attention(sp, a):
    k, s = a.k, a.s

    def load_x(b):
        row = b.row(sp)
        if (due := s["x_in"].due(b, lambda t: 16 * t)) is not None:
            sp.wait_ge(s["x_in"].sem, due)
            apart(sp, k, b)
        if (due := s["wn"].due(b, lambda t: t - 1)) is not None:
            sp.wait_ge(s["wn"].sem, due)
            apart(sp, k, b)
        sp.dma_start(k.x_in[:, b.parity], a.src[row].rearrange("(k p) c -> p k c", p=P)).then_inc(s["x_in"].sem, 16)
        if a.ctx is not None:
            if (due := s["ctx_in"].due(b, lambda t: 16 * t)) is not None:
                sp.wait_ge(s["ctx_in"].sem, due)
                apart(sp, k, b)
            if a.ctx_norm:
                if (due := s["cn"].due(b, lambda t: t - 1)) is not None:
                    sp.wait_ge(s["cn"].sem, due)
                    apart(sp, k, b)
            else:
                if (due := s["t_full"].due(b, lambda t: t - 1)) is not None:
                    sp.wait_ge(s["t_full"].sem, due)
                    apart(sp, k, b)
            sp.dma_start(k.ctx_in[:, b.parity], a.ctx[row]).then_inc(s["ctx_in"].sem, 16)

    def load_base(b):
        row = b.row(sp)
        if (due := s["base_in"].due(b, lambda t: 16 * t)) is not None:
            sp.wait_ge(s["base_in"].sem, due)
            apart(sp, k, b)
        if (due := s["res"].due(b, lambda t: t - 1)) is not None:
            sp.wait_ge(s["res"].sem, due)
            apart(sp, k, b)
        sp.dma_start(k.base_in[:, b.parity], a.base[row].rearrange("(k p) c -> p k c", p=P)).then_inc(s["base_in"].sem, 16)

    def store(b):
        row = b.row(sp)
        if (due := s["stored"].due(b, lambda t: 16 * t)) is not None:
            sp.wait_ge(s["stored"].sem, due)
            apart(sp, k, b)
        sp.wait_ge(s["res"].sem, s["res"].at(b, lambda t: t + 1))
        apart(sp, k, b)
        sp.dma_start(a.dst[row].rearrange("(k p) c -> p k c", p=P), k.res[:, b.parity]).then_inc(s["stored"].sem, 16)

    load_x(Step(0))
    load_x(Step(1))

    def body(t):
        if t.n < B - 2 or t.reg is not None:
            load_x(t + 2)
        load_base(t)
        if t.reg is None and t.n < 4:
            for dst, src in a.weights_ahead[t.n::4]:
                sp.dma_start(dst, src).then_inc(a.loaded_ahead, 16)
        if t.n > 0 or t.reg is not None:
            store(t + -1)

    pipeline(sp, B, body)
    store(Step(B - 1))
    sp.wait_ge(s["stored"].sem, s["stored"].base + 16 * B)



def tensor_attention(pe, a):
    k, s, w = a.k, a.s, a.w

    def piece(t, u, kind, i, b):
        bank = a.bank(kind, i)
        was = a.before(t, u, kind, i)
        if was is not None:
            for name, per, n in a.emptied(*was[:2]):
                if (due := s[name].due(t, lambda x: (x + was[2]) * per + n)) is not None:
                    pe.wait_ge(s[name].sem, due)
        if kind == "T":
            if a.ctx_norm:
                pe.wait_ge(s["cn"].sem, s["cn"].at(b, lambda x: x + 1))
            elif a.kind == "cross":
                pe.wait_ge(s["ctx_in"].sem, s["ctx_in"].at(b, lambda x: 16 * (x + 1)))
            pe.wait_ge(s["wn"].sem, s["wn"].at(b, lambda x: x + 1))
            for blk in range(SB):
                last = pe.transpose(bank[:, blk * P:(blk + 1) * P], k.wn[:, b.parity, blk], k.ident[:, :])
            if a.kind == "cross":
                src = k.cn if a.ctx_norm else k.ctx_in
                last = pe.transpose(bank[0:CC, 256:256 + TC], src[:, b.parity], k.ident[0:TC, 0:TC])
            last.then_inc(s["t_full"].sem, 1)
        if kind == "Q":
            pe.wait_ge(s["side"].sem, s["side"].at(b, lambda x: x + 1))
            pe.matmul(bank[:, 0:S], w["wq"][:, i * P:(i + 1) * P], k.xq[:, b.parity], start=True, stop=True)
            keys = k.xq[:, b.parity] if a.one_side else k.xk[:, b.parity] if a.kind == "self" else k.xc[:, b.parity, 0]
            pe.matmul(bank[:, S:S + a.T], w["wk"][:, i * P:(i + 1) * P], keys, start=True, stop=True)\
              .then_inc(s["qk_full"].sem, 1)
        if kind == "V":
            pe.wait_ge(s["side"].sem, s["side"].at(b, lambda x: x + 1))
            keys = k.xq if a.one_side else k.xk
            if a.kind == "cross":
                last = pe.matmul(bank[:, 0:a.G * P], k.xc[:, b.parity].rearrange("c h t -> c (h t)"), w["wv"][:, :],
                                 start=True, stop=True)
            elif a.G == 4:
                last = pe.matmul(bank[:, :], keys[:, b.parity, i * P:(i + 1) * P], w["wv"][:, :], start=True, stop=True)
            else:
                for blk in range(SB):
                    last = pe.matmul(bank[:, blk * P:(blk + 1) * P], keys[:, b.parity, blk * P:(blk + 1) * P],
                                     w["wv"][:, :], start=True, stop=True)
            last.then_inc(s["v_full"].sem, 1)
        if kind == "R":
            pe.wait_ge(s["rx"].sem, s["rx"].at(b, lambda x: x + 1))
            for blk in range(SB):
                last = pe.transpose(bank[:, blk * P:(blk + 1) * P], k.rx[:, blk, i * P:(i + 1) * P], k.ident[:, :])
            last.then_inc(s["r_full"].sem, 1)
        if kind == "Y":
            pe.wait_ge(s["ot"].sem, s["ot"].at(b, lambda x: a.G * (x + 1)))
            for blk in range(SB):
                for g in range(a.G):
                    last = pe.matmul(bank[:, blk * P:(blk + 1) * P], k.ot[:, g, blk * P:(blk + 1) * P],
                                     w["wo"][:, g], start=(g == 0), stop=(g == a.G - 1))
            last.then_inc(s["y_full"].sem, 1)

    def pieces(t, u, reciprocals):
        for kind, i, b in a.in_slot(t, u):
            if (kind == "R") == reciprocals:
                piece(t, u, kind, i, b)

    def self_scores(b, u):
        U = lambda x: UNITS * x + u
        if (due := s["exp_done"].due(b, lambda x: U(x) - 1)) is not None:
            pe.wait_ge(s["exp_done"].sem, due)
        g0 = a.head(2 * u) // a.HG
        pe.wait_ge(s["q_ready"].sem, s["q_ready"].at(b, lambda x: a.G * x + g0 + 1))
        pe.wait_ge(s["km_ready"].sem, s["km_ready"].at(b, lambda x: a.G * x + g0 + 1))
        for n in range(2):
            h = a.head(2 * u + n)
            bank = k.scores[u % 2][:, n * 512:(n + 1) * 512]
            for blk in range(SB):
                q = k.qT[:, b.parity, h // a.HG, blk * P:(blk + 1) * P]
                if a.mask == "before":
                    cols = (0, P) if blk == 0 else (P, 3 * P)
                    pe.matmul(bank[:, cols[0]:cols[1]], q, k.km[:, b.parity, h, 0:cols[1] - cols[0]],
                              start=True, stop=False, skip_group_check=True)
                    last = pe.matmul(bank[:, cols[1] - P:cols[1]], k.identb[:, :], k.above[:, :],
                                     start=False, stop=True, skip_group_check=True)
                else:
                    last = pe.matmul(bank[:, blk * S:(blk + 1) * S], q, k.km[:, b.parity, h], start=True, stop=True)
        last.then_inc(s["s_full"].sem, 1)

    def self_turn(b, u):
        pe.wait_ge(s["masked" if a.mask == "after" else "exp_done"].sem, s["masked" if a.mask == "after" else "exp_done"].at(b, lambda x: UNITS * x + u + 1))
        for n in range(2):
            hd = 2 * u + n
            copied = s["odd_pt_ready" if n else "pt_ready"]
            if (due := copied.due(b, lambda x: H // 2 * x + u)) is not None:
                pe.wait_ge(copied.sem, due)
            blocks = (0, 1, 3) if a.mask == "after" else (0, 1, 2)
            for o, blk in enumerate(blocks):
                last = pe.transpose(k.turned[hd % 2][:, o * P:(o + 1) * P], k.probs[:, u % 2, n, blk * P:(blk + 1) * P],
                                    k.ident[:, :])
            last.then_inc(s["tr_full"].sem, 1)

    def self_values(b, q):
        pe.wait_ge(s["pt_ready"].sem, s["pt_ready"].at(b, lambda x: H // 2 * x + 2 * q + 2))
        pe.wait_ge(s["odd_pt_ready"].sem, s["odd_pt_ready"].at(b, lambda x: H // 2 * x + 2 * q + 2))
        pe.wait_ge(s["v_ready"].sem, s["v_ready"].at(b, lambda x: a.nv * (x + 1)))
        r = a.regions
        reg = q if r > 1 else 0
        if (due := s["num_saved"].due(b, lambda x: r * x + reg)) is not None:
            pe.wait_ge(s["num_saved"].sem, due)
        half = (q % 2 if r > 1 else b.parity) * S
        pt = lambda n, lo, hi: k.pt[:, 4 * (q % 2) + n, lo * P:hi * P]
        first = r > 1 or q == 0
        for part in range(2):
            for n in range(4):
                h = a.head(4 * q + n)
                out = k.num[32 * n:32 * n + 32]
                tb = part if a.mask == "before" else 1 - part
                v = k.val[:, b.parity, tb, 32 * h:32 * h + 32]
                if a.mask == "before":
                    out, p = (out[:, half:half + S], pt(n, 0, 2)) if part == 0 else (out[:, half + P:half + S], pt(n, 2, 3))
                else:
                    out, p = (out[:, half:half + S], pt(n, 1, 3)) if part == 0 else (out[:, half:half + P], pt(n, 0, 1))
                last = pe.matmul(out, v, p, start=(first and part == 0), stop=(part == 1), skip_group_check=True)
        last.then_inc(s["pv_done"].sem, 1)

    def cross_scores(b, c):
        if (due := s["exp_done"].due(b, lambda x: 4 * x + c - 1)) is not None:
            pe.wait_ge(s["exp_done"].sem, due)
        half, blk = c // 2, c % 2
        g1 = min(a.G - 1, 2 * half + 1)
        pe.wait_ge(s["q_ready"].sem, s["q_ready"].at(b, lambda x: a.G * x + g1 + 1))
        pe.wait_ge(s["km_ready"].sem, s["km_ready"].at(b, lambda x: a.G * x + g1 + 1))
        bank = k.scores[0][:, (c % 2) * 512:(c % 2 + 1) * 512]
        for i in range(2 if a.G == 4 else 1):
            g = 2 * half + i if a.G == 4 else 0
            hs = 4 if a.G == 4 else 8
            h0 = 8 * half + hs * i
            last = pe.matmul(bank[:, i * hs * TC:(i + 1) * hs * TC], k.qT[:, b.parity, g, blk * P:(blk + 1) * P],
                             k.km_cross[:, b.parity, h0 * TC:(h0 + hs) * TC], start=True, stop=True)
        last.then_inc(s["s_full"].sem, 1)

    def cross_turn(b, c):
        pe.wait_ge(s["exp_done"].sem, s["exp_done"].at(b, lambda x: 4 * x + c + 1))
        if (due := s["pt_ready"].due(b, lambda x: 4 * x + c - 1)) is not None:
            pe.wait_ge(s["pt_ready"].sem, due)
        for p in range(4):
            last = pe.transpose(k.turned[c % 2][:, p * P:(p + 1) * P], k.pc[:, c % 2, p * P:(p + 1) * P], k.ident[:, :])
        last.then_inc(s["tr_full"].sem, 1)

    def cross_values(b, half):
        pe.wait_ge(s["pt_ready"].sem, s["pt_ready"].at(b, lambda x: 4 * x + 2 * half + 2))
        pe.wait_ge(s["v_ready"].sem, s["v_ready"].at(b, lambda x: x + 1))
        if a.G == 4:
            if (due := s["num_saved"].due(b, lambda x: 4 * x + 2 * half)) is not None:
                pe.wait_ge(s["num_saved"].sem, due)
            for g in range(2):
                for p in range(2):
                    pair = 4 * half + 2 * g + p
                    last = pe.matmul(k.num[:, g * S:(g + 1) * S], k.vb[:, b.parity, pair], k.ptc[:, half, 2 * g + p],
                                     start=(p == 0), stop=(p == 1), skip_group_check=True)
        else:
            if (due := s["num_saved"].due(b, lambda x: x)) is not None:
                pe.wait_ge(s["num_saved"].sem, due)
            for p in range(4):
                last = pe.matmul(k.num[:, b.parity * S:(b.parity + 1) * S], k.vb[:, b.parity, 4 * half + p],
                                 k.ptc[:, half, p], start=(half == 0 and p == 0), stop=(half == 1 and p == 3),
                                 skip_group_check=True)
        last.then_inc(s["pv_done"].sem, 1)

    for _, kind, i, b in a.pieces(-1):
        piece(Step(-1), _, kind, i, Step(b))
    scores, turn, values = ((self_scores, self_turn, self_values) if a.kind == "self" else
                            (cross_scores, cross_turn, cross_values))
    n = a.nslots
    for u in range(2):
        scores(Step(0), u)

    def body(t):
        last = t.reg is None and t.n == B - 1
        first = t.reg is None and t.n == 0
        for u in range(n):
            turn(t, u)
            if a.kind == "cross":
                pieces(t, u, True)
                pieces(t, u, False)
            if u + 2 < n:
                scores(t, u + 2)
            elif not last:
                scores(t + 1, u + 2 - n)
            if a.kind == "self":
                pieces(t, u, True)
            if u % 2 == 0 and not (first and u == 0):
                values(t + (-1 if u == 0 else 0), (u // 2 - 1) % (n // 2))
            if a.kind == "self":
                pieces(t, u, False)

    pipeline(pe, B, body)
    values(Step(B - 1), n // 2 - 1)
    for u in range(n):
        pieces(Step(B), u, True)
        pieces(Step(B), u, False)



def scalar_attention(act, a):
    k, s, w = a.k, a.s, a.w

    def piece(kind, i, b):
        bank = a.bank(kind, i)
        if kind == "Q":
            act.wait_ge(s["qk_full"].sem, s["qk_full"].at(b, lambda x: a.G * x + i + 1))
            last_use = (lambda x: UNITS * (x - 1)) if a.kind == "self" else (lambda x: 4 * (x - 1))
            if (due := s["s_full"].due(b, last_use)) is not None:
                act.wait_ge(s["s_full"].sem, due)
            if a.kind == "self":
                act.wait_ge(s["km_ready"].sem, s["km_ready"].at(b, lambda x: a.G * x + i + 1))
            act.activation(k.qT[:, b.parity, i], bank[:, 0:S], ACT.Identity, bias=w["q_bias"] if w["q_bias"] is not None else 0.0,
                           scale=a.scale).then_inc(s["q_ready"].sem, 1)
        if kind == "V" and a.kind == "self" and a.G == 4:
            act.wait_ge(s["v_full"].sem, s["v_full"].at(b, lambda x: 2 * x + i + 1))
            if (due := s["pv_done"].due(b, lambda x: QUADS * (x - 1))) is not None:
                act.wait_ge(s["pv_done"].sem, due)
            act.copy(k.val[:, b.parity, i], bank[:, :]).then_inc(s["v_ready"].sem, 1)

    def self_exp(b, u):
        act.wait_ge(s["max_ready"].sem, s["max_ready"].at(b, lambda x: UNITS * x + u + 1))
        if (due := s["tr_full"].due(b, lambda x: H * x + 2 * (u - 1))) is not None:
            act.wait_ge(s["tr_full"].sem, due)
        if (due := s["rden"].due(b, lambda x: x - 1)) is not None:
            act.wait_ge(s["rden"].sem, due)
        for n in range(2):
            h = a.head(2 * u + n)
            for blk in range(SB):
                if a.mask == "before":
                    lo, hi = (0, P) if blk == 0 else (P, 3 * P)
                else:
                    lo, hi = blk * S, (blk + 1) * S
                last = act.activation(k.probs[:, u % 2, n, lo:hi], k.scores[u % 2][:, n * 512 + lo:n * 512 + hi], ACT.Exp,
                                      bias=k.nmax[:, u % 2, 2 * n + blk:2 * n + blk + 1], scale=1.0,
                                      accum_out=k.sums[:, b.parity, blk, h:h + 1])
        last.then_inc(s["exp_done"].sem, 1)

    def self_copy(b, u):
        act.wait_ge(s["tr_full"].sem, s["tr_full"].at(b, lambda x: H * x + 2 * u + 2))
        if (due := s["pv_done"].due(b, lambda x: QUADS * x + u // 2 - 1)) is not None:
            act.wait_ge(s["pv_done"].sem, due)
        act.copy(k.pt[:, (2 * u + 1) % 8], k.turned[1][:, 0:3 * P]).then_inc(s["odd_pt_ready"].sem, 1)

    def cross_exp(b, c):
        act.wait_ge(s["max_ready"].sem, s["max_ready"].at(b, lambda x: 4 * x + c + 1))
        if (due := s["tr_full"].due(b, lambda x: 4 * x + c - 1)) is not None:
            act.wait_ge(s["tr_full"].sem, due)
        if (due := s["rden"].due(b, lambda x: x - 1)) is not None:
            act.wait_ge(s["rden"].sem, due)
        for h in range(8):
            at = c % 2 * 512 + h * TC
            last = act.activation(k.pc[:, c % 2, h * TC:(h + 1) * TC], k.scores[0][:, at:at + TC], ACT.Exp,
                                  bias=k.cmax[:, c % 2, h:h + 1], scale=1.0,
                                  accum_out=k.sums[:, b.parity, c % 2, 8 * (c // 2) + h:8 * (c // 2) + h + 1])
        last.then_inc(s["exp_done"].sem, 1)

    def save(b, q):
        if a.regions > 1:
            n, per = (1, 4) if a.kind == "self" else (2, 2)
            act.wait_ge(s["pv_done"].sem, s["pv_done"].at(b, lambda x: per * x + q + 1))
            if (due := s["ot"].due(b, lambda x: 4 * (x - 1))) is not None:
                act.wait_ge(s["ot"].sem, due)
            half = (q % 2) * S if a.kind == "self" else 0
            act.copy(k.numS[:, b.parity, n * q:n * (q + 1)], k.num[:, half:half + n * S].rearrange("p (g t) -> p g t", g=n))\
               .then_inc(s["num_saved"].sem, n)
        elif q == (3 if a.kind == "self" else 1):
            act.wait_ge(s["pv_done"].sem, s["pv_done"].at(b, lambda x: (q + 1) * (x + 1)))
            if (due := s["ot"].due(b, lambda x: x - 1)) is not None:
                act.wait_ge(s["ot"].sem, due)
            act.copy(k.numS[:, b.parity, 0], k.num[:, b.parity * S:(b.parity + 1) * S]).then_inc(s["num_saved"].sem, 1)

    exps = self_exp if a.kind == "self" else cross_exp
    n = a.nslots
    for _, kind, i, b in a.pieces(-1):
        piece(kind, i, Step(b))
    for u in range(2):
        exps(Step(0), u)

    def body(t):
        last = t.reg is None and t.n == B - 1
        first = t.reg is None and t.n == 0
        for u in range(n):
            if a.kind == "self":
                self_copy(t, u)
            if a.kind == "cross":
                for kind, i, b in a.in_slot(t, u):
                    piece(kind, i, b)
            if u + 2 < n:
                exps(t, u + 2)
            elif not last:
                exps(t + 1, u + 2 - n)
            if u % 2 == 0 and not (first and u == 0):
                save(t + (-1 if u == 0 else 0), (u // 2 - 1) % (n // 2))
            if a.kind == "self":
                for kind, i, b in a.in_slot(t, u):
                    piece(kind, i, b)

    pipeline(act, B, body)
    save(Step(B - 1), n // 2 - 1)
    for u in range(n):
        for kind, i, b in a.in_slot(Step(B), u):
            piece(kind, i, b)



def vector_norm_stats(dve, k, s, x, stats, aggr, names, b, blocks):
    for blk in range(blocks):
        last = dve.bn_stats(stats[:, blk], x[:, blk])
    last.then_inc(s[names[0]].sem, 1)
    dve.wait_ge(s[names[0]].sem, s[names[0]].at(b, lambda t: t + 1))
    apart(dve, k, b)
    for blk in range(blocks):
        last = dve.bn_aggr(aggr[:, blk], stats[:, blk])
    last.then_inc(s[names[1]].sem, 1)


def vector_attention(dve, a):
    k, s, w = a.k, a.s, a.w

    def norm_stats(b):
        dve.wait_ge(s["x_in"].sem, s["x_in"].at(b, lambda t: 16 * (t + 1)))
        vector_norm_stats(dve, k, s, k.x_in[:, b.parity], k.stats[:, b.parity], k.aggr[:, b.parity], ("stats", "aggr"), b, SB)
        if a.ctx_norm:
            dve.wait_ge(s["ctx_in"].sem, s["ctx_in"].at(b, lambda t: 16 * (t + 1)))
            vector_norm_stats(dve, k, s, k.ctx_in[:, b.parity].unsqueeze(1), k.cstats[:, b.parity], k.caggr[:, b.parity],
                              ("cstats", "caggr"), b, 1)

    def norm(b):
        dve.wait_ge(s["rstd"].sem, s["rstd"].at(b, lambda t: t + 1))
        if (due := s["t_full"].due(b, lambda t: t - 1)) is not None:
            dve.wait_ge(s["t_full"].sem, due)
        for blk in range(SB):
            last = dve.tensor_scalar(k.wn[:, b.parity, blk], k.x_in[:, b.parity, blk], k.aggr[:, b.parity, blk, 0:1],
                                     k.rstd[:, b.parity, blk:blk + 1], ALU.subtract, ALU.mult)
        last.then_inc(s["wn"].sem, 1)
        if a.ctx_norm:
            dve.wait_ge(s["crstd"].sem, s["crstd"].at(b, lambda t: t + 1))
            dve.tensor_scalar(k.cn[:, b.parity], k.ctx_in[:, b.parity], k.caggr[:, b.parity, 0, 0:1],
                              k.crstd[:, b.parity, 0:1], ALU.subtract, ALU.mult).then_inc(s["cn"].sem, 1)

    def piece(kind, i, b):
        bank = a.bank(kind, i)
        if kind == "T":
            dve.wait_ge(s["t_full"].sem, s["t_full"].at(b, lambda x: x + 1))
            if (due := s["qk_full"].due(b, lambda x: a.G * (x - 1))) is not None:
                dve.wait_ge(s["qk_full"].sem, due)
            if (due := s["v_full"].due(b, lambda x: a.nv * (x - 1))) is not None:
                dve.wait_ge(s["v_full"].sem, due)
            if w["q_gain"] is None:
                last = dve.tensor_copy(k.xq[:, b.parity], bank[:, 0:S])
            else:
                last = dve.tensor_scalar(k.xq[:, b.parity], bank[:, 0:S], w["q_gain"], w["q_shift"], ALU.mult, ALU.add)
            if a.kind == "self" and not a.one_side:
                last = dve.tensor_scalar(k.xk[:, b.parity], bank[:, 0:S], w["k_gain"], w["k_shift"], ALU.mult, ALU.add)
            if a.kind == "cross":
                both = bank[0:CC, S:S + TC].unsqueeze(1).to_broadcast([CC, 2, TC])
                if w["k_gain"] is None:
                    last = dve.tensor_copy(k.xc[:, b.parity], both)
                else:
                    last = dve.tensor_scalar(k.xc[:, b.parity], both, w["k_gain"], w["k_shift"], ALU.mult, ALU.add)
            last.then_inc(s["side"].sem, 1)
        if kind == "Q":
            if a.kind == "cross":
                dve.wait_ge(s["q_ready"].sem, s["q_ready"].at(b, lambda x: a.G * x + i + 1))
            dve.wait_ge(s["qk_full"].sem, s["qk_full"].at(b, lambda x: a.G * x + i + 1))
            last_use = (lambda x: UNITS * (x - 1)) if a.kind == "self" else (lambda x: 4 * (x - 1))
            if (due := s["s_full"].due(b, last_use)) is not None:
                dve.wait_ge(s["s_full"].sem, due)
            n = min(a.HG, 1024 // a.T)
            for j in range(0, a.HG, n):
                h0 = a.HG * i + j
                out = (k.km[:, b.parity, h0:h0 + n] if a.kind == "self" else
                       k.km_cross[:, b.parity, h0 * TC:(h0 + n) * TC].rearrange("p (h t) -> p h t", t=TC))
                keys = bank[:, S:S + a.T].unsqueeze(1).to_broadcast([P, n, a.T])
                own = w["own"][:, j:j + n].unsqueeze(2).to_broadcast([P, n, a.T])
                if w["k_bias"] is None:
                    last = dve.tensor_tensor(out, keys, own, ALU.mult)
                else:
                    last = dve.scalar_tensor_tensor(out=out, in0=keys, scalar=w["k_bias"], in1=own, op0=ALU.add, op1=ALU.mult)
            last.then_inc(s["km_ready"].sem, 1)
        if kind == "V" and a.kind == "self" and a.G == 1:
            dve.wait_ge(s["v_full"].sem, s["v_full"].at(b, lambda x: x + 1))
            if (due := s["pv_done"].due(b, lambda x: QUADS * (x - 1))) is not None:
                dve.wait_ge(s["pv_done"].sem, due)
            for blk in range(SB):
                last = dve.tensor_tensor(
                    k.val[:, b.parity, blk].rearrange("p (r j c) -> p r j c", r=4, c=32),
                    bank[:, blk * P:(blk + 1) * P].rearrange("p (r c) -> p r c", r=4).unsqueeze(2).to_broadcast([P, 4, 4, 32]),
                    k.own_columns[:, :, :].unsqueeze(1).to_broadcast([P, 4, 4, 32]), ALU.mult)
            last.then_inc(s["v_ready"].sem, 1)
        if kind == "V" and a.kind == "cross":
            dve.wait_ge(s["v_full"].sem, s["v_full"].at(b, lambda x: x + 1))
            if (due := s["pv_done"].due(b, lambda x: 2 * (x - 1))) is not None:
                dve.wait_ge(s["pv_done"].sem, due)
            if a.G == 1:
                last = dve.tensor_tensor(k.vb[:, b.parity], bank[:, 0:P].unsqueeze(1).to_broadcast([P, 8, P]),
                                         w["own_pair"], ALU.mult)
            else:
                last = dve.tensor_tensor(k.vb[:, b.parity].rearrange("p (g j) c -> p g j c", g=4),
                                         bank[:, :].rearrange("p (g c) -> p g c", g=4).unsqueeze(2).to_broadcast([P, 4, 2, P]),
                                         w["own_pair"].rearrange("p (g j) c -> p g j c", g=4), ALU.mult)
            last.then_inc(s["v_ready"].sem, 1)
        if kind == "R":
            dve.wait_ge(s["r_full"].sem, s["r_full"].at(b, lambda x: a.G * x + i + 1))
            if (due := s["num_saved"].due(b, lambda x: a.regions * x + min(i, a.regions - 1) + 1)) is not None:
                dve.wait_ge(s["num_saved"].sem, due)
            if (due := s["y_full"].due(b, lambda x: x)) is not None:
                dve.wait_ge(s["y_full"].sem, due)
            dve.tensor_tensor(k.ot[:, i], bank[:, 0:S], k.numS[:, b.parity, i], ALU.mult).then_inc(s["ot"].sem, 1)
        if kind == "Y":
            dve.wait_ge(s["y_full"].sem, s["y_full"].at(b, lambda x: x + 1))
            dve.wait_ge(s["biased"].sem, s["biased"].at(b, lambda x: x + 1))
            if (due := s["stored"].due(b, lambda x: 16 * (x - 1))) is not None:
                dve.wait_ge(s["stored"].sem, due)
            dve.tensor_tensor(k.res[:, b.parity].rearrange("p k c -> p (k c)"), bank[:, 0:S],
                              k.base_sum[:, b.parity].rearrange("p k c -> p (k c)"), ALU.add).then_inc(s["res"].sem, 1)

    def self_max(b, u):
        dve.wait_ge(s["s_full"].sem, s["s_full"].at(b, lambda x: UNITS * x + u + 1))
        if (due := s["exp_done"].due(b, lambda x: UNITS * x + u - 1)) is not None:
            dve.wait_ge(s["exp_done"].sem, due)
        bank = k.scores[u % 2][:, :].rearrange("p (n t) -> p n t", n=2)
        out = k.nmax[:, u % 2].rearrange("p (n k) -> p n k", n=2)
        if a.mask == "before":
            dve.tensor_reduce(out[:, :, 0:1], bank[:, :, 0:P], AX.X, ALU.max, negate=True)
            last = dve.tensor_reduce(out[:, :, 1:2], bank[:, :, P:3 * P], AX.X, ALU.max, negate=True)
        else:
            last = dve.tensor_reduce(k.nmax[:, u % 2], k.scores[u % 2][:, :].rearrange("p (n t) -> p n t", n=4),
                                     AX.X, ALU.max, negate=True)
        last.then_inc(s["max_ready"].sem, 1)

    def self_copy(b, u):
        dve.wait_ge(s["tr_full"].sem, s["tr_full"].at(b, lambda x: H * x + 2 * u + 1))
        if (due := s["pv_done"].due(b, lambda x: QUADS * x + u // 2 - 1)) is not None:
            dve.wait_ge(s["pv_done"].sem, due)
        dve.tensor_copy(k.pt[:, 2 * u % 8], k.turned[0][:, 0:3 * P]).then_inc(s["pt_ready"].sem, 1)

    def cross_max(b, c):
        dve.wait_ge(s["s_full"].sem, s["s_full"].at(b, lambda x: 4 * x + c + 1))
        if (due := s["exp_done"].due(b, lambda x: 4 * x + c - 1)) is not None:
            dve.wait_ge(s["exp_done"].sem, due)
        scores = k.scores[0][:, (c % 2) * 512:(c % 2 + 1) * 512].rearrange("p (h t) -> p h t", t=TC)
        dve.tensor_reduce(k.cmax[:, c % 2], scores, AX.X, ALU.max, negate=True).then_inc(s["max_ready"].sem, 1)

    def cross_copy(b, c):
        dve.wait_ge(s["tr_full"].sem, s["tr_full"].at(b, lambda x: 4 * x + c + 1))
        if (due := s["pv_done"].due(b, lambda x: 2 * (x - 1) + c // 2 + 1)) is not None:
            dve.wait_ge(s["pv_done"].sem, due)
        dve.tensor_copy(k.ptc[:, c // 2, :, (c % 2) * P:(c % 2 + 1) * P],
                        k.turned[c % 2][:, :].rearrange("p (j t) -> p j t", j=4)).then_inc(s["pt_ready"].sem, 1)

    def reciprocals(b):
        dve.wait_ge(s["exp_done"].sem, s["exp_done"].at(b, lambda x: a.nslots * (x + 1)))
        dve.reciprocal(k.rsum[:, b.parity], k.sums[:, b.parity]).then_inc(s["rden"].sem, 1)
        dve.wait_ge(s["rden"].sem, s["rden"].at(b, lambda x: x + 1))
        if (due := s["r_full"].due(b, lambda x: a.G * x)) is not None:
            dve.wait_ge(s["r_full"].sem, due)
        for blk in range(SB):
            last = dve.tensor_copy(k.rx[:, blk, 0:H * a.D].rearrange("p (h d) -> p h d", d=a.D),
                                   k.rsum[:, b.parity, blk].unsqueeze(2).to_broadcast([P, H, a.D]))
        last.then_inc(s["rx"].sem, 1)

    exists = lambda t, ahead: t.reg is not None or t.n + ahead < B
    for b in range(2):
        norm_stats(Step(b))
        norm(Step(b))
    for _, kind, i, b in a.pieces(-1):
        piece(kind, i, Step(b))
    top = self_max if a.kind == "self" else cross_max
    for u in range(2):
        top(Step(0), u)

    def body(t):
        n = a.nslots
        for u in range(n):
            if a.kind == "self":
                self_copy(t, u)
            else:
                cross_copy(t, u)
            for kind, i, b in a.in_slot(t, u):
                if kind == "R" or a.kind == "cross":
                    piece(kind, i, b)
            if u + 2 < n or exists(t, 1):
                b, v = (t, u + 2) if u + 2 < n else (t + 1, u + 2 - n)
                top(b, v)
            for kind, i, b in a.in_slot(t, u):
                if kind != "R" and a.kind == "self":
                    piece(kind, i, b)
            if u == n - 2 and exists(t, 2):
                norm_stats(t + 2)
            if u == n - 1:
                reciprocals(t)
                if exists(t, 2):
                    norm(t + 2)

    pipeline(dve, B, body)
    for u in range(a.nslots):
        for kind, i, b in a.in_slot(Step(B), u):
            piece(kind, i, b)



def gpsimd_attention(pool, a):
    k, s, w = a.k, a.s, a.w

    def rstd(b):
        pool.wait_ge(s["aggr"].sem, s["aggr"].at(b, lambda t: t + 1))
        if (due := s["wn"].due(b, lambda t: t - 1)) is not None:
            pool.wait_ge(s["wn"].sem, due)
        pool.tensor_tensor(k.vareps[:, b.parity], k.aggr[:, b.parity, :, 1], k.eps[0:k.vareps.shape[0], 0:k.vareps.shape[2]], ALU.add).then_inc(s["eps_in"].sem, 1)
        pool.wait_ge(s["eps_in"].sem, s["eps_in"].at(b, lambda t: t + 1))
        pool.tensor_tensor(k.rstd[:, b.parity], k.vareps[:, b.parity], k.minus_half[:, 0:SB], ALU.pow).then_inc(s["rstd"].sem, 1)
        if a.ctx_norm:
            pool.wait_ge(s["caggr"].sem, s["caggr"].at(b, lambda t: t + 1))
            if (due := s["cn"].due(b, lambda t: t - 1)) is not None:
                pool.wait_ge(s["cn"].sem, due)
            pool.tensor_tensor(k.cvareps[:, b.parity], k.caggr[:, b.parity, :, 1], k.eps[0:k.cvareps.shape[0], 0:k.cvareps.shape[2]], ALU.add).then_inc(s["ceps"].sem, 1)
            pool.wait_ge(s["ceps"].sem, s["ceps"].at(b, lambda t: t + 1))
            pool.tensor_tensor(k.crstd[:, b.parity], k.cvareps[:, b.parity], k.minus_half[0:TC, 0:1], ALU.pow)\
                .then_inc(s["crstd"].sem, 1)

    def bias(b):
        pool.wait_ge(s["base_in"].sem, s["base_in"].at(b, lambda t: 16 * (t + 1)))
        if (due := s["res"].due(b, lambda t: t - 1)) is not None:
            pool.wait_ge(s["res"].sem, due)
        pool.tensor_tensor(k.base_sum[:, b.parity], k.base_in[:, b.parity],
                           w["o_bias"].unsqueeze(1).to_broadcast([P, SB, C]), ALU.add).then_inc(s["biased"].sem, 1)

    def mask(b, u):
        pool.wait_ge(s["exp_done"].sem, s["exp_done"].at(b, lambda x: UNITS * x + u + 1))
        apart(pool, k, b)
        for n in range(2):
            blocks = k.probs[:, u % 2, n].rearrange("p (q t) -> p q t", t=P)[:, 0:4:3]
            last = pool.affine_select(out=blocks, in_=blocks, compare_op=ALU.is_ge, fill=0.0, base=-1,
                                      pattern=[[0, 2], [1, P]], channel_multiplier=-1)
        last.then_inc(s["masked"].sem, 1)

    exists = lambda t, ahead: t.reg is not None or t.n + ahead < B
    rstd(Step(0))
    rstd(Step(1))
    if a.mask == "after":
        for u in range(2):
            mask(Step(0), u)

    def body(t):
        n = a.nslots
        bias(t)
        for u in range(n):
            if a.mask == "after" and (u + 2 < n or exists(t, 1)):
                mask(t if u + 2 < n else t + 1, u + 2 if u + 2 < n else u + 2 - n)
            if u == n - 2 and exists(t, 2):
                rstd(t + 2)

    pipeline(pool, B, body)



class Mlp:

    def __init__(self, k, name, src, also, after, dst, keep, start, w):
        self.k, self.name, self.src, self.also, self.after = k, name, src, also, after
        self.dst, self.keep, self.start, self.w = dst, keep, start, w
        each = dict(x_in=16, stored=16, stats=1, aggr=1, eps_in=1, rstd=1, wn=1, t_full=1, xt=1, h_full=FC, gelu=FC,
                    y_full=1, biased=1, r=1, out=1)
        if after == "norm":
            each.update(rstats=1, raggr=1, reps=1, rrstd=1, rn=1, gained=1)
        if keep is not None:
            each.update(kept=16)
        if also is not None:
            each.update(both=1, also_in=16)
        if start is not None:
            each.update(start_in=16)
        self.s = k.signals(each, MSTEPS)


def mlp_rows(x, row):
    return x.rearrange("(m n) s c -> m (n s) c", n=MT // S)[row].rearrange("(k p) c -> p k c", p=P)


def sync_mlp(sp, m):
    k, s = m.k, m.s

    def load(t):
        row = t.row(sp)
        if (due := s["x_in"].due(t, lambda x: 16 * x)) is not None:
            sp.wait_ge(s["x_in"].sem, due)
            apart(sp, k, t)
        if (due := s["biased"].due(t, lambda x: x - 1)) is not None:
            sp.wait_ge(s["biased"].sem, due)
            apart(sp, k, t)
        if (due := s["wn"].due(t, lambda x: x - 1)) is not None:
            sp.wait_ge(s["wn"].sem, due)
            apart(sp, k, t)
        sp.dma_start(k.mx[:, t.parity], mlp_rows(m.src, row)).then_inc(s["x_in"].sem, 16)
        if m.also is not None:
            if (due := s["also_in"].due(t, lambda x: 16 * x)) is not None:
                sp.wait_ge(s["also_in"].sem, due)
                apart(sp, k, t)
            sp.dma_start(k.malso[:, t.parity], mlp_rows(m.also, row)).then_inc(s["also_in"].sem, 16)

    def load_start(t):
        row = t.row(sp)
        if (due := s["start_in"].due(t, lambda x: 16 * x)) is not None:
            sp.wait_ge(s["start_in"].sem, due)
            apart(sp, k, t)
        if (due := s["out"].due(t, lambda x: x - 1)) is not None:
            sp.wait_ge(s["out"].sem, due)
            apart(sp, k, t)
        sp.dma_start(k.mstart[:, t.parity], mlp_rows(m.start, row)).then_inc(s["start_in"].sem, 16)

    def store(t):
        row = t.row(sp)
        if m.keep is not None:
            if (due := s["kept"].due(t, lambda x: 16 * x)) is not None:
                sp.wait_ge(s["kept"].sem, due)
                apart(sp, k, t)
            sp.wait_ge(s["r"].sem, s["r"].at(t, lambda x: x + 1))
            apart(sp, k, t)
            sp.dma_start(mlp_rows(m.keep, row), k.mr[:, t.parity]).then_inc(s["kept"].sem, 16)
        if (due := s["stored"].due(t, lambda x: 16 * x)) is not None:
            sp.wait_ge(s["stored"].sem, due)
            apart(sp, k, t)
        sp.wait_ge(s["out"].sem, s["out"].at(t, lambda x: x + 1))
        apart(sp, k, t)
        sp.dma_start(mlp_rows(m.dst, row), k.mout[:, t.parity]).then_inc(s["stored"].sem, 16)

    load(Step(0))
    load(Step(1))

    def body(t):
        if m.start is not None:
            load_start(t)
        if t.reg is not None or t.n + 2 < MSTEPS:
            load(t + 2)
        if t.reg is not None or t.n > 0:
            store(t + -1)

    pipeline(sp, MSTEPS, body)
    store(Step(MSTEPS - 1))
    if m.keep is not None:
        sp.wait_ge(s["kept"].sem, s["kept"].base + 16 * MSTEPS)
    sp.wait_ge(s["stored"].sem, s["stored"].base + 16 * MSTEPS)


def tensor_mlp(pe, m):
    k, s, w = m.k, m.s, m.w

    def turn(t):
        pe.wait_ge(s["wn"].sem, s["wn"].at(t, lambda x: x + 1))
        if (due := s["xt"].due(t, lambda x: x)) is not None:
            pe.wait_ge(s["xt"].sem, due)
        for blk in range(MB):
            last = pe.transpose(k.misc[:, blk * P:(blk + 1) * P], k.mwn[:, t.parity, blk], k.ident[:, :])
        last.then_inc(s["t_full"].sem, 1)

    def body(t):
        pe.wait_ge(s["xt"].sem, s["xt"].at(t, lambda x: x + 1))
        for f in range(FC):
            if (due := s["gelu"].due(t, lambda x: FC * (x - 1) + f + 1)) is not None:
                pe.wait_ge(s["gelu"].sem, due)
            pe.matmul(k.scores[f // 2][:, (f % 2) * 512:(f % 2 + 1) * 512], w["w1"][:, f * P:(f + 1) * P], k.mxt[:, t.parity],
                      start=True, stop=True).then_inc(s["h_full"].sem, 1)
        if t.reg is not None or t.n + 1 < MSTEPS:
            turn(t + 1)
        if (due := s["r"].due(t, lambda x: x - 1)) is not None:
            pe.wait_ge(s["r"].sem, due)
        for blk in range(MB):
            for f in range(FC):
                if blk == 0:
                    pe.wait_ge(s["gelu"].sem, s["gelu"].at(t, lambda x: FC * x + f + 1))
                last = pe.matmul(k.turned[t.parity][:, blk * P:(blk + 1) * P], k.mh[:, t.parity, f, blk * P:(blk + 1) * P],
                                 w["w2"][:, f], start=(f == 0), stop=(f == FC - 1))
        last.then_inc(s["y_full"].sem, 1)

    turn(Step(0))
    pipeline(pe, MSTEPS, body)


def scalar_mlp(act, m):
    k, s, w = m.k, m.s, m.w

    def body(t):
        if (due := s["y_full"].due(t, lambda x: x - 1)) is not None:
            act.wait_ge(s["y_full"].sem, due)
        for f in range(FC):
            act.wait_ge(s["h_full"].sem, s["h_full"].at(t, lambda x: FC * x + f + 1))
            act.activation(k.mh[:, t.parity, f], k.scores[f // 2][:, (f % 2) * 512:(f % 2 + 1) * 512], ACT.Gelu,
                           bias=w["b1"][:, f:f + 1], scale=1.0).then_inc(s["gelu"].sem, 1)

    pipeline(act, MSTEPS, body)


def vector_mlp(dve, m):
    k, s, w = m.k, m.s, m.w

    def norm_stats(t):
        dve.wait_ge(s["x_in"].sem, s["x_in"].at(t, lambda x: 16 * (x + 1)))
        vector_norm_stats(dve, k, s, k.mx[:, t.parity], k.mstats[:, t.parity], k.maggr[:, t.parity], ("stats", "aggr"), t, MB)

    def norm(t):
        dve.wait_ge(s["rstd"].sem, s["rstd"].at(t, lambda x: x + 1))
        if (due := s["t_full"].due(t, lambda x: x - 1)) is not None:
            dve.wait_ge(s["t_full"].sem, due)
        for blk in range(MB):
            last = dve.tensor_scalar(k.mwn[:, t.parity, blk], k.mx[:, t.parity, blk], k.maggr[:, t.parity, blk, 0:1],
                                     k.mrstd[:, t.parity, blk:blk + 1], ALU.subtract, ALU.mult)
        last.then_inc(s["wn"].sem, 1)

    def gain(t):
        dve.wait_ge(s["t_full"].sem, s["t_full"].at(t, lambda x: x + 1))
        if (due := s["h_full"].due(t, lambda x: FC * (x - 1))) is not None:
            dve.wait_ge(s["h_full"].sem, due)
        if w["gain"] is None:
            last = dve.tensor_copy(k.mxt[:, t.parity], k.misc[:, :])
        else:
            last = dve.tensor_scalar(k.mxt[:, t.parity], k.misc[:, :], w["gain"], w["shift"], ALU.mult, ALU.add)
        last.then_inc(s["xt"].sem, 1)

    def finish(t):
        dve.wait_ge(s["y_full"].sem, s["y_full"].at(t, lambda x: x + 1))
        dve.wait_ge(s["biased"].sem, s["biased"].at(t, lambda x: x + 1))
        if m.keep is not None:
            if (due := s["kept"].due(t, lambda x: 16 * (x - 1))) is not None:
                dve.wait_ge(s["kept"].sem, due)
        if m.after == "norm":
            if (due := s["rn"].due(t, lambda x: x - 1)) is not None:
                dve.wait_ge(s["rn"].sem, due)
        else:
            if (due := s["out"].due(t, lambda x: x - 1)) is not None:
                dve.wait_ge(s["out"].sem, due)
        dve.tensor_tensor(k.mr[:, t.parity].rearrange("p k c -> p (k c)"), k.turned[t.parity][:, :],
                          k.msum[:, t.parity].rearrange("p k c -> p (k c)"), ALU.add).then_inc(s["r"].sem, 1)
        dve.wait_ge(s["r"].sem, s["r"].at(t, lambda x: x + 1))
        if m.after == "norm":
            vector_norm_stats(dve, k, s, k.mr[:, t.parity], k.mrstats[:, t.parity], k.mraggr[:, t.parity],
                              ("rstats", "raggr"), t, MB)
        else:
            dve.wait_ge(s["start_in"].sem, s["start_in"].at(t, lambda x: 16 * (x + 1)))
            if (due := s["stored"].due(t, lambda x: 16 * (x - 1))) is not None:
                dve.wait_ge(s["stored"].sem, due)
            dve.scalar_tensor_tensor(out=k.mout[:, t.parity].rearrange("p k c -> p (k c)"),
                                     in0=k.mr[:, t.parity].rearrange("p k c -> p (k c)"), scalar=w["gate"],
                                     in1=k.mstart[:, t.parity].rearrange("p k c -> p (k c)"), op0=ALU.mult, op1=ALU.add)\
               .then_inc(s["out"].sem, 1)

    def normed(t):
        dve.wait_ge(s["rrstd"].sem, s["rrstd"].at(t, lambda x: x + 1))
        if (due := s["gained"].due(t, lambda x: x - 1)) is not None:
            dve.wait_ge(s["gained"].sem, due)
        for blk in range(MB):
            last = dve.tensor_scalar(k.mrn[:, t.parity, blk], k.mr[:, t.parity, blk], k.mraggr[:, t.parity, blk, 0:1],
                                     k.mrrstd[:, t.parity, blk:blk + 1], ALU.subtract, ALU.mult)
        last.then_inc(s["rn"].sem, 1)

    for b in range(2):
        norm_stats(Step(b))
        norm(Step(b))
    gain(Step(0))

    def body(t):
        if t.reg is not None or t.n + 2 < MSTEPS:
            norm_stats(t + 2)
        if t.reg is not None or t.n + 1 < MSTEPS:
            gain(t + 1)
        if t.reg is not None or t.n + 2 < MSTEPS:
            norm(t + 2)
        if m.after == "norm" and (t.reg is not None or t.n > 0):
            normed(t + -1)
        finish(t)

    pipeline(dve, MSTEPS, body)
    if m.after == "norm":
        normed(Step(MSTEPS - 1))


def gpsimd_mlp(pool, m):
    k, s, w = m.k, m.s, m.w

    def power(aggr, eps, out, names, t):
        pool.wait_ge(s[names[0]].sem, s[names[0]].at(t, lambda x: x + 1))
        if (due := s[names[3]].due(t, lambda x: x - 1)) is not None:
            pool.wait_ge(s[names[3]].sem, due)
        pool.tensor_tensor(eps[:, t.parity], aggr[:, t.parity, :, 1], k.eps[:, 0:MB], ALU.add).then_inc(s[names[1]].sem, 1)
        pool.wait_ge(s[names[1]].sem, s[names[1]].at(t, lambda x: x + 1))
        pool.tensor_tensor(out[:, t.parity], eps[:, t.parity], k.minus_half[:, 0:MB], ALU.pow).then_inc(s[names[2]].sem, 1)

    def rstd(t):
        power(k.maggr, k.meps, k.mrstd, ("aggr", "eps_in", "rstd", "wn"), t)

    def bias(t):
        pool.wait_ge(s["x_in"].sem, s["x_in"].at(t, lambda x: 16 * (x + 1)))
        if (due := s["r"].due(t, lambda x: x - 1)) is not None:
            pool.wait_ge(s["r"].sem, due)
        x = k.mx[:, t.parity]
        if m.also is not None:
            pool.wait_ge(s["also_in"].sem, s["also_in"].at(t, lambda x: 16 * (x + 1)))
            pool.tensor_tensor(k.mboth[:, t.parity], x, k.malso[:, t.parity], ALU.add).then_inc(s["both"].sem, 1)
            pool.wait_ge(s["both"].sem, s["both"].at(t, lambda x: x + 1))
            x = k.mboth[:, t.parity]
        pool.tensor_tensor(k.msum[:, t.parity], x, w["bias"].unsqueeze(1).to_broadcast([P, MB, C]), ALU.add)\
            .then_inc(s["biased"].sem, 1)

    def after(t):
        power(k.mraggr, k.mreps, k.mrrstd, ("raggr", "reps", "rrstd", "rn"), t)

    def gains(t):
        pool.wait_ge(s["rn"].sem, s["rn"].at(t, lambda x: x + 1))
        if (due := s["out"].due(t, lambda x: x - 1)) is not None:
            pool.wait_ge(s["out"].sem, due)
        if (due := s["stored"].due(t, lambda x: 16 * (x - 1))) is not None:
            pool.wait_ge(s["stored"].sem, due)
        pool.tensor_tensor(k.mrg[:, t.parity], k.mrn[:, t.parity], w["out_gain"].unsqueeze(1).to_broadcast([P, MB, C]),
                           ALU.mult).then_inc(s["gained"].sem, 1)
        pool.wait_ge(s["gained"].sem, s["gained"].at(t, lambda x: x + 1))
        pool.tensor_tensor(k.mout[:, t.parity], k.mrg[:, t.parity], w["out_shift"].unsqueeze(1).to_broadcast([P, MB, C]),
                           ALU.add).then_inc(s["out"].sem, 1)

    rstd(Step(0))
    rstd(Step(1))

    def body(t):
        if t.reg is not None or t.n + 2 < MSTEPS:
            bias(t)
            rstd(t + 2)
        else:
            bias(t)
        if m.after == "norm":
            after(t)
            if t.reg is not None or t.n > 0:
                gains(t + -1)

    pipeline(pool, MSTEPS, body)
    if m.after == "norm":
        gains(Step(MSTEPS - 1))



TILES = B * S // P + EXPERTS
PAIRS = TILES // 2
BLOCKS = B * S // P


class Route:

    def __init__(self, k, src, w):
        self.k, self.src, self.w = k, src, w
        self.s = k.signals(dict(x_in=16, stats=1, aggr=1, eps_in=1, rstd=1, wn=1, t_full=1, xt=1, g_full=1, logits=1,
                                rows_kept=1), MSTEPS)


def sync_route(sp, m):
    k, s = m.k, m.s

    def load(t):
        row = t.row(sp)
        if (due := s["x_in"].due(t, lambda x: 16 * x)) is not None:
            sp.wait_ge(s["x_in"].sem, due)
            apart(sp, k, t)
        if (due := s["wn"].due(t, lambda x: x - 1)) is not None:
            sp.wait_ge(s["wn"].sem, due)
            apart(sp, k, t)
        sp.dma_start(k.mx[:, t.parity], mlp_rows(m.src, row)).then_inc(s["x_in"].sem, 16)

    load(Step(0))
    load(Step(1))

    def body(t):
        if t.reg is not None or t.n + 2 < MSTEPS:
            load(t + 2)

    pipeline(sp, MSTEPS, body)


def tensor_route(pe, m):
    k, s, w = m.k, m.s, m.w

    def body(t):
        pe.wait_ge(s["wn"].sem, s["wn"].at(t, lambda x: x + 1))
        if (due := s["xt"].due(t, lambda x: x)) is not None:
            pe.wait_ge(s["xt"].sem, due)
        for blk in range(MB):
            last = pe.transpose(k.misc[:, blk * P:(blk + 1) * P], k.mwn[:, t.parity, blk], k.ident[:, :])
        last.then_inc(s["t_full"].sem, 1)
        pe.wait_ge(s["xt"].sem, s["xt"].at(t, lambda x: x + 1))
        if (due := s["logits"].due(t, lambda x: x)) is not None:
            pe.wait_ge(s["logits"].sem, due)
        for blk in range(MB):
            last = pe.matmul(k.num[:, blk * EXPERTS:(blk + 1) * EXPERTS], k.mxt[:, t.parity, blk * P:(blk + 1) * P],
                             w["gate_w"], start=True, stop=True)
        last.then_inc(s["g_full"].sem, 1)

    pipeline(pe, MSTEPS, body)


def scalar_route(act, m):
    k, s = m.k, m.s

    def body(t):
        row = t.row(act)
        act.wait_ge(s["wn"].sem, s["wn"].at(t, lambda x: x + 1))
        act.copy(k.rows[:, bass.ds(row, 1)].rearrange("p a n -> p (a n)"), k.mwn[:, t.parity].rearrange("p k c -> p (k c)"))\
           .then_inc(s["rows_kept"].sem, 1)

    pipeline(act, MSTEPS, body)


def vector_route(dve, m):
    k, s, w = m.k, m.s, m.w

    def stats(t):
        dve.wait_ge(s["x_in"].sem, s["x_in"].at(t, lambda x: 16 * (x + 1)))
        vector_norm_stats(dve, k, s, k.mx[:, t.parity], k.mstats[:, t.parity], k.maggr[:, t.parity], ("stats", "aggr"), t, MB)

    def norm(t):
        dve.wait_ge(s["rstd"].sem, s["rstd"].at(t, lambda x: x + 1))
        if (due := s["t_full"].due(t, lambda x: x - 1)) is not None:
            dve.wait_ge(s["t_full"].sem, due)
        if (due := s["rows_kept"].due(t, lambda x: x - 1)) is not None:
            dve.wait_ge(s["rows_kept"].sem, due)
        for blk in range(MB):
            last = dve.tensor_scalar(k.mwn[:, t.parity, blk], k.mx[:, t.parity, blk], k.maggr[:, t.parity, blk, 0:1],
                                     k.mrstd[:, t.parity, blk:blk + 1], ALU.subtract, ALU.mult)
        last.then_inc(s["wn"].sem, 1)

    for n in range(2):
        stats(Step(n))
        norm(Step(n))

    def body(t):
        row = t.row(dve)
        more = t.reg is not None or t.n + 2 < MSTEPS
        if more:
            stats(t + 2)
        dve.wait_ge(s["t_full"].sem, s["t_full"].at(t, lambda x: x + 1))
        if (due := s["g_full"].due(t, lambda x: x - 1)) is not None:
            dve.wait_ge(s["g_full"].sem, due)
        dve.tensor_copy(k.mxt[:, t.parity], k.misc[:, :]).then_inc(s["xt"].sem, 1)
        if more:
            norm(t + 2)
        dve.wait_ge(s["g_full"].sem, s["g_full"].at(t, lambda x: x + 1))
        dve.tensor_tensor(k.logits[:, bass.ds(row, 1)].rearrange("p a n -> p (a n)").rearrange("p (k e) -> p k e", e=EXPERTS),
                          k.num[:, 0:MB * EXPERTS].rearrange("p (k e) -> p k e", e=EXPERTS),
                          w["gate_b"].unsqueeze(1).to_broadcast([P, MB, EXPERTS]), ALU.add).then_inc(s["logits"].sem, 1)

    pipeline(dve, MSTEPS, body)


def gpsimd_route(pool, m):
    k, s = m.k, m.s

    def body(t):
        pool.wait_ge(s["aggr"].sem, s["aggr"].at(t, lambda x: x + 1))
        if (due := s["wn"].due(t, lambda x: x - 1)) is not None:
            pool.wait_ge(s["wn"].sem, due)
        pool.tensor_tensor(k.meps[:, t.parity], k.maggr[:, t.parity, :, 1], k.eps[:, 0:MB], ALU.add)\
            .then_inc(s["eps_in"].sem, 1)
        pool.wait_ge(s["eps_in"].sem, s["eps_in"].at(t, lambda x: x + 1))
        pool.tensor_tensor(k.mrstd[:, t.parity], k.meps[:, t.parity], k.minus_half[:, 0:MB], ALU.pow)\
            .then_inc(s["rstd"].sem, 1)

    pipeline(pool, MSTEPS, body)


class Sort:

    def __init__(self, k, places):
        self.k, self.places = k, places
        self.chosen, self.counted, self.placed, self.scattered = (k.sem(n) for n in ("chosen", "counted", "placed", "scattered"))


def tensor_sort(pe, m):
    k = m.k
    pe.wait_ge(m.chosen, 5)
    pe.matmul(k.num[:, 0:256], k.up_to[:, :], k.chosen, start=True, stop=True)
    pe.matmul(k.num[:, 256:512], k.ones[:, :], k.chosen, start=True, stop=True).then_inc(m.counted, 1)


def vector_sort(dve, m):
    k, E = m.k, EXPERTS
    blocks = lambda x: x.rearrange("p (k e) -> p k e", e=E)
    chosen = Count(m.chosen)

    def choose(ins):
        chosen.inc(ins)
        dve.wait_ge(m.chosen, chosen.n)

    logits = blocks(k.logits.rearrange("p a n -> p (a n)"))
    choose(dve.tensor_reduce(k.best, logits, AX.X, ALU.max))
    choose(dve.tensor_tensor(blocks(k.equal), logits, k.best.unsqueeze(2).to_broadcast([P, BLOCKS, E]), ALU.is_equal))
    choose(dve.tensor_tensor(blocks(k.rank), blocks(k.equal), k.falling[:, :].unsqueeze(1).to_broadcast([P, BLOCKS, E]), ALU.mult))
    choose(dve.tensor_reduce(k.first, blocks(k.rank), AX.X, ALU.max))
    choose(dve.tensor_tensor(blocks(k.chosen), blocks(k.rank), k.first.unsqueeze(2).to_broadcast([P, BLOCKS, E]), ALU.is_equal))
    assert chosen.n == 5
    placed = Count(m.placed)

    def place(ins):
        placed.inc(ins)
        dve.wait_ge(m.placed, placed.n)

    dve.wait_ge(m.counted, 1)
    sums = [k.sums_a, k.sums_b]
    place(dve.tensor_copy(sums[0], k.num[:, 256:512]))
    d, n = 1, 0
    while d < BLOCKS:
        a, b = sums[n % 2], sums[(n + 1) % 2]
        dve.tensor_copy(b[:, 0:d * E], a[:, 0:d * E])
        place(dve.tensor_tensor(b[:, d * E:], a[:, d * E:], a[:, 0:(BLOCKS - d) * E], ALU.add))
        d, n = 2 * d, n + 1
    total = sums[n % 2]
    place(dve.tensor_scalar(k.tiles_x, total[:, (BLOCKS - 1) * E:], (P - 1) / 2, 1.0 / P, ALU.add, ALU.mult))
    place(dve.tensor_scalar(k.tiles, k.tiles_x, ROUND, ROUND, ALU.add, ALU.subtract))
    ends = [k.tiles, k.ends_a, k.ends_b, k.ends_c]
    for n in range(3):
        d, a, b = 1 << n, ends[n], ends[n + 1]
        dve.tensor_copy(b[:, 0:d], a[:, 0:d])
        place(dve.tensor_tensor(b[:, d:], a[:, d:], a[:, 0:E - d], ALU.add))
    place(dve.tensor_tensor(k.ended.rearrange("p (t e) -> p t e", e=E), k.tile_numbers[:, :].unsqueeze(2).to_broadcast([P, TILES, E]),
                            k.ends_c.unsqueeze(1).to_broadcast([P, TILES, E]), ALU.is_ge))
    place(dve.tensor_reduce(k.tile_expert_f, k.ended.rearrange("p (t e) -> p t e", e=E), AX.X, ALU.add))
    place(dve.tensor_scalar(k.tile_expert[:, :], k.tile_expert_f, float(E - 1), None, ALU.min))
    place(dve.tensor_tensor(k.starts, k.ends_c, k.tiles, ALU.subtract))
    place(dve.tensor_scalar(k.start_rows, k.starts, float(P), -1.0, ALU.mult, ALU.add))
    place(dve.tensor_tensor(k.equal, total, k.num[:, 256:512], ALU.subtract))
    place(dve.tensor_tensor(k.rank, k.equal, k.num[:, 0:256], ALU.add))
    place(dve.tensor_tensor(blocks(k.equal), blocks(k.rank), k.start_rows.unsqueeze(1).to_broadcast([P, BLOCKS, E]), ALU.add))
    place(dve.tensor_tensor(k.rank, k.equal, k.chosen, ALU.mult))
    place(dve.tensor_reduce(k.first, blocks(k.rank), AX.X, ALU.add))
    place(dve.tensor_copy(k.place[:, :], k.first))
    assert placed.n == PLACED, placed.n


PLACED = 22


def gpsimd_sort(pool, m):
    k = m.k
    rows = k.rows.rearrange("p a n -> p (a n)")
    pool.wait_ge(m.placed, PLACED)
    for j in range(BLOCKS):
        pool.indirect_dma_start(m.places, bass.IndirectOffsetOnAxis(ap=k.place[:, j:j + 1], axis=0), rows[:, j * P:(j + 1) * P], None)\
            .then_inc(m.scattered, 16)
    pool.wait_ge(m.scattered, 16 * BLOCKS)


class Tiles:

    def __init__(self, k, src, dst, w):
        self.k, self.src, self.dst, self.w = k, src, dst, w
        self.s = k.signals(dict(x_in=16, stored=16, t_full=1, xt=1, w1_in=2, h_full=2, relu_scalar=2, relu_vector=2, y_full=1, out=1), PAIRS)


def sync_tiles(sp, m):
    k, s = m.k, m.s

    def load(t):
        row = t.row(sp)
        if (due := s["x_in"].due(t, lambda x: 16 * x)) is not None:
            sp.wait_ge(s["x_in"].sem, due)
            apart(sp, k, t)
        if (due := s["t_full"].due(t, lambda x: x - 1)) is not None:
            sp.wait_ge(s["t_full"].sem, due)
            apart(sp, k, t)
        sp.dma_start(k.tx[:, t.parity], m.src.rearrange("(t n p) c -> t p n c", n=2, p=P)[row]).then_inc(s["x_in"].sem, 16)

    def store(t):
        row = t.row(sp)
        if (due := s["stored"].due(t, lambda x: 16 * x)) is not None:
            sp.wait_ge(s["stored"].sem, due)
            apart(sp, k, t)
        sp.wait_ge(s["out"].sem, s["out"].at(t, lambda x: x + 1))
        apart(sp, k, t)
        sp.dma_start(m.dst.rearrange("(t n p) c -> t p n c", n=2, p=P)[row], k.ty[:, t.parity]).then_inc(s["stored"].sem, 16)

    load(Step(0))
    load(Step(1))

    def body(t):
        if t.reg is not None or t.n + 2 < PAIRS:
            load(t + 2)
        if t.reg is not None or t.n > 0:
            store(t + -1)

    pipeline(sp, PAIRS, body)
    store(Step(PAIRS - 1))
    sp.wait_ge(s["stored"].sem, s["stored"].base + 16 * PAIRS)


def expert_of(eng, k, t, n):
    tile = 2 * t.n + n if t.reg is None else eng.snap(t.reg * 4 + (2 * t.n + n))
    return eng.value_load(k.tile_expert[0:1, bass.ds(tile, 1)], min_val=0, max_val=EXPERTS - 1)


def tensor_tiles(pe, m):
    k, s, w = m.k, m.s, m.w

    def turn(t):
        pe.wait_ge(s["x_in"].sem, s["x_in"].at(t, lambda x: 16 * (x + 1)))
        if (due := s["xt"].due(t, lambda x: x)) is not None:
            pe.wait_ge(s["xt"].sem, due)
        for n in range(2):
            last = pe.transpose(k.misc[:, n * P:(n + 1) * P], k.tx[:, t.parity, n], k.ident[:, :])
        last.then_inc(s["t_full"].sem, 1)

    def hidden(t, n):
        if (due := s["relu_vector"].due(t, lambda x: 2 * (x - 1) + n + 1)) is not None:
            pe.wait_ge(s["relu_vector"].sem, due)
        pe.wait_ge(s["xt"].sem, s["xt"].at(t, lambda x: x + 1))
        pe.wait_ge(s["w1_in"].sem, s["w1_in"].at(t, lambda x: 2 * x + n + 1))
        for f in range(FC):
            last = pe.matmul(k.scores[n][:, f * P:(f + 1) * P], k.tw1[:, t.parity, n * W1_COLS + f * P:n * W1_COLS + (f + 1) * P],
                             k.txt[:, t.parity, n * P:(n + 1) * P], start=True, stop=True)
        last.then_inc(s["h_full"].sem, 1)

    def outs(t, n, expert):
        at = pe.snap(expert * HID)
        if n == 0:
            if (due := s["out"].due(t, lambda x: x - 1)) is not None:
                pe.wait_ge(s["out"].sem, due)
        pe.wait_ge(s["relu_vector"].sem, s["relu_vector"].at(t, lambda x: 2 * x + n + 1))
        for f in range(FC):
            last = pe.matmul(k.turned[t.parity][:, n * P:(n + 1) * P], k.th[:, t.parity, (n * FC + f) * P:(n * FC + f + 1) * P],
                             w["w2"][:, bass.ds(at + f * P, P)], start=(f == 0), stop=(f == FC - 1))
        if n == 1:
            last.then_inc(s["y_full"].sem, 1)

    turn(Step(0))
    hidden(Step(0), 0)

    def body(t):
        experts = [expert_of(pe, k, t, n) for n in range(2)]
        hidden(t, 1)
        more = t.reg is not None or t.n + 1 < PAIRS
        if more:
            turn(t + 1)
        outs(t, 0, experts[0])
        if more:
            hidden(t + 1, 0)
        outs(t, 1, experts[1])

    pipeline(pe, PAIRS, body)


def scalar_tiles(act, m):
    k, s, w = m.k, m.s, m.w

    def weights(t, n):
        at = act.snap(expert_of(act, k, t, n) * W1_COLS)
        if (due := s["h_full"].due(t, lambda x: 2 * (x - 1) + n - 1)) is not None:
            act.wait_ge(s["h_full"].sem, due)
        if (due := s["relu_vector"].due(t, lambda x: 2 * (x - 1) + n - 1)) is not None:
            act.wait_ge(s["relu_vector"].sem, due)
        act.copy(k.tw1[:, t.parity, n * W1_COLS:(n + 1) * W1_COLS], w["w1"][:, bass.ds(at, W1_COLS)]).then_inc(s["w1_in"].sem, 1)

    for n in range(4):
        weights(Step(n // 2), n % 2)

    def body(t):
        more = t.reg is not None or t.n + 2 < PAIRS
        for n in range(2):
            act.wait_ge(s["h_full"].sem, s["h_full"].at(t, lambda x: 2 * x + n + 1))
            act.wait_ge(s["w1_in"].sem, s["w1_in"].at(t, lambda x: 2 * x + n + 1))
            if (due := s["y_full"].due(t, lambda x: x - 1)) is not None:
                act.wait_ge(s["y_full"].sem, due)
            for f in range(2):
                last = act.activation(k.th[:, t.parity, (n * FC + f) * P:(n * FC + f + 1) * P], k.scores[n][:, f * P:(f + 1) * P],
                                      ACT.Relu, bias=k.tw1[:, t.parity, n * W1_COLS + HID + f:n * W1_COLS + HID + f + 1], scale=1.0)
            last.then_inc(s["relu_scalar"].sem, 1)
            if more:
                weights(t + 2, n)

    pipeline(act, PAIRS, body)


def vector_tiles(dve, m):
    k, s, w = m.k, m.s, m.w

    def turned(t):
        dve.wait_ge(s["t_full"].sem, s["t_full"].at(t, lambda x: x + 1))
        if (due := s["h_full"].due(t, lambda x: 2 * (x - 1))) is not None:
            dve.wait_ge(s["h_full"].sem, due)
        dve.tensor_copy(k.txt[:, t.parity], k.misc[:, 0:2 * P]).then_inc(s["xt"].sem, 1)

    def relu(t, n):
        dve.wait_ge(s["relu_scalar"].sem, s["relu_scalar"].at(t, lambda x: 2 * x + n + 1))
        for f in range(2, FC):
            last = dve.tensor_scalar(k.th[:, t.parity, (n * FC + f) * P:(n * FC + f + 1) * P], k.scores[n][:, f * P:(f + 1) * P],
                                     k.tw1[:, t.parity, n * W1_COLS + HID + f:n * W1_COLS + HID + f + 1], 0.0, ALU.add, ALU.max)
        last.then_inc(s["relu_vector"].sem, 1)

    def finish(t, experts):
        at = [dve.snap(e * C) for e in experts]
        dve.wait_ge(s["y_full"].sem, s["y_full"].at(t, lambda x: x + 1))
        if (due := s["stored"].due(t, lambda x: 16 * (x - 1))) is not None:
            dve.wait_ge(s["stored"].sem, due)
        for n in range(2):
            last = dve.tensor_tensor(k.ty[:, t.parity, n], k.turned[t.parity][:, n * P:(n + 1) * P],
                                     w["b2"][:, bass.ds(at[n], C)], ALU.add)
        last.then_inc(s["out"].sem, 1)

    turned(Step(0))

    def body(t):
        experts = [expert_of(dve, k, t, n) for n in range(2)]
        relu(t, 0)
        if t.reg is not None or t.n + 1 < PAIRS:
            turned(t + 1)
        relu(t, 1)
        finish(t, experts)

    pipeline(dve, PAIRS, body)


class Gather:

    def __init__(self, k, rows, src, dst, w):
        self.k, self.rows, self.src, self.dst, self.w = k, rows, src, dst, w
        self.s = k.signals(dict(x_in=16, even_rows_in=8 * MB, odd_rows_in=8 * MB, stored=16, out=1), MSTEPS)


def sync_gather(sp, m):
    k, s = m.k, m.s

    def load(t):
        row = t.row(sp)
        if (due := s["x_in"].due(t, lambda x: 16 * x)) is not None:
            sp.wait_ge(s["x_in"].sem, due)
            apart(sp, k, t)
        if (due := s["out"].due(t, lambda x: x - 1)) is not None:
            sp.wait_ge(s["out"].sem, due)
            apart(sp, k, t)
        sp.dma_start(k.mx[:, t.parity], mlp_rows(m.src, row)).then_inc(s["x_in"].sem, 16)

    def store(t):
        row = t.row(sp)
        if (due := s["stored"].due(t, lambda x: 16 * x)) is not None:
            sp.wait_ge(s["stored"].sem, due)
            apart(sp, k, t)
        sp.wait_ge(s["out"].sem, s["out"].at(t, lambda x: x + 1))
        apart(sp, k, t)
        sp.dma_start(mlp_rows(m.dst, row), k.mout[:, t.parity]).then_inc(s["stored"].sem, 16)

    load(Step(0))
    load(Step(1))

    def body(t):
        store(t)
        if t.reg is not None or t.n + 2 < MSTEPS:
            load(t + 2)

    pipeline(sp, MSTEPS, body)
    sp.wait_ge(s["stored"].sem, s["stored"].base + 16 * MSTEPS)


def gpsimd_gather(pool, m):
    k, s = m.k, m.s
    for t in range(MSTEPS):
        if t >= 2:
            pool.wait_ge(s["out"].sem, s["out"].base + t - 1)
        for blk in range(MB):
            j = MB * t + blk
            pool.indirect_dma_start(k.my[:, t % 2, blk], None, m.rows, bass.IndirectOffsetOnAxis(ap=k.place[:, j:j + 1], axis=0))\
                .then_inc(s["odd_rows_in" if t % 2 else "even_rows_in"].sem, 16)


def vector_gather(dve, m):
    k, s = m.k, m.s

    def body(t):
        flat = lambda x: x.rearrange("p k c -> p (k c)")
        dve.wait_ge(s["x_in"].sem, s["x_in"].at(t, lambda x: 16 * (x + 1)))
        rows_in = s["odd_rows_in" if t.parity else "even_rows_in"]
        dve.wait_ge(rows_in.sem, rows_in.at(t, lambda x: 16 * MB * (x // 2 + 1)))
        if (due := s["stored"].due(t, lambda x: 16 * (x - 1))) is not None:
            dve.wait_ge(s["stored"].sem, due)
        dve.scalar_tensor_tensor(out=flat(k.mout[:, t.parity]), in0=flat(k.my[:, t.parity]), scalar=m.w["gate"],
                                 in1=flat(k.mx[:, t.parity]), op0=ALU.mult, op1=ALU.add).then_inc(s["out"].sem, 1)

    pipeline(dve, MSTEPS, body)



class Core:

    def __init__(self, nc, ctx):
        self.nc, self.ctx, self.counts = nc, ctx, {}
        self.scores = [ctx.enter_context(nc.psum_tensor(f"scores{i}", [P, 1024], F32)) for i in range(2)]
        self.turned = [ctx.enter_context(nc.psum_tensor(f"turned{i}", [P, 512], F32)) for i in range(2)]
        self.num = ctx.enter_context(nc.psum_tensor("num", [P, 512], F32))
        self.misc = ctx.enter_context(nc.psum_tensor("misc", [P, 512], F32))
        self.ident = self.sb("ident", [P, P])
        self.identb = self.sb("identb", [P, P], BF16)
        self.above = self.sb("above", [P, P], BF16)
        self.own8 = self.sb("own8", [P, 16])
        self.own32 = self.sb("own32", [P, 4])
        self.own_columns = self.sb("own_columns", [P, 4, 32])
        self.own_pair8 = self.sb("own_pair8", [P, 8, P])
        self.own_pair32 = self.sb("own_pair32", [P, 8, P])
        self.minus_half = self.sb("minus_half", [P, 4])
        self.eps = self.sb("eps", [P, 4])
        self.falling = self.sb("falling", [P, EXPERTS])
        self.ones = self.sb("ones", [P, P])
        self.zeros = self.sb("zeros", [P, 512])
        self.up_to = self.sb("up_to", [P, P])
        self.tile_numbers = self.sb("tile_numbers", [P, TILES])
        self.tile_expert = self.sb("tile_expert", [P, TILES], I32)
        self.place = self.sb("place", [P, BLOCKS], I32)
        self.space = self.sb("space", [P, SPACE])
        self.at = 0
        t = self.take
        self.through = self.sem("through")
        self.km, self.qT, self.val = t(2, 16, 256), t(2, 4, 256), t(2, 2, 512)
        self.probs, self.pt = t(2, 2, 512), t(8, 384)
        self.numS, self.rx, self.ot = t(2, 4, 256), t(2, 512), t(4, 256)
        self.xq, self.xk, self.wn, self.x_in = t(2, 256), t(2, 256), t(2, 2, 128), t(2, 2, 128)
        self.base_in, self.base_sum, self.res = t(2, 2, 128), t(2, 2, 128), t(2, 2, 128)
        self.nmax, self.sums, self.rsum = t(2, 4), t(2, 2, 16), t(2, 2, 16)
        self.stats, self.aggr, self.vareps, self.rstd = t(2, 2, 6), t(2, 2, 2), t(2, 2), t(2, 2)
        self.cstats, self.caggr, self.cvareps, self.crstd = t(2, 1, 6)[0:TC], t(2, 1, 2)[0:TC], t(2, 1)[0:TC], t(2, 1)[0:TC]
        self.cmax = t(2, 8)
        mark = self.at
        self.at = 0
        self.km_cross, self.vb, self.ptc = t(2, 1024), t(2, 8, 128), t(2, 4, 256)
        self.pc = t(2, 512)
        self.ctx_in, self.cn, self.xc = t(2, 64)[0:TC], t(2, 64)[0:TC], t(2, 2, 64)[0:TC]
        assert self.at <= 2 * 16 * 256, self.at
        self.at = 0
        self.mx, self.malso, self.mstart, self.mwn = t(2, 4, 128), t(2, 4, 128), t(2, 4, 128), t(2, 4, 128)
        self.mxt, self.msum, self.mboth, self.mr = t(2, 512), t(2, 4, 128), t(2, 4, 128), t(2, 4, 128)
        self.mrn, self.mrg, self.mout = t(2, 4, 128), t(2, 4, 128), t(2, 4, 128)
        tiles_at = self.at
        self.mh = t(2, 4, 512)
        self.mstats, self.maggr, self.meps, self.mrstd = t(2, 4, 6), t(2, 4, 2), t(2, 4), t(2, 4)
        self.mrstats, self.mraggr, self.mreps, self.mrrstd = t(2, 4, 6), t(2, 4, 2), t(2, 4), t(2, 4)
        self.rows, self.logits = t(MSTEPS, 512), t(MSTEPS, MB * EXPERTS)
        self.equal, self.rank, self.chosen, self.sums_a, self.sums_b = t(256), t(256), t(256), t(256), t(256)
        self.best, self.first, self.ended, self.tile_expert_f = t(BLOCKS), t(BLOCKS), t(TILES * EXPERTS), t(TILES)
        self.tiles_x, self.tiles, self.ends_a, self.ends_b, self.ends_c = (t(EXPERTS) for _ in range(5))
        self.starts, self.start_rows = t(EXPERTS), t(EXPERTS)
        end, self.at = self.at, tiles_at
        self.tx, self.txt, self.tw1, self.ty = t(2, 2, P), t(2, 2 * P), t(2, 2 * W1_COLS), t(2, 2, C)
        assert self.at <= tiles_at + 2 * 4 * 512
        self.at = end
        self.th, self.my = t(2, 2 * HID), t(2, MB, C)
        mark = max(mark, self.at)
        self.at = 0
        self.quant, self.quant_round, self.quant_out, self.proj_sum = t(1024), t(1024), t(1024), t(512)
        self.fc_t, self.proj_t, self.bfc_t, self.bproj_t = t(512), t(512), t(512)[0:RANK], t(128)[0:RANK]
        self.amax, self.amax_t, self.amax_d, self.amax_b = t(2), t(1)[0:2], t(2)[0:2], t(2)
        self.qscale, self.qinv = t(2), t(2)
        self.bv_b, self.bcv_b, self.bp_g, self.value_rows = t(128), t(128), t(128), t(256)
        mark = max(mark, self.at)
        assert mark <= SPACE, mark

    def sb(self, name, shape, dt=F32):
        return self.ctx.enter_context(self.nc.sbuf_tensor(name, shape, dt))

    def sem(self, name):
        return self.ctx.enter_context(self.nc.semaphore(name))

    def signals(self, each, steps):
        out = {}
        for name, n in each.items():
            if name not in self.counts:
                self.counts[name] = (self.sem(name), 0)
            sem, base = self.counts[name]
            out[name] = Signal(sem, base)
            self.counts[name] = (sem, base + n * steps)
        return out

    def take(self, *shape):
        n = 1
        for x in shape:
            n *= x
        flat = self.space[:, self.at:self.at + n]
        self.at += n
        if len(shape) == 1:
            return flat
        if len(shape) == 2:
            return flat.rearrange("p (a b) -> p a b", b=shape[1])
        return flat.rearrange("p (a b c) -> p a b c", b=shape[1], c=shape[2])


class Weights:

    FIRST_ROWS = ("bk", "bq", "bck", "bcq", "bv", "bcv")
    LATER_ROWS = tuple(f"{a}_{n}" for a in ("a1", "a2") for n in ("lnx_g", "lnx_b", "lny_g", "lny_b", "ln3_g", "ln3_b"))

    def __init__(self, k):
        self.k = k
        t = lambda name, *shape: k.sb("w_" + name, list(shape))
        self.first_rows, self.first_cols = t("first_rows", 8, P), t("first_cols", P, 8)
        self.later_rows, self.later_cols = t("later_rows", 64, P), t("later_cols", P, 64)
        self.scaled = t("scaled", P, 2)
        self.raw_gates, self.gates = t("raw_gates", P, 4), t("gates", P, 4)
        self.Wq, self.Wk, self.Wv, self.Wcq = (t(n, C, C) for n in ("Wq", "Wk", "Wv", "Wcq"))
        self.Wck, self.Wcv = t("Wck", CC, C), t("Wcv", CC, C)
        self.raw_wp, self.wp, self.bp = t("raw_wp", C, C), t("wp", P, 1, C), t("bp", P, C)
        self.o_bias1, self.o_bias2 = t("o_bias1", P, C), t("o_bias2", P, C)
        self.fc, self.proj = t("fc", P, HID), t("proj", P, FC, C)
        self.raw_bfc, self.raw_bproj = t("raw_bfc", P, FC, RANK), t("raw_bproj", P, RANK)
        self.a_fc, self.a_proj = t("a_fc", RANK, C), t("a_proj", RANK, HID)
        self.proj_b, self.proj_bg = t("proj_b", P, C), t("proj_bg", P, C)
        self.ln = {n: t(n, P, C) for n in ("ln1_g", "ln1_b", "ln2_g", "ln2_b")}
        self.attn = {}
        for a, cy in (("a1", C), ("a2", CC)):
            self.attn[a] = dict(wq=t(a + "_wq", C, H, 32), wk=t(a + "_wk", cy, H, 32), wv=t(a + "_wv", cy, H, 32),
                                li1_w=t(a + "_li1_w", P, 4, C), li2_w=t(a + "_li2_w", C, HID), li3_w=t(a + "_li3_w", P, FC, C),
                                li1_b=t(a + "_li1_b", P, C), li3_b=t(a + "_li3_b", P, C))
        self.raw_gate, self.gate_w, self.gate_b = t("raw_gate", EXPERTS, C), t("gate_w", C, EXPERTS), t("gate_b", P, EXPERTS)
        self.w1, self.w2 = t("w1", P, EXPERTS, W1_COLS), t("w2", P, EXPERTS, FC, C)
        self.b2 = t("b2", P, EXPERTS * C)

    def col(self, name):
        if name in self.FIRST_ROWS:
            i = self.FIRST_ROWS.index(name)
            return self.first_cols[:, i:i + 1]
        i = self.LATER_ROWS.index(name)
        return self.later_cols[0:CC if name[0:6] == "a2_lny" else P, i:i + 1]

    def hidden_bias(self, i):
        n = len(self.LATER_ROWS) + FC * i
        return self.later_cols[:, n:n + FC]

    @property
    def expert_bias(self):
        return self.later_cols[:, 32:64].rearrange("p (e f) -> p e f", f=FC)


def on_every_partition(v):
    return v.rearrange("(a n) -> a n", a=1).to_broadcast([P, v.shape[0]])


def first_loads(w, g_xattn, g_ffn, A):
    rows = [(w.first_rows[i:i + 1, :], A[n].rearrange("(a n) -> a n", a=1)) for i, n in enumerate(w.FIRST_ROWS)]
    return rows + [
        (w.raw_gates[:, 0:2], on_every_partition(g_xattn)), (w.raw_gates[:, 2:4], on_every_partition(g_ffn)),
        (w.raw_wp[:, :], A["Wp"]), (w.Wq[:, :], A["Wq"]), (w.Wk[:, :], A["Wk"]), (w.Wv[:, :], A["Wv"]),
        (w.Wcq[:, :], A["Wcq"]), (w.Wck[:, :], A["Wck"]), (w.Wcv[:, :], A["Wcv"]), (w.bp[:, :], on_every_partition(A["bp"]))]


def later_loads(w, F, X, M):
    out = []
    for i, n in enumerate(w.LATER_ROWS):
        out.append((w.later_rows[i:i + 1, 0:X[n].shape[0]], X[n].rearrange("(a n) -> a n", a=1)))
    for i, v in enumerate((F["b_fc"], X["a1_li2_b"], X["a2_li2_b"])):
        n = len(w.LATER_ROWS) + FC * i
        out.append((w.later_rows[n:n + FC, :], v.rearrange("(f p) -> f p", p=P)))
    out += [
        (w.later_rows[32:64, :], M["b1"].rearrange("e (f p) -> (e f) p", p=P)),
        (w.fc[:, :].rearrange("p (f c) -> p f c", f=FC), F["W_fc"].rearrange("(f p) c -> p f c", p=P)),
        (w.proj[:, :, :].rearrange("p f c -> p (f c)"), F["W_proj"]),
        (w.raw_bfc[:, :, :], F["B_fc"].rearrange("(f p) r -> p f r", p=P)), (w.raw_bproj[:, :], F["B_proj"]),
        (w.a_fc[:, :], F["A_fc"]), (w.a_proj[:, :], F["A_proj"]), (w.proj_b[:, :], on_every_partition(F["b_proj"])),
        (w.raw_gate[:, :], M["gate_w"]), (w.gate_b[:, :], on_every_partition(M["gate_b"])), (w.b2[:, :], on_every_partition(M["b2"].rearrange("e c -> (e c)"))),
        (w.w2[:, :, :, :].rearrange("p e f c -> p e (f c)"), M["w2"].rearrange("e p h -> p e h"))]
    out += [(w.w1[:, e, 0:HID].rearrange("p (f c) -> p f c", c=C), M["w1"][e].rearrange("(f p) c -> p f c", p=P))
            for e in range(EXPERTS)]
    for a, t in w.attn.items():
        out += [(t[n][:, :, :], X[f"{a}_{n}"].rearrange("h c d -> c h d")) for n in ("wq", "wk", "wv")]
        out += [(t[n][:, :, :], X[f"{a}_{n}"].rearrange("(g p) c -> p g c", p=P)) for n in ("li1_w", "li3_w")]
        out += [(t["li2_w"][:, :], X[f"{a}_li2_w"])]
        out += [(t[n][:, :], on_every_partition(X[f"{a}_{n}"])) for n in ("li1_b", "li3_b")]
    return out + [(w.ln[n][:, :], on_every_partition(X[n])) for n in w.ln]



class Ready:

    FILLED_FIRST, RESULTS_FIRST = 2, 5

    def __init__(self, k):
        self.made, self.loaded_first, self.loaded_later = k.sem("made"), k.sem("loaded_first"), k.sem("loaded_later")
        self.gated, self.filled, self.result = k.sem("gated"), k.sem("filled"), k.sem("result")
        self.turned, self.emptied = k.sem("turned"), k.sem("emptied")


def tensor_first(pe, k, w, r):
    pe.transpose(k.num[:, 0:8], w.first_rows[:, :], k.ident[0:8, 0:8]).then_inc(r.filled, 1)
    pe.wait_ge(r.result, 3)
    pe.matmul(k.misc[:, 0:P], k.bv_b, w.raw_wp[:, :], start=True, stop=True)
    pe.matmul(k.misc[:, P:2 * P], k.bcv_b, w.raw_wp[:, :], start=True, stop=True).then_inc(r.filled, 1)


def vector_first(dve, k, w, r):
    result = Count(r.result)
    dve.wait_ge(r.filled, 1)
    result.inc(dve.tensor_copy(w.first_cols[:, :], k.num[:, 0:8]))
    dve.wait_ge(r.result, result.n)
    result.inc(dve.tensor_scalar(k.bv_b, k.ones[:, :], w.col("bv"), None, ALU.mult))
    result.inc(dve.tensor_scalar(k.bcv_b, k.ones[:, :], w.col("bcv"), None, ALU.mult))
    dve.tensor_scalar(w.scaled[:, 0:1], w.col("bq"), 8.0 ** -0.5, None, ALU.mult)
    dve.tensor_scalar(w.scaled[:, 1:2], w.col("bcq"), 8.0 ** -0.5, None, ALU.mult)
    dve.wait_ge(r.gated, 1)
    dve.tensor_scalar(w.wp[:, 0], w.raw_wp[:, :], w.gates[:, 0:1], None, ALU.mult)
    dve.wait_ge(r.filled, 2)
    result.inc(dve.tensor_tensor(k.bp_g, w.bp[:, :], k.misc[:, 0:P], ALU.add))
    dve.wait_ge(r.result, result.n)
    dve.tensor_scalar(w.o_bias1[:, :], k.bp_g, w.gates[:, 0:1], None, ALU.mult)
    result.inc(dve.tensor_scalar(w.o_bias2[:, :], k.misc[:, P:2 * P], w.gates[:, 0:1], None, ALU.mult))
    assert result.n == Ready.RESULTS_FIRST



class Prepare:

    ROW_MAX, MAX, DIAGONAL, SCALE, INVERSE, QUANTISED = 1, 2, 3, 4, 5, 15

    def __init__(self, k, w, r, later):
        self.k, self.w, self.r, self.later = k, w, r, later


def nothing(eng, m):
    pass


def tensor_prepare(pe, m):
    k, w, r, n = m.k, m.w, m.r, Ready.RESULTS_FIRST
    turned, filled = Count(r.turned), Count(r.filled)

    def turn(bank, parts, rows):
        for f, part in enumerate(parts):
            last = pe.transpose(bank[0:part.shape[1], f * rows:(f + 1) * rows], part, k.ident[0:rows, 0:rows])
        return last

    def to_scalar(parts, rows):
        if turned.n >= 4:
            pe.wait_ge(r.emptied, turned.n - 3)
        half = turned.n % 2 * 512
        turned.inc(turn(k.scores[turned.n // 2 % 2][:, half:half + 512], parts, rows))

    pe.wait_ge(r.loaded_later, m.later)
    to_scalar([w.later_rows[:, :]], 64)
    to_scalar([w.raw_bfc[:, f] for f in range(FC)], P)
    to_scalar([w.raw_bproj[:, :]], P)
    to_scalar([w.raw_gate[:, :]], EXPERTS)
    pe.wait_ge(r.result, n + m.ROW_MAX)
    filled.inc(turn(k.num, [k.amax], P))
    for e in range(EXPERTS):
        to_scalar([w.w1[:, e, f * P:(f + 1) * P] for f in range(FC)], P)
        to_scalar([w.w2[:, e, f] for f in range(FC)], P)
        if e == 1:
            pe.wait_ge(r.result, n + m.DIAGONAL)
            filled.inc(pe.matmul(k.misc[:, 0:2], k.ones[0:2, :], k.amax_d, start=True, stop=True))
    pe.wait_ge(r.result, n + m.QUANTISED)
    q = k.quant_out
    filled.inc(turn(k.turned[0], [q[:, f * P:(f + 1) * P] for f in range(FC)], P))
    filled.inc(turn(k.turned[1], [q[:, HID + f * P:HID + (f + 1) * P] for f in range(FC)], P))
    pe.wait_ge(r.emptied, turned.n)
    filled.inc(pe.matmul(k.num[:, :], w.a_fc[:, :], k.bfc_t, start=True, stop=True))
    for f in range(FC):
        last = pe.matmul(k.misc[:, f * P:(f + 1) * P], w.a_proj[:, f * P:(f + 1) * P], k.bproj_t, start=True, stop=True)
    filled.inc(last)


def scalar_prepare(act, m):
    k, w, r = m.k, m.w, m.r
    emptied = Count(r.emptied)

    def empty(out, scale=None):
        act.wait_ge(r.turned, emptied.n + 1)
        half = emptied.n % 2 * 512
        bank = k.scores[emptied.n // 2 % 2][0:out.shape[0], half:half + out.shape[1]]
        emptied.inc(act.copy(out, bank) if scale is None else act.mul(out, bank, scale))

    empty(w.later_cols[:, :])
    empty(k.bfc_t, LORA_SCALE)
    empty(k.bproj_t, LORA_SCALE)
    empty(w.gate_w[:, :])
    act.wait_ge(r.emptied, 1)
    act.copy(w.w1[:, :, HID:W1_COLS], w.expert_bias)
    for e in range(EXPERTS):
        empty(w.w1[:, e, 0:HID])
        empty(w.w2[:, e].rearrange("p f c -> p (f c)"))


def vector_prepare(dve, m):
    k, w, r = m.k, m.w, m.r
    n, filled = Ready.RESULTS_FIRST, Ready.FILLED_FIRST
    result = Count(r.result)
    result.n = n
    raws = (w.fc[:, :], w.proj[:, :, :].rearrange("p f c -> p (f c)"))
    dve.wait_ge(r.loaded_later, m.later)
    dve.tensor_reduce(k.amax[:, 0:1], raws[0], AX.X, ALU.max, apply_absolute_value=True)
    result.inc(dve.tensor_reduce(k.amax[:, 1:2], raws[1], AX.X, ALU.max, apply_absolute_value=True))
    dve.wait_ge(r.filled, filled + 1)
    result.inc(dve.tensor_reduce(k.amax_t, k.num[0:2, 0:P], AX.X, ALU.max))
    dve.wait_ge(r.result, result.n)
    result.inc(dve.tensor_scalar(k.amax_d, k.ident[0:2, 0:2], k.amax_t, None, ALU.mult))
    dve.wait_ge(r.filled, filled + 2)
    result.inc(dve.tensor_scalar(k.qscale, k.misc[:, 0:2], 1.0 / QMAX, None, ALU.mult))
    dve.wait_ge(r.result, result.n)
    result.inc(dve.reciprocal(k.qinv, k.qscale))
    assert result.n == n + m.INVERSE

    def quantise(step, j):
        half = slice(j * HID, (j + 1) * HID)
        q, rounded, raw = k.quant[:, half], k.quant_round[:, half], raws[j]
        if step == 0:
            return dve.tensor_scalar(q, raw, k.qinv[:, j:j + 1], ROUND, ALU.mult, ALU.add)
        if step == 1:
            return dve.tensor_scalar(rounded, q, ROUND, QMAX, ALU.subtract, ALU.min)
        if step == 2:
            return dve.tensor_scalar(q, rounded, -QMAX - 1.0, k.qscale[:, j:j + 1], ALU.max, ALU.mult)
        if step == 3:
            return dve.tensor_tensor(rounded, q, raw, ALU.subtract)
        return dve.tensor_tensor(k.quant_out[:, half], raw, rounded, ALU.add)

    for step in range(5):
        for j in range(2):
            dve.wait_ge(r.result, result.n - (1 if step else j))
            result.inc(quantise(step, j))
    assert result.n == n + m.QUANTISED
    dve.wait_ge(r.filled, filled + 3)
    dve.tensor_copy(k.fc_t, k.turned[0][:, :])
    dve.wait_ge(r.filled, filled + 4)
    result.inc(dve.tensor_copy(k.proj_t, k.turned[1][:, :]))
    dve.wait_ge(r.result, result.n)
    dve.wait_ge(r.filled, filled + 5)
    dve.tensor_tensor(w.fc[:, :], k.num[:, :], k.fc_t, ALU.add)
    dve.wait_ge(r.filled, filled + 6)
    result.inc(dve.tensor_tensor(k.proj_sum, k.misc[:, :], k.proj_t, ALU.add))
    dve.wait_ge(r.result, result.n)
    dve.tensor_scalar(raws[1], k.proj_sum, w.gates[:, 2:3], None, ALU.mult)
    result.inc(dve.tensor_scalar(w.proj_bg[:, :], w.proj_b[:, :], w.gates[:, 2:3], None, ALU.mult))


def gpsimd_constants(pool, k, w, made):
    def fill(t, v):
        made.inc(pool.memset(t, v))

    def keep(t, pattern, base, cm, op=ALU.is_ge, v=0.0):
        pool.wait_ge(made.sem, made.n)
        made.inc(pool.affine_select(out=t, in_=t, compare_op=op, fill=v, base=base, pattern=pattern, channel_multiplier=cm))

    fill(k.ident[:, :], 0.0)
    keep(k.ident[:, :], [[-1, P]], 0, 1, ALU.not_equal, 1.0)
    for t, v in ((k.identb, 0.0), (k.above, 0.0), (k.own8, 1.0), (k.own32, 1.0), (k.ones, 1.0), (k.up_to, 1.0), (k.zeros, 0.0), (k.minus_half, -0.5), (k.eps, EPS)):
        fill(t[:, :], v)
    for t in (k.own_columns, k.own_pair8, k.own_pair32):
        fill(t[:, :, :], 1.0)
    for e in range(EXPERTS):
        fill(k.falling[:, e:e + 1], float(EXPERTS - e))
    for tile in range(TILES):
        fill(k.tile_numbers[:, tile:tile + 1], float(tile))
    keep(k.up_to[:, :], [[1, P]], 0, -1)
    keep(k.identb[:, :], [[-1, P]], 0, 1, ALU.not_equal, 1.0)
    keep(k.above[:, :], [[-1, P]], 0, 1, ALU.is_ge, MASKED)
    for own, n in ((k.own8, 8), (k.own32, 32)):
        keep(own[:, :], [[-n, P // n]], 0, 1)
        keep(own[:, :], [[n, P // n]], n - 1, -1)
    keep(k.own_columns[:, :, :], [[-8, 4], [1, 32]], 0, 0)
    keep(k.own_columns[:, :, :], [[8, 4], [-1, 32]], 7, 0)
    for half in range(2):
        part = slice(64 * half, 64 * half + 64)
        keep(k.own_pair8[part], [[-16, 8], [1, P]], -8 * half, 0)
        keep(k.own_pair8[part], [[16, 8], [-1, P]], 8 * half + 7, 0)
        for j in range(2):
            four = k.own_pair32[part].rearrange("p (g j) c -> p g j c", j=2)[:, :, j]
            keep(four, [[0, 4], [1, P]], -(64 * j + 32 * half), 0)
            keep(four, [[0, 4], [-1, P]], 64 * j + 32 * half + 31, 0)


def network(nc, x, ctx_512, g_xattn, g_ffn, A, F, X, M, out, parts_run=None):
    with ExitStack() as stack:
        k = Core(nc, stack)
        w, r = Weights(k), Ready(k)
        made = Count(r.made)
        first, later = first_loads(w, g_xattn, g_ffn, A), later_loads(w, F, X, M)
        phase, cleared = k.sem("phase"), k.sem("cleared")
        made_all = 43 + TILES

        def dram(name):
            return nc.dram_tensor(name, [B, S, C], F32, kind="Internal").ap()

        s1, s2, x2, xx, xo1, xm, xo2, x3 = (dram(n) for n in ("s1", "s2", "x2", "xx", "xo1", "xm", "xo2", "x3"))

        sorted_in, sorted_out = (nc.dram_tensor(n, [TILES * P, C], F32, kind="Internal").ap() for n in ("sorted_in", "sorted_out"))
        later += [(sorted_in.rearrange("(t p n) c -> t p (n c)", p=P, n=4)[i], k.zeros[:, :]) for i in range(TILES // 4)]

        def second(a):
            t = w.attn[a]
            wide = {n: t[n][:, :, :].rearrange("c h d -> c (h d)") for n in ("wq", "wk", "wv")}
            return dict(wide, wo=t["li1_w"], q_gain=w.col(a + "_lnx_g"), q_shift=w.col(a + "_lnx_b"),
                        k_gain=w.col(a + "_lny_g"), k_shift=w.col(a + "_lny_b"), q_bias=None, k_bias=None,
                        o_bias=t["li1_b"][:, :], own=k.own32, own_pair=k.own_pair32[:, :, :])

        def first_layer(wq, wk, wv, q_bias, k_bias, o_bias):
            return dict(wq=wq, wk=wk, wv=wv, wo=w.wp, q_gain=None, q_shift=None, k_gain=None, k_shift=None, q_bias=q_bias,
                        k_bias=k_bias, o_bias=o_bias[:, :], own=k.own8, own_pair=k.own_pair8[:, :, :])

        def mlp(a, i):
            t = w.attn[a]
            return dict(gain=w.col(a + "_ln3_g"), shift=w.col(a + "_ln3_b"), w1=t["li2_w"], b1=w.hidden_bias(i), w2=t["li3_w"],
                        bias=t["li3_b"][:, :], out_gain=w.ln["ln2_g"][:, :], out_shift=w.ln["ln2_b"][:, :], gate=w.gates[:, 1:2])

        parts = [
            Attention(k, "a", "self", 8, "before", x, x, s1, None, False,
                      first_layer(w.Wq, w.Wk, w.Wv, w.scaled[:, 0:1], w.col("bk"), w.o_bias1)),
            Attention(k, "b", "cross", 8, None, x, s1, s2, ctx_512, False,
                      first_layer(w.Wcq, w.Wck, w.Wcv, w.scaled[:, 1:2], w.col("bck"), w.o_bias2)),
            Prepare(k, w, r, 16 * len(later)),
            Mlp(k, "c", s2, None, "norm", xx, x2, None, dict(
                gain=None, shift=None, w1=w.fc, b1=w.hidden_bias(0), w2=w.proj, bias=w.proj_bg[:, :],
                out_gain=w.ln["ln1_g"][:, :], out_shift=w.ln["ln1_b"][:, :])),
            Attention(k, "d", "self", 32, "after", xx, xx, xo1, None, False, second("a1")),
            Mlp(k, "e", xo1, xx, "norm", xm, None, None, mlp("a1", 1)),
            Attention(k, "f", "cross", 32, None, xm, xm, xo2, ctx_512, True, second("a2")),
            Mlp(k, "g", xo2, xm, "add", x3, None, x2, mlp("a2", 2)),
            Route(k, x3, dict(gate_w=w.gate_w[:, :], gate_b=w.gate_b[:, :])),
            Sort(k, sorted_in),
            Tiles(k, sorted_in, sorted_out, dict(w1=w.w1[:, :, :].rearrange("p e n -> p (e n)"),
                                                 w2=w.w2[:, :, :, :].rearrange("p e f c -> p (e f c)"), b2=w.b2)),
            Gather(k, sorted_out, x3, out, dict(gate=w.gates[:, 3:4])),
        ][0:parts_run]
        [p for p in parts if not isinstance(p, Prepare)][-1].dst = out
        parts[0].weights_ahead, parts[0].loaded_ahead = later, r.loaded_later
        block = stack.enter_context(nc.Block())

        def phases(eng, programs):
            for n, part in enumerate(parts):
                eng.drain().then_inc(phase, 1)
                eng.wait_ge(phase, 5 * (n + 1))
                programs[type(part)](eng, part)

        @block.sync
        def _(sp):
            sp.wait_ge(cleared, 1)
            for dst, src in first:
                sp.dma_start(dst, src).then_inc(r.loaded_first, 16)
            phases(sp, {Attention: sync_attention, Mlp: sync_mlp, Route: sync_route, Sort: nothing, Tiles: sync_tiles, Gather: sync_gather, Prepare: nothing})

        @block.gpsimd
        def _(pool):
            gpsimd_constants(pool, k, w, made)
            assert made.n == made_all, made.n
            pool.wait_ge(r.made, made_all)
            phases(pool, {Attention: gpsimd_attention, Mlp: gpsimd_mlp, Route: gpsimd_route, Sort: gpsimd_sort, Tiles: nothing, Gather: gpsimd_gather, Prepare: nothing})

        @block.scalar
        def _(act):
            act.wait_ge(cleared, 1)
            act.wait_ge(r.loaded_first, 16 * len(first))
            act.activation(w.gates[:, :], w.raw_gates[:, :], ACT.Tanh).then_inc(r.gated, 1)
            phases(act, {Attention: scalar_attention, Mlp: scalar_mlp, Route: scalar_route, Sort: nothing, Tiles: scalar_tiles, Gather: nothing, Prepare: scalar_prepare})

        @block.tensor
        def _(pe):
            pe.wait_ge(r.loaded_first, 16 * len(first))
            pe.wait_ge(r.made, made_all)
            tensor_first(pe, k, w, r)
            phases(pe, {Attention: tensor_attention, Mlp: tensor_mlp, Route: tensor_route, Sort: tensor_sort, Tiles: tensor_tiles, Gather: nothing, Prepare: tensor_prepare})

        @block.vector
        def _(dve):
            dve.memset(w.first_rows[:, :], 0.0)
            dve.memset(w.later_rows[:, :], 0.0).then_inc(cleared, 1)
            dve.wait_ge(r.loaded_first, 16 * len(first))
            dve.wait_ge(r.made, made_all)
            vector_first(dve, k, w, r)
            phases(dve, {Attention: vector_attention, Mlp: vector_mlp, Route: vector_route, Sort: vector_sort, Tiles: vector_tiles, Gather: vector_gather, Prepare: vector_prepare})


OUT = (B, S, C)


def kernel(**inputs):
    import numpy as np
    import concourse.bacc as bacc
    from concourse.bass_utils import run_bass_kernel_spmd

    nc = bacc.Bacc("TRN2", target_bir_lowering=False, num_devices=1)
    arrays, aps = {}, {}
    for name, value in inputs.items():
        a = np.ascontiguousarray(value)
        arrays[f"in_{name}"] = a
        aps[name] = nc.dram_tensor(f"in_{name}", a.shape, mybir.dt.from_np(a.dtype), kind="ExternalInput").ap()
    out = nc.dram_tensor("out", OUT, F32, kind="ExternalOutput").ap()

    def group(prefix):
        return {n[len(prefix):]: ap for n, ap in aps.items() if n.startswith(prefix)}

    network(nc, aps["x"], aps["ctx_512"], aps["g_xattn"], aps["g_ffn"], group("L0_xattn_"), group("L0_ffn_"),
            group("L1_xattn_"), group("L1_ffn_"), out)
    r = run_bass_kernel_spmd(nc, [arrays], core_ids=[0])
    return r.results[0]["out"]
```

```python
from contextlib import ExitStack

import concourse.bass as bass
from concourse import mybir

P = 128
B, S, C = 16, 256, 128
TC, CC = 64, 64
H = 16
SB = S // P
UNITS = H // 2
QUADS = H // 4
EPS = 1e-5
MASKED = -1e30
EXPERTS, HID = 8, 512
W1_COLS = HID + HID // P
MT = 512
MB = MT // P
MSTEPS = B * S // MT
FC = HID // P
RANK, LORA_SCALE = 16, 2.0
QMAX = 127.0
ROUND = 12582912.0
SPACE = 28720

F32 = mybir.dt.float32
BF16 = mybir.dt.bfloat16
I32 = mybir.dt.int32
ALU = mybir.AluOpType
ACT = mybir.ActivationFunctionType
AX = mybir.AxisListType


class Count:

    def __init__(self, sem):
        self.sem, self.n = sem, 0

    def inc(self, ins, by=1):
        ins.then_inc(self.sem, by)
        self.n += by


class Step:

    def __init__(self, n, reg=None, start=0):
        self.n, self.reg, self.start = n, reg, start

    def __add__(self, k):
        return Step(self.n + k, self.reg, self.start)

    @property
    def parity(self):
        return self.n % 2

    def count(self, fn):
        if self.reg is None:
            v = fn(self.n)
            return v if v > 0 else None
        n = self.n + 2 * self.start
        first, slope = fn(n), fn(n + 2) - fn(n)
        assert slope > 0 and fn(n + 4) - fn(n + 2) == slope
        assert first > 0, "a wait below one"
        return self.reg * slope + (first - slope * self.start)

    def row(self, eng):
        return self.n if self.reg is None else eng.snap(self.reg * 2 + self.n)


class Signal:

    def __init__(self, sem, base):
        self.sem, self.base = sem, base

    def due(self, step, fn):
        v = step.count(fn)
        return None if v is None else v + self.base

    def at(self, step, fn):
        v = self.due(step, fn)
        assert v is not None
        return v


def apart(eng, k, step):
    if step.reg is not None:
        eng.sem_inc(k.through)


def pipeline(eng, steps, body):
    for n in range(4):
        body(Step(n))
    with eng.Fori(2, steps // 2 - 1) as i:
        body(Step(0, i, 2))
        body(Step(1, i, 2))
    body(Step(steps - 2))
    body(Step(steps - 1))


class Attention:

    SLOTS = {
        ("self", 1): [["T0+"], ["R0-"], ["Q0+"], ["V0+"], ["Y0-"], [], [], []],
        ("self", 4): [["R0-", "T0+"], ["Q0+"], ["R1-", "Q1+"], ["Q2+"], ["R2-", "Q3+"], ["V0+"], ["R3-", "V1+"], ["Y0-"]],
        ("cross", 1): [["T0+"], ["Q0+"], ["R0-", "V0+"], ["Y0-"]],
        ("cross", 4): [["R0-", "R1-", "T0+"], ["Q0+", "Q1+"], ["R2-", "R3-", "V0+"], ["Q2+", "Q3+", "Y0-"]],
    }

    def __init__(self, k, name, kind, D, mask, src, base, dst, ctx, ctx_norm, w):
        self.name, self.kind, self.D, self.mask = name, kind, D, mask
        self.src, self.base, self.dst, self.ctx, self.ctx_norm = src, base, dst, ctx, ctx_norm
        self.w = w
        self.scale = float(D) ** -0.5
        self.G = H * D // P
        self.HG = H // self.G
        self.T = S if kind == "self" else TC
        self.KC = C if kind == "self" else CC
        self.one_side = kind == "self" and w["q_gain"] is None
        self.nv = 2 if kind == "self" and self.G == 4 else 1
        self.slots = self.SLOTS[(kind, self.G)]
        self.nslots = len(self.slots)
        self.regions = QUADS if self.G == 4 else 1
        self.k = k
        self.weights_ahead, self.loaded_ahead, self.constants_ahead = [], None, None
        U, G = (UNITS, self.G) if kind == "self" else (4, self.G)
        turned = H if kind == "self" else 4
        copied = H // 2 if kind == "self" else 4
        each = dict(x_in=16, base_in=16, stored=16, stats=1, aggr=1, eps_in=1, rstd=1, wn=1, t_full=1, side=1, qk_full=G,
                    q_ready=G, km_ready=G, v_full=self.nv, v_ready=self.nv, s_full=U, max_ready=U, exp_done=U,
                    tr_full=turned, pt_ready=copied, pv_done=QUADS if kind == "self" else 2, num_saved=self.regions,
                    rden=1, rx=1, r_full=G, ot=G, y_full=1, res=1, biased=1)
        if kind == "self":
            each.update(odd_pt_ready=copied)
            each.update(k_out=G, km_ready=UNITS, odd_km_ready=UNITS)
        if mask == "after":
            each.update(masked=U)
        self.halves = 2 if kind == "cross" and self.G == 1 else 1
        if kind == "cross":
            each.update(ctx_in=16, km_ready=G * self.halves)
        if ctx_norm:
            each.update(cstats=1, caggr=1, ceps=1, crstd=1, cn=1)
        self.s = k.signals(each, B)

    def pieces(self, t):
        out = []
        for u, names in enumerate(self.slots):
            for n in names:
                b = t + (1 if n[2] == "+" else -1)
                if 0 <= b < B:
                    out.append((u, n[0], int(n[1]), b))
        return out

    def in_slot(self, step, u):
        at = 5 if step.reg is not None else step.n
        return [(kind, i, step + (b - at)) for (v, kind, i, b) in self.pieces(at) if v == u]

    def before(self, step, u, kind, i):
        at = 5 if step.reg is not None else step.n
        order = [p for t in range(-1, at + 1) for p in self.pieces(t) if self.same_bank(kind, i, p[1], p[2])]
        here = [n for n, p in enumerate(order) if p[1:3] == (kind, i) and p[0] == u][-1]
        if here == 0:
            return None
        _, kind, i, b = order[here - 1]
        return kind, i, b - at

    def bank(self, kind, i):
        if self.kind == "cross" and kind in "QR":
            return self.k.scores[1][:, i % 2 * 512:(i % 2 + 1) * 512]
        return self.k.misc

    def keys_bank(self, i):
        if self.kind == "cross" and self.G == 1:
            return self.k.scores[1][:, 512:1024]
        return self.bank("Q", i)

    def same_bank(self, kind, i, other, j):
        pair = self.kind == "cross" and kind in "QR", self.kind == "cross" and other in "QR"
        return pair == (True, True) and i % 2 == j % 2 or pair == (False, False)

    def emptied(self, kind, i):
        return {
            "T": [("side", 1, 1)],
            "Q": [("q_ready", self.G, i + 1), ("k_out", self.G, i + 1) if self.kind == "self" else
                  ("km_ready", self.G * self.halves, (i + 1) * self.halves)],
            "V": [("v_ready", self.nv, i + 1)],
            "R": [("ot", self.G, i + 1)],
            "Y": [("res", 1, 1)],
        }[kind]

    def group(self, v):
        return v * self.G // UNITS

    def keys_at(self, b, group):
        return b.parity if self.G == 1 else group

    def head(self, n):
        return 4 * (n % 4) + n // 4 if self.G == 1 else n



def attention_load(sp, a):
    k, s = a.k, a.s

    def load_x(b):
        row = b.row(sp)
        if (due := s["x_in"].due(b, lambda t: 16 * t)) is not None:
            sp.wait_ge(s["x_in"].sem, due)
            apart(sp, k, b)
        if (due := s["wn"].due(b, lambda t: t - 1)) is not None:
            sp.wait_ge(s["wn"].sem, due)
            apart(sp, k, b)
        sp.dma_start(k.x_in[:, b.parity], a.src[row].rearrange("(k p) c -> p k c", p=P)).then_inc(s["x_in"].sem, 16)
        if a.ctx is not None:
            if (due := s["ctx_in"].due(b, lambda t: 16 * t)) is not None:
                sp.wait_ge(s["ctx_in"].sem, due)
                apart(sp, k, b)
            if a.ctx_norm:
                if (due := s["cn"].due(b, lambda t: t - 1)) is not None:
                    sp.wait_ge(s["cn"].sem, due)
                    apart(sp, k, b)
            else:
                if (due := s["t_full"].due(b, lambda t: t - 1)) is not None:
                    sp.wait_ge(s["t_full"].sem, due)
                    apart(sp, k, b)
            sp.dma_start(k.ctx_in[:, b.parity], a.ctx[row]).then_inc(s["ctx_in"].sem, 16)

    return load_x


def sync_attention_ahead(sp, a):
    load = attention_load(sp, a)
    if a.s["wn"].base:
        sp.wait_ge(a.s["wn"].sem, a.s["wn"].base)
    load(Step(0))
    load(Step(1))


def sync_attention(sp, a, ahead):
    k, s = a.k, a.s

    load_x = attention_load(sp, a)

    def load_base(b):
        row = b.row(sp)
        if (due := s["base_in"].due(b, lambda t: 16 * t)) is not None:
            sp.wait_ge(s["base_in"].sem, due)
            apart(sp, k, b)
        if (due := s["res"].due(b, lambda t: t - 1)) is not None:
            sp.wait_ge(s["res"].sem, due)
            apart(sp, k, b)
        sp.dma_start(k.base_in[:, b.parity], a.base[row].rearrange("(k p) c -> p k c", p=P)).then_inc(s["base_in"].sem, 16)

    def store(b):
        row = b.row(sp)
        if (due := s["stored"].due(b, lambda t: 16 * t)) is not None:
            sp.wait_ge(s["stored"].sem, due)
            apart(sp, k, b)
        sp.wait_ge(s["res"].sem, s["res"].at(b, lambda t: t + 1))
        apart(sp, k, b)
        sp.dma_start(a.dst[row].rearrange("(k p) c -> p k c", p=P), k.res[:, b.parity]).then_inc(s["stored"].sem, 16)

    def body(t):
        if t.n < B - 2 or t.reg is not None:
            load_x(t + 2)
        load_base(t)
        if t.reg is None and t.n < 4:
            for dst, src in a.weights_ahead[t.n::4]:
                sp.dma_start(dst, src).then_inc(a.loaded_ahead, 16)
        if t.n > 0 or t.reg is not None:
            store(t + -1)

    pipeline(sp, B, body)
    ahead()
    store(Step(B - 1))
    sp.wait_ge(s["stored"].sem, s["stored"].base + 16 * B)



def tensor_attention(pe, a):
    k, s, w = a.k, a.s, a.w

    def piece(t, u, kind, i, b):
        bank = a.bank(kind, i)
        was = a.before(t, u, kind, i)
        if was is not None:
            for name, per, n in a.emptied(*was[:2]):
                if (due := s[name].due(t, lambda x: (x + was[2]) * per + n)) is not None:
                    pe.wait_ge(s[name].sem, due)
        if kind == "T":
            if a.ctx_norm:
                pe.wait_ge(s["cn"].sem, s["cn"].at(b, lambda x: x + 1))
            elif a.kind == "cross":
                pe.wait_ge(s["ctx_in"].sem, s["ctx_in"].at(b, lambda x: 16 * (x + 1)))
            pe.wait_ge(s["wn"].sem, s["wn"].at(b, lambda x: x + 1))
            for blk in range(SB):
                last = pe.transpose(bank[:, blk * P:(blk + 1) * P], k.wn[:, b.parity, blk], k.ident[:, :])
            if a.kind == "cross":
                src = k.cn if a.ctx_norm else k.ctx_in
                last = pe.transpose(bank[0:CC, 256:256 + TC], src[:, b.parity], k.ident[0:TC, 0:TC])
            last.then_inc(s["t_full"].sem, 1)
        if kind == "Q":
            pe.wait_ge(s["side"].sem, s["side"].at(b, lambda x: x + 1))
            pe.matmul(bank[:, 0:S], w["wq"][:, i * P:(i + 1) * P], k.xq[:, b.parity], start=True, stop=True)
            keys = k.xq[:, b.parity] if a.one_side else k.xk[:, b.parity] if a.kind == "self" else k.xc[:, b.parity, 0]
            pe.matmul(a.keys_bank(i)[:, S:S + a.T], w["wk"][:, i * P:(i + 1) * P], keys, start=True, stop=True)\
              .then_inc(s["qk_full"].sem, 1)
        if kind == "V":
            pe.wait_ge(s["side"].sem, s["side"].at(b, lambda x: x + 1))
            keys = k.xq if a.one_side else k.xk
            if a.kind == "cross":
                last = pe.matmul(bank[:, 0:a.G * P], k.xc[:, b.parity].rearrange("c h t -> c (h t)"), w["wv"][:, :],
                                 start=True, stop=True)
            elif a.G == 4:
                last = pe.matmul(bank[:, :], keys[:, b.parity, i * P:(i + 1) * P], w["wv"][:, :], start=True, stop=True)
            else:
                for blk in range(SB):
                    last = pe.matmul(bank[:, blk * P:(blk + 1) * P], keys[:, b.parity, blk * P:(blk + 1) * P],
                                     w["wv"][:, :], start=True, stop=True)
            last.then_inc(s["v_full"].sem, 1)
        if kind == "R":
            pe.wait_ge(s["rx"].sem, s["rx"].at(b, lambda x: x + 1))
            for blk in range(SB):
                last = pe.transpose(bank[:, blk * P:(blk + 1) * P], k.rx[:, blk, i * P:(i + 1) * P], k.ident[:, :])
            last.then_inc(s["r_full"].sem, 1)
        if kind == "Y":
            pe.wait_ge(s["ot"].sem, s["ot"].at(b, lambda x: a.G * (x + 1)))
            for blk in range(SB):
                for g in range(a.G):
                    last = pe.matmul(bank[:, blk * P:(blk + 1) * P], k.ot[:, g, blk * P:(blk + 1) * P],
                                     w["wo"][:, g], start=(g == 0), stop=(g == a.G - 1))
            last.then_inc(s["y_full"].sem, 1)

    def pieces(t, u, reciprocals):
        for kind, i, b in a.in_slot(t, u):
            if (kind == "R") == reciprocals:
                piece(t, u, kind, i, b)

    def self_scores(b, u):
        U = lambda x: UNITS * x + u
        if (due := s["exp_done"].due(b, lambda x: U(x) - 1)) is not None:
            pe.wait_ge(s["exp_done"].sem, due)
        g0 = a.head(2 * u) // a.HG
        pe.wait_ge(s["q_ready"].sem, s["q_ready"].at(b, lambda x: a.G * x + g0 + 1))
        pe.wait_ge(s["km_ready"].sem, s["km_ready"].at(b, lambda x: UNITS * x + u + 1))
        pe.wait_ge(s["odd_km_ready"].sem, s["odd_km_ready"].at(b, lambda x: UNITS * x + u + 1))
        for n in range(2):
            h = a.head(2 * u + n)
            bank = k.scores[u % 2][:, n * 512:(n + 1) * 512]
            for blk in range(SB):
                q = k.qT[:, b.parity, h // a.HG, blk * P:(blk + 1) * P]
                if a.mask == "before":
                    cols = (0, P) if blk == 0 else (P, 3 * P)
                    pe.matmul(bank[:, cols[0]:cols[1]], q, k.km[:, b.parity, h, 0:cols[1] - cols[0]],
                              start=True, stop=False, skip_group_check=True)
                    last = pe.matmul(bank[:, cols[1] - P:cols[1]], k.identb[:, :], k.above[:, :],
                                     start=False, stop=True, skip_group_check=True)
                else:
                    last = pe.matmul(bank[:, blk * S:(blk + 1) * S], q, k.km[:, b.parity, h], start=True, stop=True)
        last.then_inc(s["s_full"].sem, 1)

    def self_turn(b, u):
        probs_done = s["masked" if a.mask == "after" else "exp_done"]
        pe.wait_ge(probs_done.sem, probs_done.at(b, lambda x: UNITS * x + u + 1))
        for n in range(2):
            hd = 2 * u + n
            copied = s["odd_pt_ready" if n else "pt_ready"]
            if (due := copied.due(b, lambda x: H // 2 * x + u)) is not None:
                pe.wait_ge(copied.sem, due)
            blocks = (0, 1, 3) if a.mask == "after" else (0, 1, 2)
            for o, blk in enumerate(blocks):
                last = pe.transpose(k.turned[hd % 2][:, o * P:(o + 1) * P], k.probs[:, u % 2, n, blk * P:(blk + 1) * P],
                                    k.ident[:, :])
            last.then_inc(s["tr_full"].sem, 1)

    def self_values(b, q):
        pe.wait_ge(s["pt_ready"].sem, s["pt_ready"].at(b, lambda x: H // 2 * x + 2 * q + 2))
        pe.wait_ge(s["odd_pt_ready"].sem, s["odd_pt_ready"].at(b, lambda x: H // 2 * x + 2 * q + 2))
        pe.wait_ge(s["v_ready"].sem, s["v_ready"].at(b, lambda x: a.nv * (x + 1)))
        r = a.regions
        reg = q if r > 1 else 0
        if (due := s["num_saved"].due(b, lambda x: r * x + reg)) is not None:
            pe.wait_ge(s["num_saved"].sem, due)
        half = (q % 2 if r > 1 else b.parity) * S
        pt = lambda n, lo, hi: k.pt[:, 4 * (q % 2) + n, lo * P:hi * P]
        first = r > 1 or q == 0
        for part in range(2):
            for n in range(4):
                h = a.head(4 * q + n)
                out = k.num[32 * n:32 * n + 32]
                tb = part if a.mask == "before" else 1 - part
                v = k.val[:, b.parity, tb, 32 * h:32 * h + 32]
                if a.mask == "before":
                    out, p = (out[:, half:half + S], pt(n, 0, 2)) if part == 0 else (out[:, half + P:half + S], pt(n, 2, 3))
                else:
                    out, p = (out[:, half:half + S], pt(n, 1, 3)) if part == 0 else (out[:, half:half + P], pt(n, 0, 1))
                last = pe.matmul(out, v, p, start=(first and part == 0), stop=(part == 1), skip_group_check=True)
        last.then_inc(s["pv_done"].sem, 1)

    def cross_scores(b, c):
        if (due := s["exp_done"].due(b, lambda x: 4 * x + c - 1)) is not None:
            pe.wait_ge(s["exp_done"].sem, due)
        half, blk = c // 2, c % 2
        g1 = min(a.G - 1, 2 * half + 1)
        pe.wait_ge(s["q_ready"].sem, s["q_ready"].at(b, lambda x: a.G * x + g1 + 1))
        parts = half + 1 if a.G == 1 else g1 + 1
        pe.wait_ge(s["km_ready"].sem, s["km_ready"].at(b, lambda x: a.G * a.halves * x + parts))
        bank = k.scores[0][:, (c % 2) * 512:(c % 2 + 1) * 512]
        for i in range(2 if a.G == 4 else 1):
            g = 2 * half + i if a.G == 4 else 0
            hs = 4 if a.G == 4 else 8
            h0 = 8 * half + hs * i
            last = pe.matmul(bank[:, i * hs * TC:(i + 1) * hs * TC], k.qT[:, b.parity, g, blk * P:(blk + 1) * P],
                             k.km_cross[:, b.parity, h0 * TC:(h0 + hs) * TC], start=True, stop=True)
        last.then_inc(s["s_full"].sem, 1)

    def cross_turn(b, c):
        pe.wait_ge(s["exp_done"].sem, s["exp_done"].at(b, lambda x: 4 * x + c + 1))
        if (due := s["pt_ready"].due(b, lambda x: 4 * x + c - 1)) is not None:
            pe.wait_ge(s["pt_ready"].sem, due)
        for p in range(4):
            last = pe.transpose(k.turned[c % 2][:, p * P:(p + 1) * P], k.pc[:, c % 2, p * P:(p + 1) * P], k.ident[:, :])
        last.then_inc(s["tr_full"].sem, 1)

    def cross_values(b, half):
        pe.wait_ge(s["pt_ready"].sem, s["pt_ready"].at(b, lambda x: 4 * x + 2 * half + 2))
        pe.wait_ge(s["v_ready"].sem, s["v_ready"].at(b, lambda x: x + 1))
        if a.G == 4:
            if (due := s["num_saved"].due(b, lambda x: 4 * x + 2 * half)) is not None:
                pe.wait_ge(s["num_saved"].sem, due)
            for g in range(2):
                for p in range(2):
                    pair = 4 * half + 2 * g + p
                    last = pe.matmul(k.num[:, g * S:(g + 1) * S], k.vb[:, b.parity, pair], k.ptc[:, half, 2 * g + p],
                                     start=(p == 0), stop=(p == 1), skip_group_check=True)
        else:
            if (due := s["num_saved"].due(b, lambda x: x)) is not None:
                pe.wait_ge(s["num_saved"].sem, due)
            for p in range(4):
                last = pe.matmul(k.num[:, b.parity * S:(b.parity + 1) * S], k.vb[:, b.parity, 4 * half + p],
                                 k.ptc[:, half, p], start=(half == 0 and p == 0), stop=(half == 1 and p == 3),
                                 skip_group_check=True)
        last.then_inc(s["pv_done"].sem, 1)

    for _, kind, i, b in a.pieces(-1):
        piece(Step(-1), _, kind, i, Step(b))
    scores, turn, values = ((self_scores, self_turn, self_values) if a.kind == "self" else
                            (cross_scores, cross_turn, cross_values))
    n = a.nslots
    for u in range(2):
        scores(Step(0), u)

    def body(t):
        last = t.reg is None and t.n == B - 1
        first = t.reg is None and t.n == 0
        for u in range(n):
            turn(t, u)
            if a.kind == "cross":
                pieces(t, u, True)
                pieces(t, u, False)
            if u + 2 < n:
                scores(t, u + 2)
            elif not last:
                scores(t + 1, u + 2 - n)
            if a.kind == "self":
                pieces(t, u, True)
            if u % 2 == 0 and not (first and u == 0):
                values(t + (-1 if u == 0 else 0), (u // 2 - 1) % (n // 2))
            if a.kind == "self":
                pieces(t, u, False)

    pipeline(pe, B, body)
    values(Step(B - 1), n // 2 - 1)
    for u in range(n):
        pieces(Step(B), u, True)
        pieces(Step(B), u, False)



def scalar_attention(act, a):
    k, s, w = a.k, a.s, a.w

    def piece(kind, i, b):
        bank = a.bank(kind, i)
        if kind == "Q":
            act.wait_ge(s["qk_full"].sem, s["qk_full"].at(b, lambda x: a.G * x + i + 1))
            last_use = (lambda x: UNITS * (x - 1)) if a.kind == "self" else (lambda x: 4 * (x - 1))
            if (due := s["s_full"].due(b, last_use)) is not None:
                act.wait_ge(s["s_full"].sem, due)
            if a.kind == "self":
                act.wait_ge(s["k_out"].sem, s["k_out"].at(b, lambda x: a.G * x + i + 1))
            act.activation(k.qT[:, b.parity, i], bank[:, 0:S], ACT.Identity, bias=w["q_bias"] if w["q_bias"] is not None else 0.0,
                           scale=a.scale).then_inc(s["q_ready"].sem, 1)
        if kind == "V" and a.kind == "self" and a.G == 4:
            act.wait_ge(s["v_full"].sem, s["v_full"].at(b, lambda x: 2 * x + i + 1))
            if (due := s["pv_done"].due(b, lambda x: QUADS * (x - 1))) is not None:
                act.wait_ge(s["pv_done"].sem, due)
            act.copy(k.val[:, b.parity, i], bank[:, :]).then_inc(s["v_ready"].sem, 1)

    def self_exp(b, u):
        act.wait_ge(s["max_ready"].sem, s["max_ready"].at(b, lambda x: UNITS * x + u + 1))
        if (due := s["tr_full"].due(b, lambda x: H * x + 2 * (u - 1))) is not None:
            act.wait_ge(s["tr_full"].sem, due)
        if (due := s["rden"].due(b, lambda x: x - 1)) is not None:
            act.wait_ge(s["rden"].sem, due)
        for n in range(2):
            h = a.head(2 * u + n)
            for blk in range(SB):
                if a.mask == "before":
                    lo, hi = (0, P) if blk == 0 else (P, 3 * P)
                else:
                    lo, hi = blk * S, (blk + 1) * S
                last = act.activation(k.probs[:, u % 2, n, lo:hi], k.scores[u % 2][:, n * 512 + lo:n * 512 + hi], ACT.Exp,
                                      bias=k.nmax[:, u % 2, 2 * n + blk:2 * n + blk + 1], scale=1.0,
                                      accum_out=k.sums[:, b.parity, blk, h:h + 1])
        last.then_inc(s["exp_done"].sem, 1)

    def own_keys(b, v):
        act.wait_ge(s["k_out"].sem, s["k_out"].at(b, lambda x: a.G * x + a.group(v) + 1))
        if (due := s["s_full"].due(b, lambda x: UNITS * (x - 2) + v + 1)) is not None:
            act.wait_ge(s["s_full"].sem, due)
        h = a.head(2 * v + 1)
        act.mul(k.km[:, b.parity, h], k.kT[:, a.keys_at(b, a.group(v))], w["own"][:, h % a.HG:h % a.HG + 1])\
            .then_inc(s["odd_km_ready"].sem, 1)

    def self_copy(b, u):
        act.wait_ge(s["tr_full"].sem, s["tr_full"].at(b, lambda x: H * x + 2 * u + 2))
        if (due := s["pv_done"].due(b, lambda x: QUADS * x + u // 2 - 1)) is not None:
            act.wait_ge(s["pv_done"].sem, due)
        act.copy(k.pt[:, (2 * u + 1) % 8], k.turned[1][:, 0:3 * P]).then_inc(s["odd_pt_ready"].sem, 1)

    def cross_exp(b, c):
        act.wait_ge(s["max_ready"].sem, s["max_ready"].at(b, lambda x: 4 * x + c + 1))
        if (due := s["tr_full"].due(b, lambda x: 4 * x + c - 1)) is not None:
            act.wait_ge(s["tr_full"].sem, due)
        if (due := s["rden"].due(b, lambda x: x - 1)) is not None:
            act.wait_ge(s["rden"].sem, due)
        for h in range(8):
            at = c % 2 * 512 + h * TC
            last = act.activation(k.pc[:, c % 2, h * TC:(h + 1) * TC], k.scores[0][:, at:at + TC], ACT.Exp,
                                  bias=k.cmax[:, c % 2, h:h + 1], scale=1.0,
                                  accum_out=k.sums[:, b.parity, c % 2, 8 * (c // 2) + h:8 * (c // 2) + h + 1])
        last.then_inc(s["exp_done"].sem, 1)

    def save(b, q):
        if a.regions > 1:
            n, per = (1, 4) if a.kind == "self" else (2, 2)
            act.wait_ge(s["pv_done"].sem, s["pv_done"].at(b, lambda x: per * x + q + 1))
            if (due := s["ot"].due(b, lambda x: 4 * (x - 1))) is not None:
                act.wait_ge(s["ot"].sem, due)
            half = (q % 2) * S if a.kind == "self" else 0
            act.copy(k.numS[:, b.parity, n * q:n * (q + 1)], k.num[:, half:half + n * S].rearrange("p (g t) -> p g t", g=n))\
               .then_inc(s["num_saved"].sem, n)
        elif q == (3 if a.kind == "self" else 1):
            act.wait_ge(s["pv_done"].sem, s["pv_done"].at(b, lambda x: (q + 1) * (x + 1)))
            if (due := s["ot"].due(b, lambda x: x - 1)) is not None:
                act.wait_ge(s["ot"].sem, due)
            act.copy(k.numS[:, b.parity, 0], k.num[:, b.parity * S:(b.parity + 1) * S]).then_inc(s["num_saved"].sem, 1)

    exps = self_exp if a.kind == "self" else cross_exp
    n = a.nslots
    for _, kind, i, b in a.pieces(-1):
        piece(kind, i, Step(b))
    if a.kind == "self":
        for v in range(n // 2):
            own_keys(Step(0), v)
    for u in range(2):
        exps(Step(0), u)

    def body(t):
        last = t.reg is None and t.n == B - 1
        first = t.reg is None and t.n == 0
        for u in range(n):
            if a.kind == "self":
                self_copy(t, u)
            if a.kind == "cross":
                for kind, i, b in a.in_slot(t, u):
                    piece(kind, i, b)
            if u + 2 < n:
                exps(t, u + 2)
            elif not last:
                exps(t + 1, u + 2 - n)
            if u % 2 == 0 and not (first and u == 0):
                save(t + (-1 if u == 0 else 0), (u // 2 - 1) % (n // 2))
            if a.kind == "self":
                for kind, i, b in a.in_slot(t, u):
                    piece(kind, i, b)
            if a.kind == "self" and (u < n // 2 or not last):
                own_keys(t if u < n // 2 else t + 1, (u + n // 2) % n)

    pipeline(act, B, body)
    save(Step(B - 1), n // 2 - 1)
    for u in range(n):
        for kind, i, b in a.in_slot(Step(B), u):
            piece(kind, i, b)



def vector_norm_stats(dve, k, s, x, stats, aggr, names, b, blocks):
    for blk in range(blocks):
        last = dve.bn_stats(stats[:, blk], x[:, blk])
    last.then_inc(s[names[0]].sem, 1)
    dve.wait_ge(s[names[0]].sem, s[names[0]].at(b, lambda t: t + 1))
    apart(dve, k, b)
    for blk in range(blocks):
        last = dve.bn_aggr(aggr[:, blk], stats[:, blk])
    last.then_inc(s[names[1]].sem, 1)


def attention_norm(dve, a):
    k, s = a.k, a.s

    def norm_stats(b):
        dve.wait_ge(s["x_in"].sem, s["x_in"].at(b, lambda t: 16 * (t + 1)))
        vector_norm_stats(dve, k, s, k.x_in[:, b.parity], k.stats[:, b.parity], k.aggr[:, b.parity], ("stats", "aggr"), b, SB)
        if a.ctx_norm:
            dve.wait_ge(s["ctx_in"].sem, s["ctx_in"].at(b, lambda t: 16 * (t + 1)))
            vector_norm_stats(dve, k, s, k.ctx_in[:, b.parity].unsqueeze(1), k.cstats[:, b.parity], k.caggr[:, b.parity],
                              ("cstats", "caggr"), b, 1)

    def norm(b):
        dve.wait_ge(s["rstd"].sem, s["rstd"].at(b, lambda t: t + 1))
        if (due := s["t_full"].due(b, lambda t: t - 1)) is not None:
            dve.wait_ge(s["t_full"].sem, due)
        for blk in range(SB):
            last = dve.tensor_scalar(k.wn[:, b.parity, blk], k.x_in[:, b.parity, blk], k.aggr[:, b.parity, blk, 0:1],
                                     k.rstd[:, b.parity, blk:blk + 1], ALU.subtract, ALU.mult)
        last.then_inc(s["wn"].sem, 1)
        if a.ctx_norm:
            dve.wait_ge(s["crstd"].sem, s["crstd"].at(b, lambda t: t + 1))
            dve.tensor_scalar(k.cn[:, b.parity], k.ctx_in[:, b.parity], k.caggr[:, b.parity, 0, 0:1],
                              k.crstd[:, b.parity, 0:1], ALU.subtract, ALU.mult).then_inc(s["cn"].sem, 1)

    return norm_stats, norm


def vector_ahead(dve, part, norms):
    norm_stats, norm = norms(dve, part)
    for b in range(2):
        norm_stats(Step(b))
        norm(Step(b))


def vector_attention(dve, a):
    k, s, w = a.k, a.s, a.w

    norm_stats, norm = attention_norm(dve, a)

    def piece(kind, i, b):
        bank = a.bank(kind, i)
        if kind == "T":
            dve.wait_ge(s["t_full"].sem, s["t_full"].at(b, lambda x: x + 1))
            if (due := s["qk_full"].due(b, lambda x: a.G * (x - 1))) is not None:
                dve.wait_ge(s["qk_full"].sem, due)
            if (due := s["v_full"].due(b, lambda x: a.nv * (x - 1))) is not None:
                dve.wait_ge(s["v_full"].sem, due)
            if w["q_gain"] is None:
                last = dve.tensor_copy(k.xq[:, b.parity], bank[:, 0:S])
            else:
                last = dve.tensor_scalar(k.xq[:, b.parity], bank[:, 0:S], w["q_gain"], w["q_shift"], ALU.mult, ALU.add)
            if a.kind == "self" and not a.one_side:
                last = dve.tensor_scalar(k.xk[:, b.parity], bank[:, 0:S], w["k_gain"], w["k_shift"], ALU.mult, ALU.add)
            if a.kind == "cross":
                both = bank[0:CC, S:S + TC].unsqueeze(1).to_broadcast([CC, 2, TC])
                if w["k_gain"] is None:
                    last = dve.tensor_copy(k.xc[:, b.parity], both)
                else:
                    last = dve.tensor_scalar(k.xc[:, b.parity], both, w["k_gain"], w["k_shift"], ALU.mult, ALU.add)
            last.then_inc(s["side"].sem, 1)
        if kind == "Q":
            if a.kind == "cross" and a.G > 1:
                dve.wait_ge(s["q_ready"].sem, s["q_ready"].at(b, lambda x: a.G * x + i + 1))
            dve.wait_ge(s["qk_full"].sem, s["qk_full"].at(b, lambda x: a.G * x + i + 1))
            last_use = (lambda x: UNITS * (x - 1)) if a.kind == "self" else (lambda x: 4 * (x - 1))
            if (due := s["s_full"].due(b, last_use)) is not None:
                dve.wait_ge(s["s_full"].sem, due)
            if a.kind == "self":
                used = lambda x: UNITS * (x - 1) + (0 if a.G == 1 else 2 * i + 2)
                if (due := s["km_ready"].due(b, used)) is not None:
                    dve.wait_ge(s["km_ready"].sem, due)
                if (due := s["odd_km_ready"].due(b, used)) is not None:
                    dve.wait_ge(s["odd_km_ready"].sem, due)
                out, keys = k.kT[:, a.keys_at(b, i)], bank[:, S:S + a.T]
                last = (dve.tensor_copy(out, keys) if w["k_bias"] is None else
                        dve.tensor_scalar(out, keys, w["k_bias"], None, ALU.add))
                last.then_inc(s["k_out"].sem, 1)
                return
            for h in range(0, a.HG, a.HG // a.halves):
                n = a.HG // a.halves
                h0 = a.HG * i + h
                out = k.km_cross[:, b.parity, h0 * TC:(h0 + n) * TC].rearrange("p (h t) -> p h t", t=TC)
                keys = a.keys_bank(i)[:, S:S + TC].unsqueeze(1).to_broadcast([P, n, TC])
                own = w["own"][:, h:h + n].unsqueeze(2).to_broadcast([P, n, TC])
                if w["k_bias"] is None:
                    last = dve.tensor_tensor(out, keys, own, ALU.mult)
                else:
                    last = dve.scalar_tensor_tensor(out=out, in0=keys, scalar=w["k_bias"], in1=own, op0=ALU.add, op1=ALU.mult)
                last.then_inc(s["km_ready"].sem, 1)
        if kind == "V" and a.kind == "self" and a.G == 1:
            dve.wait_ge(s["v_full"].sem, s["v_full"].at(b, lambda x: x + 1))
            if (due := s["pv_done"].due(b, lambda x: QUADS * (x - 1))) is not None:
                dve.wait_ge(s["pv_done"].sem, due)
            for blk in range(SB):
                last = dve.tensor_tensor(
                    k.val[:, b.parity, blk].rearrange("p (r j c) -> p r j c", r=4, c=32),
                    bank[:, blk * P:(blk + 1) * P].rearrange("p (r c) -> p r c", r=4).unsqueeze(2).to_broadcast([P, 4, 4, 32]),
                    k.own_columns[:, :, :].unsqueeze(1).to_broadcast([P, 4, 4, 32]), ALU.mult)
            last.then_inc(s["v_ready"].sem, 1)
        if kind == "V" and a.kind == "cross":
            dve.wait_ge(s["v_full"].sem, s["v_full"].at(b, lambda x: x + 1))
            if (due := s["pv_done"].due(b, lambda x: 2 * (x - 1))) is not None:
                dve.wait_ge(s["pv_done"].sem, due)
            if a.G == 1:
                last = dve.tensor_tensor(k.vb[:, b.parity], bank[:, 0:P].unsqueeze(1).to_broadcast([P, 8, P]),
                                         w["own_pair"], ALU.mult)
            else:
                last = dve.tensor_tensor(k.vb[:, b.parity].rearrange("p (g j) c -> p g j c", g=4),
                                         bank[:, :].rearrange("p (g c) -> p g c", g=4).unsqueeze(2).to_broadcast([P, 4, 2, P]),
                                         w["own_pair"].rearrange("p (g j) c -> p g j c", g=4), ALU.mult)
            last.then_inc(s["v_ready"].sem, 1)
        if kind == "R":
            dve.wait_ge(s["r_full"].sem, s["r_full"].at(b, lambda x: a.G * x + i + 1))
            if (due := s["num_saved"].due(b, lambda x: a.regions * x + min(i, a.regions - 1) + 1)) is not None:
                dve.wait_ge(s["num_saved"].sem, due)
            if (due := s["y_full"].due(b, lambda x: x)) is not None:
                dve.wait_ge(s["y_full"].sem, due)
            dve.tensor_tensor(k.ot[:, i], bank[:, 0:S], k.numS[:, b.parity, i], ALU.mult).then_inc(s["ot"].sem, 1)
        if kind == "Y":
            dve.wait_ge(s["y_full"].sem, s["y_full"].at(b, lambda x: x + 1))
            dve.wait_ge(s["biased"].sem, s["biased"].at(b, lambda x: x + 1))
            if (due := s["stored"].due(b, lambda x: 16 * (x - 1))) is not None:
                dve.wait_ge(s["stored"].sem, due)
            dve.tensor_tensor(k.res[:, b.parity].rearrange("p k c -> p (k c)"), bank[:, 0:S],
                              k.base_sum[:, b.parity].rearrange("p k c -> p (k c)"), ALU.add).then_inc(s["res"].sem, 1)

    def own_keys(b, v):
        dve.wait_ge(s["k_out"].sem, s["k_out"].at(b, lambda x: a.G * x + a.group(v) + 1))
        if (due := s["s_full"].due(b, lambda x: UNITS * (x - 2) + v + 1)) is not None:
            dve.wait_ge(s["s_full"].sem, due)
        h = a.head(2 * v)
        own = w["own"][:, h % a.HG:h % a.HG + 1]
        dve.tensor_scalar(k.km[:, b.parity, h], k.kT[:, a.keys_at(b, a.group(v))], own, None, ALU.mult)\
           .then_inc(s["km_ready"].sem, 1)

    def self_max(b, u):
        dve.wait_ge(s["s_full"].sem, s["s_full"].at(b, lambda x: UNITS * x + u + 1))
        if (due := s["exp_done"].due(b, lambda x: UNITS * x + u - 1)) is not None:
            dve.wait_ge(s["exp_done"].sem, due)
        bank = k.scores[u % 2][:, :].rearrange("p (n t) -> p n t", n=2)
        out = k.nmax[:, u % 2].rearrange("p (n k) -> p n k", n=2)
        if a.mask == "before":
            dve.tensor_reduce(out[:, :, 0:1], bank[:, :, 0:P], AX.X, ALU.max, negate=True)
            last = dve.tensor_reduce(out[:, :, 1:2], bank[:, :, P:3 * P], AX.X, ALU.max, negate=True)
        else:
            last = dve.tensor_reduce(k.nmax[:, u % 2], k.scores[u % 2][:, :].rearrange("p (n t) -> p n t", n=4),
                                     AX.X, ALU.max, negate=True)
        last.then_inc(s["max_ready"].sem, 1)

    def self_copy(b, u):
        dve.wait_ge(s["tr_full"].sem, s["tr_full"].at(b, lambda x: H * x + 2 * u + 1))
        if (due := s["pv_done"].due(b, lambda x: QUADS * x + u // 2 - 1)) is not None:
            dve.wait_ge(s["pv_done"].sem, due)
        dve.tensor_copy(k.pt[:, 2 * u % 8], k.turned[0][:, 0:3 * P]).then_inc(s["pt_ready"].sem, 1)

    def cross_max(b, c):
        dve.wait_ge(s["s_full"].sem, s["s_full"].at(b, lambda x: 4 * x + c + 1))
        if (due := s["exp_done"].due(b, lambda x: 4 * x + c - 1)) is not None:
            dve.wait_ge(s["exp_done"].sem, due)
        scores = k.scores[0][:, (c % 2) * 512:(c % 2 + 1) * 512].rearrange("p (h t) -> p h t", t=TC)
        dve.tensor_reduce(k.cmax[:, c % 2], scores, AX.X, ALU.max, negate=True).then_inc(s["max_ready"].sem, 1)

    def cross_copy(b, c):
        dve.wait_ge(s["tr_full"].sem, s["tr_full"].at(b, lambda x: 4 * x + c + 1))
        if (due := s["pv_done"].due(b, lambda x: 2 * (x - 1) + c // 2 + 1)) is not None:
            dve.wait_ge(s["pv_done"].sem, due)
        dve.tensor_copy(k.ptc[:, c // 2, :, (c % 2) * P:(c % 2 + 1) * P],
                        k.turned[c % 2][:, :].rearrange("p (j t) -> p j t", j=4)).then_inc(s["pt_ready"].sem, 1)

    def reciprocals(b):
        dve.wait_ge(s["exp_done"].sem, s["exp_done"].at(b, lambda x: a.nslots * (x + 1)))
        dve.reciprocal(k.rsum[:, b.parity], k.sums[:, b.parity]).then_inc(s["rden"].sem, 1)
        dve.wait_ge(s["rden"].sem, s["rden"].at(b, lambda x: x + 1))
        if (due := s["r_full"].due(b, lambda x: a.G * x)) is not None:
            dve.wait_ge(s["r_full"].sem, due)
        for blk in range(SB):
            last = dve.tensor_copy(k.rx[:, blk, 0:H * a.D].rearrange("p (h d) -> p h d", d=a.D),
                                   k.rsum[:, b.parity, blk].unsqueeze(2).to_broadcast([P, H, a.D]))
        last.then_inc(s["rx"].sem, 1)

    exists = lambda t, ahead: t.reg is not None or t.n + ahead < B
    for _, kind, i, b in a.pieces(-1):
        piece(kind, i, Step(b))
    if a.kind == "self":
        for v in range(a.nslots // 2):
            own_keys(Step(0), v)
    top = self_max if a.kind == "self" else cross_max
    for u in range(2):
        top(Step(0), u)

    def body(t):
        n = a.nslots
        for u in range(n):
            if u == n - 1:
                reciprocals(t)
            if a.kind == "self":
                self_copy(t, u)
            else:
                cross_copy(t, u)
            for kind, i, b in a.in_slot(t, u):
                if kind == "R" or a.kind == "cross":
                    piece(kind, i, b)
            if u + 2 < n or exists(t, 1):
                b, v = (t, u + 2) if u + 2 < n else (t + 1, u + 2 - n)
                top(b, v)
            for kind, i, b in a.in_slot(t, u):
                if kind != "R" and a.kind == "self":
                    piece(kind, i, b)
            if a.kind == "self" and (u < n // 2 or exists(t, 1)):
                own_keys(t if u < n // 2 else t + 1, (u + n // 2) % n)
            if u == n - 2 and exists(t, 2):
                norm_stats(t + 2)
            if u == n - 1 and exists(t, 2):
                norm(t + 2)

    pipeline(dve, B, body)
    for u in range(a.nslots):
        for kind, i, b in a.in_slot(Step(B), u):
            piece(kind, i, b)



def attention_rstd(pool, a):
    k, s = a.k, a.s

    def rstd(b):
        pool.wait_ge(s["aggr"].sem, s["aggr"].at(b, lambda t: t + 1))
        if (due := s["wn"].due(b, lambda t: t - 1)) is not None:
            pool.wait_ge(s["wn"].sem, due)
        pool.tensor_tensor(k.vareps[:, b.parity], k.aggr[:, b.parity, :, 1], k.eps[:, 0:SB], ALU.add)\
            .then_inc(s["eps_in"].sem, 1)
        pool.wait_ge(s["eps_in"].sem, s["eps_in"].at(b, lambda t: t + 1))
        pool.tensor_tensor(k.rstd[:, b.parity], k.vareps[:, b.parity], k.minus_half[:, 0:SB], ALU.pow).then_inc(s["rstd"].sem, 1)
        if a.ctx_norm:
            pool.wait_ge(s["caggr"].sem, s["caggr"].at(b, lambda t: t + 1))
            if (due := s["cn"].due(b, lambda t: t - 1)) is not None:
                pool.wait_ge(s["cn"].sem, due)
            pool.tensor_tensor(k.cvareps[:, b.parity], k.caggr[:, b.parity, :, 1], k.eps[0:TC, 0:1], ALU.add)\
                .then_inc(s["ceps"].sem, 1)
            pool.wait_ge(s["ceps"].sem, s["ceps"].at(b, lambda t: t + 1))
            pool.tensor_tensor(k.crstd[:, b.parity], k.cvareps[:, b.parity], k.minus_half[0:TC, 0:1], ALU.pow)\
                .then_inc(s["crstd"].sem, 1)

    return rstd


def gpsimd_ahead(pool, part, powers):
    rstd = powers(pool, part)
    rstd(Step(0))
    rstd(Step(1))


def gpsimd_attention(pool, a):
    k, s, w = a.k, a.s, a.w

    rstd = attention_rstd(pool, a)

    def bias(b):
        pool.wait_ge(s["base_in"].sem, s["base_in"].at(b, lambda t: 16 * (t + 1)))
        if (due := s["res"].due(b, lambda t: t - 1)) is not None:
            pool.wait_ge(s["res"].sem, due)
        pool.tensor_tensor(k.base_sum[:, b.parity], k.base_in[:, b.parity],
                           w["o_bias"].unsqueeze(1).to_broadcast([P, SB, C]), ALU.add).then_inc(s["biased"].sem, 1)

    def mask(b, u):
        pool.wait_ge(s["exp_done"].sem, s["exp_done"].at(b, lambda x: UNITS * x + u + 1))
        apart(pool, k, b)
        for n in range(2):
            blocks = k.probs[:, u % 2, n].rearrange("p (q t) -> p q t", t=P)[:, 0:4:3]
            last = pool.affine_select(out=blocks, in_=blocks, compare_op=ALU.is_ge, fill=0.0, base=-1,
                                      pattern=[[0, 2], [1, P]], channel_multiplier=-1)
        last.then_inc(s["masked"].sem, 1)

    exists = lambda t, ahead: t.reg is not None or t.n + ahead < B
    if a.constants_ahead is not None:
        a.constants_ahead(pool)
    if a.mask == "after":
        for u in range(2):
            mask(Step(0), u)

    def body(t):
        n = a.nslots
        bias(t)
        for u in range(n):
            if a.mask == "after" and (u + 2 < n or exists(t, 1)):
                mask(t if u + 2 < n else t + 1, u + 2 if u + 2 < n else u + 2 - n)
            if u == n - 2 and exists(t, 2):
                rstd(t + 2)

    pipeline(pool, B, body)



class Mlp:

    def __init__(self, k, name, src, also, after, dst, keep, start, w):
        self.k, self.name, self.src, self.also, self.after = k, name, src, also, after
        self.dst, self.keep, self.start, self.w = dst, keep, start, w
        each = dict(x_in=16, stored=16, stats=1, aggr=1, eps_in=1, rstd=1, wn=1, t_full=1, xt=1, h_full=FC, gelu=FC,
                    y_full=1, biased=1, r=1, out=1)
        if after == "norm":
            each.update(rstats=1, raggr=1, reps=1, rrstd=1, rn=1, gained=1)
        if after == "route":
            each.update(rstats=1, raggr=1, reps=1, rrstd=1, rn=1, rt_full=1, rxt=1, g_full=1, logits=1, rows_kept=1)
        if keep is not None:
            each.update(kept=16)
        if also is not None:
            each.update(both=1, also_in=16)
        if start is not None:
            each.update(start_in=16)
        self.s = k.signals(each, MSTEPS)


def mlp_rows(x, row):
    return x.rearrange("(m n) s c -> m (n s) c", n=MT // S)[row].rearrange("(k p) c -> p k c", p=P)


def mlp_load(sp, m):
    k, s = m.k, m.s

    def load(t):
        row = t.row(sp)
        if (due := s["x_in"].due(t, lambda x: 16 * x)) is not None:
            sp.wait_ge(s["x_in"].sem, due)
            apart(sp, k, t)
        if (due := s["biased"].due(t, lambda x: x - 1)) is not None:
            sp.wait_ge(s["biased"].sem, due)
            apart(sp, k, t)
        if (due := s["wn"].due(t, lambda x: x - 1)) is not None:
            sp.wait_ge(s["wn"].sem, due)
            apart(sp, k, t)
        sp.dma_start(k.mx[:, t.parity], mlp_rows(m.src, row)).then_inc(s["x_in"].sem, 16)

    return load


def sync_mlp_ahead(sp, m):
    load = mlp_load(sp, m)
    load(Step(0))
    load(Step(1))


def sync_mlp(sp, m, ahead):
    k, s = m.k, m.s

    load = mlp_load(sp, m)

    def load_also(t):
        row = t.row(sp)
        if (due := s["also_in"].due(t, lambda x: 16 * x)) is not None:
            sp.wait_ge(s["also_in"].sem, due)
            apart(sp, k, t)
        sp.dma_start(k.malso[:, t.parity], mlp_rows(m.also, row)).then_inc(s["also_in"].sem, 16)

    def load_start(t):
        row = t.row(sp)
        if (due := s["start_in"].due(t, lambda x: 16 * x)) is not None:
            sp.wait_ge(s["start_in"].sem, due)
            apart(sp, k, t)
        if (due := s["out"].due(t, lambda x: x - 1)) is not None:
            sp.wait_ge(s["out"].sem, due)
            apart(sp, k, t)
        sp.dma_start(k.mstart[:, t.parity], mlp_rows(m.start, row)).then_inc(s["start_in"].sem, 16)

    def store(t):
        row = t.row(sp)
        if m.keep is not None:
            if (due := s["kept"].due(t, lambda x: 16 * x)) is not None:
                sp.wait_ge(s["kept"].sem, due)
                apart(sp, k, t)
            sp.wait_ge(s["r"].sem, s["r"].at(t, lambda x: x + 1))
            apart(sp, k, t)
            sp.dma_start(mlp_rows(m.keep, row), k.mr[:, t.parity]).then_inc(s["kept"].sem, 16)
        if (due := s["stored"].due(t, lambda x: 16 * x)) is not None:
            sp.wait_ge(s["stored"].sem, due)
            apart(sp, k, t)
        sp.wait_ge(s["out"].sem, s["out"].at(t, lambda x: x + 1))
        apart(sp, k, t)
        sp.dma_start(mlp_rows(m.dst, row), k.mout[:, t.parity]).then_inc(s["stored"].sem, 16)

    if m.also is not None:
        load_also(Step(0))
        load_also(Step(1))

    def body(t):
        if m.start is not None:
            load_start(t)
        if t.reg is not None or t.n + 2 < MSTEPS:
            load(t + 2)
            if m.also is not None:
                load_also(t + 2)
        if t.reg is not None or t.n > 1:
            store(t + -2)

    pipeline(sp, MSTEPS, body)
    ahead()
    store(Step(MSTEPS - 2))
    store(Step(MSTEPS - 1))
    if m.keep is not None:
        sp.wait_ge(s["kept"].sem, s["kept"].base + 16 * MSTEPS)
    sp.wait_ge(s["stored"].sem, s["stored"].base + 16 * MSTEPS)


def tensor_mlp(pe, m):
    k, s, w = m.k, m.s, m.w

    def turn(t):
        pe.wait_ge(s["wn"].sem, s["wn"].at(t, lambda x: x + 1))
        if (due := s["xt"].due(t, lambda x: x)) is not None:
            pe.wait_ge(s["xt"].sem, due)
        for blk in range(MB):
            last = pe.transpose(k.misc[:, blk * P:(blk + 1) * P], k.mwn[:, t.parity, blk], k.ident[:, :])
        last.then_inc(s["t_full"].sem, 1)

    def body(t):
        pe.wait_ge(s["xt"].sem, s["xt"].at(t, lambda x: x + 1))
        for f in range(FC):
            if (due := s["gelu"].due(t, lambda x: FC * (x - 1) + f + 1)) is not None:
                pe.wait_ge(s["gelu"].sem, due)
            pe.matmul(k.scores[f // 2][:, (f % 2) * 512:(f % 2 + 1) * 512], w["w1"][:, f * P:(f + 1) * P], k.mxt[:, t.parity],
                      start=True, stop=True).then_inc(s["h_full"].sem, 1)
        if t.reg is not None or t.n + 1 < MSTEPS:
            turn(t + 1)
        if m.after == "route" and (t.reg is not None or t.n > 1):
            route_logits(t + -2)
        if (due := s["r"].due(t, lambda x: x - 1)) is not None:
            pe.wait_ge(s["r"].sem, due)
        for blk in range(MB):
            for f in range(FC):
                if blk == 0:
                    pe.wait_ge(s["gelu"].sem, s["gelu"].at(t, lambda x: FC * x + f + 1))
                last = pe.matmul(k.turned[t.parity][:, blk * P:(blk + 1) * P], k.mh[:, t.parity, f, blk * P:(blk + 1) * P],
                                 w["w2"][:, f], start=(f == 0), stop=(f == FC - 1))
        last.then_inc(s["y_full"].sem, 1)
        if m.after == "route" and (t.reg is not None or t.n > 0):
            route_turn(t + -1)

    def route_turn(t):
        pe.wait_ge(s["rn"].sem, s["rn"].at(t, lambda x: x + 1))
        if (due := s["logits"].due(t, lambda x: x)) is not None:
            pe.wait_ge(s["logits"].sem, due)
        for blk in range(MB):
            last = pe.transpose(k.num[:, blk * P:(blk + 1) * P], k.mrn[:, t.parity, blk], k.ident[:, :])
        last.then_inc(s["rt_full"].sem, 1)

    def route_logits(t):
        pe.wait_ge(s["rxt"].sem, s["rxt"].at(t, lambda x: x + 1))
        for blk in range(MB):
            last = pe.matmul(k.num[:, blk * EXPERTS:(blk + 1) * EXPERTS], k.mrg[:, t.parity, blk], w["gate_w"], start=True, stop=True)
        last.then_inc(s["g_full"].sem, 1)

    turn(Step(0))
    pipeline(pe, MSTEPS, body)
    if m.after == "route":
        route_logits(Step(MSTEPS - 2))
        route_turn(Step(MSTEPS - 1))
        route_logits(Step(MSTEPS - 1))


def scalar_mlp(act, m):
    k, s, w = m.k, m.s, m.w

    def body(t):
        if (due := s["y_full"].due(t, lambda x: x - 1)) is not None:
            act.wait_ge(s["y_full"].sem, due)
        for f in range(FC):
            act.wait_ge(s["h_full"].sem, s["h_full"].at(t, lambda x: FC * x + f + 1))
            act.activation(k.mh[:, t.parity, f], k.scores[f // 2][:, (f % 2) * 512:(f % 2 + 1) * 512], ACT.Gelu,
                           bias=w["b1"][:, f:f + 1], scale=1.0).then_inc(s["gelu"].sem, 1)

        if m.after == "route" and (t.reg is not None or t.n > 0):
            keep_rows(t + -1)

    def keep_rows(t):
        row = t.row(act)
        act.wait_ge(s["rn"].sem, s["rn"].at(t, lambda x: x + 1))
        act.copy(k.rows[:, bass.ds(row, 1)].rearrange("p a n -> p (a n)"), k.mrn[:, t.parity].rearrange("p k c -> p (k c)"))\
           .then_inc(s["rows_kept"].sem, 1)

    pipeline(act, MSTEPS, body)
    if m.after == "route":
        keep_rows(Step(MSTEPS - 1))


def mlp_norm(dve, m):
    k, s = m.k, m.s

    def norm_stats(t):
        dve.wait_ge(s["x_in"].sem, s["x_in"].at(t, lambda x: 16 * (x + 1)))
        vector_norm_stats(dve, k, s, k.mx[:, t.parity], k.mstats[:, t.parity], k.maggr[:, t.parity], ("stats", "aggr"), t, MB)

    def norm(t):
        dve.wait_ge(s["rstd"].sem, s["rstd"].at(t, lambda x: x + 1))
        if (due := s["t_full"].due(t, lambda x: x - 1)) is not None:
            dve.wait_ge(s["t_full"].sem, due)
        for blk in range(MB):
            last = dve.tensor_scalar(k.mwn[:, t.parity, blk], k.mx[:, t.parity, blk], k.maggr[:, t.parity, blk, 0:1],
                                     k.mrstd[:, t.parity, blk:blk + 1], ALU.subtract, ALU.mult)
        last.then_inc(s["wn"].sem, 1)

    return norm_stats, norm


def vector_mlp(dve, m):
    k, s, w = m.k, m.s, m.w

    norm_stats, norm = mlp_norm(dve, m)

    def gain(t):
        dve.wait_ge(s["t_full"].sem, s["t_full"].at(t, lambda x: x + 1))
        if (due := s["h_full"].due(t, lambda x: FC * (x - 1))) is not None:
            dve.wait_ge(s["h_full"].sem, due)
        if w["gain"] is None:
            last = dve.tensor_copy(k.mxt[:, t.parity], k.misc[:, :])
        else:
            last = dve.tensor_scalar(k.mxt[:, t.parity], k.misc[:, :], w["gain"], w["shift"], ALU.mult, ALU.add)
        last.then_inc(s["xt"].sem, 1)

    def finish(t):
        dve.wait_ge(s["y_full"].sem, s["y_full"].at(t, lambda x: x + 1))
        dve.wait_ge(s["biased"].sem, s["biased"].at(t, lambda x: x + 1))
        if m.keep is not None:
            if (due := s["kept"].due(t, lambda x: 16 * (x - 1))) is not None:
                dve.wait_ge(s["kept"].sem, due)
        if m.after == "norm":
            if (due := s["rn"].due(t, lambda x: x - 1)) is not None:
                dve.wait_ge(s["rn"].sem, due)
        else:
            if (due := s["out"].due(t, lambda x: x - 1)) is not None:
                dve.wait_ge(s["out"].sem, due)
            if (due := s["rn"].due(t, lambda x: x - 1)) is not None:
                dve.wait_ge(s["rn"].sem, due)
        dve.tensor_tensor(k.mr[:, t.parity].rearrange("p k c -> p (k c)"), k.turned[t.parity][:, :],
                          k.msum[:, t.parity].rearrange("p k c -> p (k c)"), ALU.add).then_inc(s["r"].sem, 1)
        dve.wait_ge(s["r"].sem, s["r"].at(t, lambda x: x + 1))
        if m.after == "norm":
            vector_norm_stats(dve, k, s, k.mr[:, t.parity], k.mrstats[:, t.parity], k.mraggr[:, t.parity],
                              ("rstats", "raggr"), t, MB)
        else:
            dve.wait_ge(s["start_in"].sem, s["start_in"].at(t, lambda x: 16 * (x + 1)))
            if (due := s["stored"].due(t, lambda x: 16 * (x - 1))) is not None:
                dve.wait_ge(s["stored"].sem, due)
            dve.scalar_tensor_tensor(out=k.mout[:, t.parity].rearrange("p k c -> p (k c)"),
                                     in0=k.mr[:, t.parity].rearrange("p k c -> p (k c)"), scalar=w["gate"],
                                     in1=k.mstart[:, t.parity].rearrange("p k c -> p (k c)"), op0=ALU.mult, op1=ALU.add)\
               .then_inc(s["out"].sem, 1)
            dve.wait_ge(s["out"].sem, s["out"].at(t, lambda x: x + 1))
            vector_norm_stats(dve, k, s, k.mout[:, t.parity], k.mrstats[:, t.parity], k.mraggr[:, t.parity],
                              ("rstats", "raggr"), t, MB)

    def normed(t):
        dve.wait_ge(s["rrstd"].sem, s["rrstd"].at(t, lambda x: x + 1))
        for name in ("gained",) if m.after == "norm" else ("rt_full", "rows_kept"):
            if (due := s[name].due(t, lambda x: x - 1)) is not None:
                dve.wait_ge(s[name].sem, due)
        src = k.mr if m.after == "norm" else k.mout
        for blk in range(MB):
            last = dve.tensor_scalar(k.mrn[:, t.parity, blk], src[:, t.parity, blk], k.mraggr[:, t.parity, blk, 0:1],
                                     k.mrrstd[:, t.parity, blk:blk + 1], ALU.subtract, ALU.mult)
        last.then_inc(s["rn"].sem, 1)

    gain(Step(0))

    def body(t):
        if t.reg is not None or t.n + 1 < MSTEPS:
            gain(t + 1)
        if t.reg is not None or t.n + 2 < MSTEPS:
            norm_stats(t + 2)
        if t.reg is not None or t.n > 0:
            normed(t + -1)
        if t.reg is not None or t.n + 2 < MSTEPS:
            norm(t + 2)
        if m.after == "route" and (t.reg is not None or t.n > 1):
            route_logits(t + -2)
        finish(t)
        if m.after == "route" and (t.reg is not None or t.n > 0):
            route_turned(t + -1)

    def route_turned(t):
        dve.wait_ge(s["rt_full"].sem, s["rt_full"].at(t, lambda x: x + 1))
        if (due := s["g_full"].due(t, lambda x: x - 1)) is not None:
            dve.wait_ge(s["g_full"].sem, due)
        dve.tensor_copy(k.mrg[:, t.parity].rearrange("p k c -> p (k c)"), k.num[:, :]).then_inc(s["rxt"].sem, 1)

    def route_logits(t):
        row = t.row(dve)
        dve.wait_ge(s["g_full"].sem, s["g_full"].at(t, lambda x: x + 1))
        dve.tensor_tensor(k.logits[:, bass.ds(row, 1)].rearrange("p a n -> p (a n)").rearrange("p (k e) -> p k e", e=EXPERTS),
                          k.num[:, 0:MB * EXPERTS].rearrange("p (k e) -> p k e", e=EXPERTS),
                          w["gate_b"].unsqueeze(1).to_broadcast([P, MB, EXPERTS]), ALU.add).then_inc(s["logits"].sem, 1)

    pipeline(dve, MSTEPS, body)
    if m.after == "route":
        route_logits(Step(MSTEPS - 2))
    normed(Step(MSTEPS - 1))
    if m.after == "route":
        route_turned(Step(MSTEPS - 1))
        route_logits(Step(MSTEPS - 1))


def mlp_power(pool, m):
    k, s = m.k, m.s

    def power(aggr, eps, out, names, t):
        pool.wait_ge(s[names[0]].sem, s[names[0]].at(t, lambda x: x + 1))
        if (due := s[names[3]].due(t, lambda x: x - 1)) is not None:
            pool.wait_ge(s[names[3]].sem, due)
        pool.tensor_tensor(eps[:, t.parity], aggr[:, t.parity, :, 1], k.eps[:, 0:MB], ALU.add).then_inc(s[names[1]].sem, 1)
        pool.wait_ge(s[names[1]].sem, s[names[1]].at(t, lambda x: x + 1))
        pool.tensor_tensor(out[:, t.parity], eps[:, t.parity], k.minus_half[:, 0:MB], ALU.pow).then_inc(s[names[2]].sem, 1)

    return power


def mlp_rstd(pool, m):
    k, power = m.k, mlp_power(pool, m)

    def rstd(t):
        power(k.maggr, k.meps, k.mrstd, ("aggr", "eps_in", "rstd", "wn"), t)

    return rstd


def gpsimd_mlp(pool, m):
    k, s, w = m.k, m.s, m.w

    power = mlp_power(pool, m)
    rstd = mlp_rstd(pool, m)

    def bias(t):
        pool.wait_ge(s["x_in"].sem, s["x_in"].at(t, lambda x: 16 * (x + 1)))
        if (due := s["r"].due(t, lambda x: x - 1)) is not None:
            pool.wait_ge(s["r"].sem, due)
        x = k.mx[:, t.parity]
        if m.also is not None:
            pool.wait_ge(s["also_in"].sem, s["also_in"].at(t, lambda x: 16 * (x + 1)))
            pool.tensor_tensor(k.mboth[:, t.parity], x, k.malso[:, t.parity], ALU.add).then_inc(s["both"].sem, 1)
            pool.wait_ge(s["both"].sem, s["both"].at(t, lambda x: x + 1))
            x = k.mboth[:, t.parity]
        pool.tensor_tensor(k.msum[:, t.parity], x, w["bias"].unsqueeze(1).to_broadcast([P, MB, C]), ALU.add)\
            .then_inc(s["biased"].sem, 1)

    def after(t):
        power(k.mraggr, k.mreps, k.mrrstd, ("raggr", "reps", "rrstd", "rn"), t)

    def gains(t):
        pool.wait_ge(s["rn"].sem, s["rn"].at(t, lambda x: x + 1))
        if (due := s["out"].due(t, lambda x: x - 1)) is not None:
            pool.wait_ge(s["out"].sem, due)
        if (due := s["stored"].due(t, lambda x: 16 * (x - 1))) is not None:
            pool.wait_ge(s["stored"].sem, due)
        pool.tensor_tensor(k.mrg[:, t.parity], k.mrn[:, t.parity], w["out_gain"].unsqueeze(1).to_broadcast([P, MB, C]),
                           ALU.mult).then_inc(s["gained"].sem, 1)
        pool.wait_ge(s["gained"].sem, s["gained"].at(t, lambda x: x + 1))
        pool.tensor_tensor(k.mout[:, t.parity], k.mrg[:, t.parity], w["out_shift"].unsqueeze(1).to_broadcast([P, MB, C]),
                           ALU.add).then_inc(s["out"].sem, 1)

    bias(Step(0))

    def body(t):
        if t.reg is not None or t.n + 2 < MSTEPS:
            rstd(t + 2)
        if t.reg is not None or t.n + 1 < MSTEPS:
            bias(t + 1)
        if m.after == "norm" and (t.reg is not None or t.n > 0):
            gains(t + -1)
        after(t)

    pipeline(pool, MSTEPS, body)
    if m.after == "norm":
        gains(Step(MSTEPS - 1))



TILES = B * S // P + EXPERTS
PAIRS = TILES // 2
BLOCKS = B * S // P


class Sort:

    def __init__(self, k, places):
        self.k, self.places = k, places
        self.chosen, self.counted, self.placed, self.scattered = (k.sem(n) for n in ("chosen", "counted", "placed", "scattered"))


def tensor_sort(pe, m):
    k = m.k
    pe.wait_ge(m.chosen, 5)
    pe.matmul(k.num[:, 0:256], k.up_to[:, :], k.chosen, start=True, stop=True)
    pe.matmul(k.num[:, 256:512], k.ones[:, :], k.chosen, start=True, stop=True).then_inc(m.counted, 1)


def vector_sort(dve, m):
    k, E = m.k, EXPERTS
    blocks = lambda x: x.rearrange("p (k e) -> p k e", e=E)
    chosen = Count(m.chosen)

    def choose(ins):
        chosen.inc(ins)
        dve.wait_ge(m.chosen, chosen.n)

    logits = blocks(k.logits.rearrange("p a n -> p (a n)"))
    choose(dve.tensor_reduce(k.best, logits, AX.X, ALU.max))
    choose(dve.tensor_tensor(blocks(k.equal), logits, k.best.unsqueeze(2).to_broadcast([P, BLOCKS, E]), ALU.is_equal))
    choose(dve.tensor_tensor(blocks(k.rank), blocks(k.equal), k.falling[:, :].unsqueeze(1).to_broadcast([P, BLOCKS, E]), ALU.mult))
    choose(dve.tensor_reduce(k.first, blocks(k.rank), AX.X, ALU.max))
    choose(dve.tensor_tensor(blocks(k.chosen), blocks(k.rank), k.first.unsqueeze(2).to_broadcast([P, BLOCKS, E]), ALU.is_equal))
    assert chosen.n == 5
    placed = Count(m.placed)

    def place(ins):
        placed.inc(ins)
        dve.wait_ge(m.placed, placed.n)

    dve.wait_ge(m.counted, 1)
    sums = [k.sums_a, k.sums_b]
    place(dve.tensor_copy(sums[0], k.num[:, 256:512]))
    d, n = 1, 0
    while d < BLOCKS:
        a, b = sums[n % 2], sums[(n + 1) % 2]
        dve.tensor_copy(b[:, 0:d * E], a[:, 0:d * E])
        place(dve.tensor_tensor(b[:, d * E:], a[:, d * E:], a[:, 0:(BLOCKS - d) * E], ALU.add))
        d, n = 2 * d, n + 1
    total = sums[n % 2]
    place(dve.tensor_scalar(k.tiles_x, total[:, (BLOCKS - 1) * E:], (P - 1) / 2, 1.0 / P, ALU.add, ALU.mult))
    place(dve.tensor_scalar(k.tiles, k.tiles_x, ROUND, ROUND, ALU.add, ALU.subtract))
    ends = [k.tiles, k.ends_a, k.ends_b, k.ends_c]
    for n in range(3):
        d, a, b = 1 << n, ends[n], ends[n + 1]
        dve.tensor_copy(b[:, 0:d], a[:, 0:d])
        place(dve.tensor_tensor(b[:, d:], a[:, d:], a[:, 0:E - d], ALU.add))
    place(dve.tensor_tensor(k.ended.rearrange("p (t e) -> p t e", e=E), k.tile_numbers[:, :].unsqueeze(2).to_broadcast([P, TILES, E]),
                            k.ends_c.unsqueeze(1).to_broadcast([P, TILES, E]), ALU.is_ge))
    place(dve.tensor_reduce(k.tile_expert_f, k.ended.rearrange("p (t e) -> p t e", e=E), AX.X, ALU.add))
    place(dve.tensor_scalar(k.tile_expert[:, :], k.tile_expert_f, float(E - 1), None, ALU.min))
    place(dve.tensor_tensor(k.starts, k.ends_c, k.tiles, ALU.subtract))
    place(dve.tensor_scalar(k.start_rows, k.starts, float(P), -1.0, ALU.mult, ALU.add))
    place(dve.tensor_tensor(k.equal, total, k.num[:, 256:512], ALU.subtract))
    place(dve.tensor_tensor(k.rank, k.equal, k.num[:, 0:256], ALU.add))
    place(dve.tensor_tensor(blocks(k.equal), blocks(k.rank), k.start_rows.unsqueeze(1).to_broadcast([P, BLOCKS, E]), ALU.add))
    place(dve.tensor_tensor(k.rank, k.equal, k.chosen, ALU.mult))
    place(dve.tensor_reduce(k.first, blocks(k.rank), AX.X, ALU.add))
    place(dve.tensor_copy(k.place[:, :], k.first))
    assert placed.n == PLACED, placed.n


PLACED = 22


def gpsimd_sort(pool, m):
    k = m.k
    rows = k.rows.rearrange("p a n -> p (a n)")
    pool.wait_ge(m.placed, PLACED)
    for j in range(BLOCKS):
        pool.indirect_dma_start(m.places, bass.IndirectOffsetOnAxis(ap=k.place[:, j:j + 1], axis=0), rows[:, j * P:(j + 1) * P], None)\
            .then_inc(m.scattered, 16)
    pool.wait_ge(m.scattered, 16 * BLOCKS)


class Tiles:

    def __init__(self, k, src, dst, w):
        self.k, self.src, self.dst, self.w = k, src, dst, w
        self.s = k.signals(dict(x_in=16, stored=16, t_full=1, xt=1, w1_in=2, h_full=2, relu_scalar=2, relu_vector=2, y_full=1, out=1), PAIRS)


def sync_tiles(sp, m):
    k, s = m.k, m.s

    def load(t):
        row = t.row(sp)
        if (due := s["x_in"].due(t, lambda x: 16 * x)) is not None:
            sp.wait_ge(s["x_in"].sem, due)
            apart(sp, k, t)
        if (due := s["t_full"].due(t, lambda x: x - 1)) is not None:
            sp.wait_ge(s["t_full"].sem, due)
            apart(sp, k, t)
        sp.dma_start(k.tx[:, t.parity], m.src.rearrange("(t n p) c -> t p n c", n=2, p=P)[row]).then_inc(s["x_in"].sem, 16)

    def store(t):
        row = t.row(sp)
        if (due := s["stored"].due(t, lambda x: 16 * x)) is not None:
            sp.wait_ge(s["stored"].sem, due)
            apart(sp, k, t)
        sp.wait_ge(s["out"].sem, s["out"].at(t, lambda x: x + 1))
        apart(sp, k, t)
        sp.dma_start(m.dst.rearrange("(t n p) c -> t p n c", n=2, p=P)[row], k.ty[:, t.parity]).then_inc(s["stored"].sem, 16)

    load(Step(0))
    load(Step(1))

    def body(t):
        if t.reg is not None or t.n + 2 < PAIRS:
            load(t + 2)
        if t.reg is not None or t.n > 0:
            store(t + -1)

    pipeline(sp, PAIRS, body)
    store(Step(PAIRS - 1))
    sp.wait_ge(s["stored"].sem, s["stored"].base + 16 * PAIRS)


def expert_of(eng, k, t, n):
    tile = 2 * t.n + n if t.reg is None else eng.snap(t.reg * 4 + (2 * t.n + n))
    return eng.value_load(k.tile_expert[0:1, bass.ds(tile, 1)], min_val=0, max_val=EXPERTS - 1)


def tile_bank(k, t, n):
    return k.scores[n][:, t.parity * 512:(t.parity + 1) * 512]


def tensor_tiles(pe, m):
    k, s, w = m.k, m.s, m.w

    def turn(t):
        pe.wait_ge(s["x_in"].sem, s["x_in"].at(t, lambda x: 16 * (x + 1)))
        if (due := s["xt"].due(t, lambda x: x)) is not None:
            pe.wait_ge(s["xt"].sem, due)
        for n in range(2):
            last = pe.transpose(k.misc[:, n * P:(n + 1) * P], k.tx[:, t.parity, n], k.ident[:, :])
        last.then_inc(s["t_full"].sem, 1)

    def hidden(t, n):
        if (due := s["relu_vector"].due(t, lambda x: 2 * (x - 2) + n + 1)) is not None:
            pe.wait_ge(s["relu_vector"].sem, due)
        pe.wait_ge(s["xt"].sem, s["xt"].at(t, lambda x: x + 1))
        pe.wait_ge(s["w1_in"].sem, s["w1_in"].at(t, lambda x: 2 * x + n + 1))
        for f in range(FC):
            last = pe.matmul(tile_bank(k, t, n)[:, f * P:(f + 1) * P], k.tw1[:, t.parity, n * W1_COLS + f * P:n * W1_COLS + (f + 1) * P],
                             k.txt[:, t.parity, n * P:(n + 1) * P], start=True, stop=True)
        last.then_inc(s["h_full"].sem, 1)

    def outs(t, n):
        at = pe.snap(expert_of(pe, k, t, n) * HID)
        if n == 0:
            if (due := s["out"].due(t, lambda x: x - 1)) is not None:
                pe.wait_ge(s["out"].sem, due)
        pe.wait_ge(s["relu_vector"].sem, s["relu_vector"].at(t, lambda x: 2 * x + n + 1))
        for f in range(FC):
            last = pe.matmul(k.turned[t.parity][:, n * P:(n + 1) * P], k.th[:, t.parity, (n * FC + f) * P:(n * FC + f + 1) * P],
                             w["w2"][:, bass.ds(at + f * P, P)], start=(f == 0), stop=(f == FC - 1))
        if n == 1:
            last.then_inc(s["y_full"].sem, 1)

    turn(Step(0))
    for n in range(2):
        hidden(Step(0), n)
    turn(Step(1))

    def body(t):
        for n in range(2):
            if t.reg is not None or t.n + 1 < PAIRS:
                hidden(t + 1, n)
            outs(t, n)
            if n == 0 and (t.reg is not None or t.n + 2 < PAIRS):
                turn(t + 2)

    pipeline(pe, PAIRS, body)


def scalar_tiles(act, m):
    k, s, w = m.k, m.s, m.w

    def weights(t, n):
        at = act.snap(expert_of(act, k, t, n) * W1_COLS)
        if (due := s["h_full"].due(t, lambda x: 2 * (x - 1) + n - 1)) is not None:
            act.wait_ge(s["h_full"].sem, due)
        if (due := s["relu_vector"].due(t, lambda x: 2 * (x - 1) + n - 1)) is not None:
            act.wait_ge(s["relu_vector"].sem, due)
        act.copy(k.tw1[:, t.parity, n * W1_COLS:(n + 1) * W1_COLS], w["w1"][:, bass.ds(at, W1_COLS)]).then_inc(s["w1_in"].sem, 1)

    for n in range(4):
        weights(Step(n // 2), n % 2)

    def body(t):
        more = t.reg is not None or t.n + 2 < PAIRS
        for n in range(2):
            act.wait_ge(s["h_full"].sem, s["h_full"].at(t, lambda x: 2 * x + n + 1))
            act.wait_ge(s["w1_in"].sem, s["w1_in"].at(t, lambda x: 2 * x + n + 1))
            if (due := s["y_full"].due(t, lambda x: x - 1)) is not None:
                act.wait_ge(s["y_full"].sem, due)
            for f in range(2):
                last = act.activation(k.th[:, t.parity, (n * FC + f) * P:(n * FC + f + 1) * P], tile_bank(k, t, n)[:, f * P:(f + 1) * P],
                                      ACT.Relu, bias=k.tw1[:, t.parity, n * W1_COLS + HID + f:n * W1_COLS + HID + f + 1], scale=1.0)
            last.then_inc(s["relu_scalar"].sem, 1)
            if more:
                weights(t + 2, n)

    pipeline(act, PAIRS, body)


def vector_tiles(dve, m):
    k, s, w = m.k, m.s, m.w

    def turned(t):
        dve.wait_ge(s["t_full"].sem, s["t_full"].at(t, lambda x: x + 1))
        if (due := s["h_full"].due(t, lambda x: 2 * (x - 1))) is not None:
            dve.wait_ge(s["h_full"].sem, due)
        dve.tensor_copy(k.txt[:, t.parity], k.misc[:, 0:2 * P]).then_inc(s["xt"].sem, 1)

    def relu(t, n):
        dve.wait_ge(s["relu_scalar"].sem, s["relu_scalar"].at(t, lambda x: 2 * x + n + 1))
        for f in range(2, FC):
            last = dve.tensor_scalar(k.th[:, t.parity, (n * FC + f) * P:(n * FC + f + 1) * P], tile_bank(k, t, n)[:, f * P:(f + 1) * P],
                                     k.tw1[:, t.parity, n * W1_COLS + HID + f:n * W1_COLS + HID + f + 1], 0.0, ALU.add, ALU.max)
        last.then_inc(s["relu_vector"].sem, 1)

    def finish(t):
        at = [dve.snap(expert_of(dve, k, t, n) * C) for n in range(2)]
        dve.wait_ge(s["y_full"].sem, s["y_full"].at(t, lambda x: x + 1))
        if (due := s["stored"].due(t, lambda x: 16 * (x - 1))) is not None:
            dve.wait_ge(s["stored"].sem, due)
        for n in range(2):
            last = dve.tensor_tensor(k.ty[:, t.parity, n], k.turned[t.parity][:, n * P:(n + 1) * P],
                                     w["b2"][:, bass.ds(at[n], C)], ALU.add)
        last.then_inc(s["out"].sem, 1)

    turned(Step(0))
    turned(Step(1))

    def body(t):
        relu(t, 0)
        relu(t, 1)
        if t.reg is not None or t.n + 2 < PAIRS:
            turned(t + 2)
        finish(t)

    pipeline(dve, PAIRS, body)


class Gather:

    def __init__(self, k, rows, src, dst, w):
        self.k, self.rows, self.src, self.dst, self.w = k, rows, src, dst, w
        self.s = k.signals(dict(x_in=16, even_rows_in=8 * MB, odd_rows_in=8 * MB, stored=16, out=1), MSTEPS)


def sync_gather(sp, m):
    k, s = m.k, m.s

    def load(t):
        row = t.row(sp)
        if (due := s["x_in"].due(t, lambda x: 16 * x)) is not None:
            sp.wait_ge(s["x_in"].sem, due)
            apart(sp, k, t)
        if (due := s["out"].due(t, lambda x: x - 1)) is not None:
            sp.wait_ge(s["out"].sem, due)
            apart(sp, k, t)
        sp.dma_start(k.mx[:, t.parity], mlp_rows(m.src, row)).then_inc(s["x_in"].sem, 16)

    def store(t):
        row = t.row(sp)
        if (due := s["stored"].due(t, lambda x: 16 * x)) is not None:
            sp.wait_ge(s["stored"].sem, due)
            apart(sp, k, t)
        sp.wait_ge(s["out"].sem, s["out"].at(t, lambda x: x + 1))
        apart(sp, k, t)
        sp.dma_start(mlp_rows(m.dst, row), k.mout[:, t.parity]).then_inc(s["stored"].sem, 16)

    load(Step(0))
    load(Step(1))

    def body(t):
        store(t)
        if t.reg is not None or t.n + 2 < MSTEPS:
            load(t + 2)

    pipeline(sp, MSTEPS, body)
    sp.wait_ge(s["stored"].sem, s["stored"].base + 16 * MSTEPS)


def gpsimd_gather(pool, m):
    k, s = m.k, m.s
    for t in range(MSTEPS):
        if t >= 2:
            pool.wait_ge(s["out"].sem, s["out"].base + t - 1)
        for blk in range(MB):
            j = MB * t + blk
            pool.indirect_dma_start(k.my[:, t % 2, blk], None, m.rows, bass.IndirectOffsetOnAxis(ap=k.place[:, j:j + 1], axis=0))\
                .then_inc(s["odd_rows_in" if t % 2 else "even_rows_in"].sem, 16)


def vector_gather(dve, m):
    k, s = m.k, m.s

    def body(t):
        flat = lambda x: x.rearrange("p k c -> p (k c)")
        dve.wait_ge(s["x_in"].sem, s["x_in"].at(t, lambda x: 16 * (x + 1)))
        rows_in = s["odd_rows_in" if t.parity else "even_rows_in"]
        dve.wait_ge(rows_in.sem, rows_in.at(t, lambda x: 16 * MB * (x // 2 + 1)))
        if (due := s["stored"].due(t, lambda x: 16 * (x - 1))) is not None:
            dve.wait_ge(s["stored"].sem, due)
        dve.scalar_tensor_tensor(out=flat(k.mout[:, t.parity]), in0=flat(k.my[:, t.parity]), scalar=m.w["gate"],
                                 in1=flat(k.mx[:, t.parity]), op0=ALU.mult, op1=ALU.add).then_inc(s["out"].sem, 1)

    pipeline(dve, MSTEPS, body)



class Core:

    def __init__(self, nc, ctx):
        self.nc, self.ctx, self.counts = nc, ctx, {}
        self.scores = [ctx.enter_context(nc.psum_tensor(f"scores{i}", [P, 1024], F32)) for i in range(2)]
        self.turned = [ctx.enter_context(nc.psum_tensor(f"turned{i}", [P, 512], F32)) for i in range(2)]
        self.num = ctx.enter_context(nc.psum_tensor("num", [P, 512], F32))
        self.misc = ctx.enter_context(nc.psum_tensor("misc", [P, 512], F32))
        self.ident = self.sb("ident", [P, P])
        self.identb = self.sb("identb", [P, P], BF16)
        self.above = self.sb("above", [P, P], BF16)
        self.own8 = self.sb("own8", [P, 16])
        self.own32 = self.sb("own32", [P, 4])
        self.own_columns = self.sb("own_columns", [P, 4, 32])
        self.own_pair8 = self.sb("own_pair8", [P, 8, P])
        self.own_pair32 = self.sb("own_pair32", [P, 8, P])
        self.minus_half = self.sb("minus_half", [P, 4])
        self.eps = self.sb("eps", [P, 4])
        self.falling = self.sb("falling", [P, EXPERTS])
        self.ones = self.sb("ones", [P, P])
        self.zeros = self.sb("zeros", [P, 512])
        self.up_to = self.sb("up_to", [P, P])
        self.tile_numbers = self.sb("tile_numbers", [P, TILES])
        self.tile_expert = self.sb("tile_expert", [P, TILES], I32)
        self.place = self.sb("place", [P, BLOCKS], I32)
        self.space = self.sb("space", [P, SPACE])
        self.at = 0
        t = self.take
        self.through = self.sem("through")
        self.km, self.qT, self.val = t(2, 16, 256), t(2, 4, 256), t(2, 2, 512)
        self.probs, self.pt = t(2, 2, 512), t(8, 384)
        self.numS, self.rx, self.ot = t(2, 4, 256), t(2, 512), t(4, 256)
        self.xq, self.xk, self.wn, self.x_in = t(2, 256), t(2, 256), t(2, 2, 128), t(2, 2, 128)
        self.base_in, self.base_sum, self.res = t(2, 2, 128), t(2, 2, 128), t(2, 2, 128)
        self.kT = t(4, 256)
        self.nmax, self.sums, self.rsum = t(2, 4), t(2, 2, 16), t(2, 2, 16)
        self.stats, self.aggr, self.vareps, self.rstd = t(2, 2, 6), t(2, 2, 2), t(2, 2), t(2, 2)
        self.cstats, self.caggr, self.cvareps, self.crstd = t(2, 1, 6)[0:TC], t(2, 1, 2)[0:TC], t(2, 1)[0:TC], t(2, 1)[0:TC]
        self.cmax = t(2, 8)
        self.ctx_in, self.cn = t(2, 64)[0:TC], t(2, 64)[0:TC]
        self.mx, self.mwn = t(2, 4, 128), t(2, 4, 128)
        self.mstats, self.maggr, self.meps, self.mrstd = t(2, 4, 6), t(2, 4, 2), t(2, 4), t(2, 4)
        mark = self.at
        self.at = 0
        self.km_cross, self.vb, self.ptc = t(2, 1024), t(2, 8, 128), t(2, 4, 256)
        self.pc = t(2, 512)
        self.xc = t(2, 2, 64)[0:TC]
        assert self.at <= 2 * 16 * 256, self.at
        self.at = 0
        self.malso, self.mstart = t(2, 4, 128), t(2, 4, 128)
        self.mxt, self.msum, self.mboth, self.mr = t(2, 512), t(2, 4, 128), t(2, 4, 128), t(2, 4, 128)
        self.mrn, self.mrg, self.mout = t(2, 4, 128), t(2, 4, 128), t(2, 4, 128)
        tiles_at = self.at
        self.mh = t(2, 4, 512)
        self.mrstats, self.mraggr, self.mreps, self.mrrstd = t(2, 4, 6), t(2, 4, 2), t(2, 4), t(2, 4)
        self.rows, self.logits = t(MSTEPS, 512), t(MSTEPS, MB * EXPERTS)
        self.equal, self.rank, self.chosen, self.sums_a, self.sums_b = t(256), t(256), t(256), t(256), t(256)
        self.best, self.first, self.ended, self.tile_expert_f = t(BLOCKS), t(BLOCKS), t(TILES * EXPERTS), t(TILES)
        self.tiles_x, self.tiles, self.ends_a, self.ends_b, self.ends_c = (t(EXPERTS) for _ in range(5))
        self.starts, self.start_rows = t(EXPERTS), t(EXPERTS)
        end, self.at = self.at, tiles_at
        self.tx, self.txt, self.tw1, self.ty = t(2, 2, P), t(2, 2 * P), t(2, 2 * W1_COLS), t(2, 2, C)
        assert self.at <= tiles_at + 2 * 4 * 512
        self.at = end
        self.th, self.my = t(2, 2 * HID), t(2, MB, C)
        mark = max(mark, self.at)
        self.at = 0
        self.quant, self.quant_round, self.quant_out, self.proj_sum = t(1024), t(1024), t(1024), t(512)
        self.fc_t, self.proj_t, self.bfc_t, self.bproj_t = t(512), t(512), t(512)[0:RANK], t(128)[0:RANK]
        self.amax, self.amax_t, self.amax_d = t(2), t(1)[0:2], t(2)[0:2]
        self.qscale, self.qinv = t(2), t(2)
        self.bv_b, self.bcv_b, self.bp_g = t(128), t(128), t(128)
        mark = max(mark, self.at)
        assert mark <= SPACE, mark

    def sb(self, name, shape, dt=F32):
        return self.ctx.enter_context(self.nc.sbuf_tensor(name, shape, dt))

    def sem(self, name):
        return self.ctx.enter_context(self.nc.semaphore(name))

    def signals(self, each, steps):
        out = {}
        for name, n in each.items():
            if name not in self.counts:
                self.counts[name] = (self.sem(name), 0)
            sem, base = self.counts[name]
            out[name] = Signal(sem, base)
            self.counts[name] = (sem, base + n * steps)
        return out

    def take(self, *shape):
        n = 1
        for x in shape:
            n *= x
        flat = self.space[:, self.at:self.at + n]
        self.at += n
        if len(shape) == 1:
            return flat
        if len(shape) == 2:
            return flat.rearrange("p (a b) -> p a b", b=shape[1])
        return flat.rearrange("p (a b c) -> p a b c", b=shape[1], c=shape[2])


class Weights:

    FIRST_ROWS = ("bk", "bq", "bck", "bcq", "bv", "bcv")
    LATER_ROWS = tuple(f"{a}_{n}" for a in ("a1", "a2") for n in ("lnx_g", "lnx_b", "lny_g", "lny_b", "ln3_g", "ln3_b"))

    def __init__(self, k):
        self.k = k
        t = lambda name, *shape: k.sb("w_" + name, list(shape))
        self.first_rows, self.first_cols = t("first_rows", 8, P), t("first_cols", P, 8)
        self.later_rows, self.later_cols = t("later_rows", 64, P), t("later_cols", P, 64)
        self.scaled = t("scaled", P, 2)
        self.raw_gates, self.gates = t("raw_gates", P, 4), t("gates", P, 4)
        self.Wq, self.Wk, self.Wv, self.Wcq = (t(n, C, C) for n in ("Wq", "Wk", "Wv", "Wcq"))
        self.Wck, self.Wcv = t("Wck", CC, C), t("Wcv", CC, C)
        self.raw_wp, self.wp, self.bp = t("raw_wp", C, C), t("wp", P, 1, C), t("bp", P, C)
        self.o_bias1, self.o_bias2 = t("o_bias1", P, C), t("o_bias2", P, C)
        self.fc, self.proj = t("fc", P, HID), t("proj", P, FC, C)
        self.raw_bfc, self.raw_bproj = t("raw_bfc", P, FC, RANK), t("raw_bproj", P, RANK)
        self.a_fc, self.a_proj = t("a_fc", RANK, C), t("a_proj", RANK, HID)
        self.proj_b, self.proj_bg = t("proj_b", P, C), t("proj_bg", P, C)
        self.ln = {n: t(n, P, C) for n in ("ln1_g", "ln1_b", "ln2_g", "ln2_b")}
        self.attn = {}
        for a, cy in (("a1", C), ("a2", CC)):
            self.attn[a] = dict(wq=t(a + "_wq", C, H, 32), wk=t(a + "_wk", cy, H, 32), wv=t(a + "_wv", cy, H, 32),
                                li1_w=t(a + "_li1_w", P, 4, C), li2_w=t(a + "_li2_w", C, HID), li3_w=t(a + "_li3_w", P, FC, C),
                                li1_b=t(a + "_li1_b", P, C), li3_b=t(a + "_li3_b", P, C))
        self.raw_gate, self.gate_w, self.gate_b = t("raw_gate", EXPERTS, C), t("gate_w", C, EXPERTS), t("gate_b", P, EXPERTS)
        self.w1, self.w2 = t("w1", P, EXPERTS, W1_COLS), t("w2", P, EXPERTS, FC, C)
        self.b2 = t("b2", P, EXPERTS * C)

    def col(self, name):
        if name in self.FIRST_ROWS:
            i = self.FIRST_ROWS.index(name)
            return self.first_cols[:, i:i + 1]
        i = self.LATER_ROWS.index(name)
        return self.later_cols[0:CC if name[0:6] == "a2_lny" else P, i:i + 1]

    def hidden_bias(self, i):
        n = len(self.LATER_ROWS) + FC * i
        return self.later_cols[:, n:n + FC]

    @property
    def expert_bias(self):
        return self.later_cols[:, 32:64].rearrange("p (e f) -> p e f", f=FC)


def on_every_partition(v):
    return v.rearrange("(a n) -> a n", a=1).to_broadcast([P, v.shape[0]])


def first_loads(w, g_xattn, g_ffn, A):
    rows = [(w.first_rows[i:i + 1, :], A[n].rearrange("(a n) -> a n", a=1)) for i, n in enumerate(w.FIRST_ROWS)]
    return rows + [
        (w.raw_gates[:, 0:2], on_every_partition(g_xattn)), (w.raw_gates[:, 2:4], on_every_partition(g_ffn)),
        (w.raw_wp[:, :], A["Wp"]), (w.Wq[:, :], A["Wq"]), (w.Wk[:, :], A["Wk"]), (w.Wv[:, :], A["Wv"]),
        (w.Wcq[:, :], A["Wcq"]), (w.Wck[:, :], A["Wck"]), (w.Wcv[:, :], A["Wcv"]), (w.bp[:, :], on_every_partition(A["bp"]))]


def later_loads(w, F, X, M):
    out = []
    for i, n in enumerate(w.LATER_ROWS):
        out.append((w.later_rows[i:i + 1, 0:X[n].shape[0]], X[n].rearrange("(a n) -> a n", a=1)))
    for i, v in enumerate((F["b_fc"], X["a1_li2_b"], X["a2_li2_b"])):
        n = len(w.LATER_ROWS) + FC * i
        out.append((w.later_rows[n:n + FC, :], v.rearrange("(f p) -> f p", p=P)))
    out += [
        (w.later_rows[32:64, :], M["b1"].rearrange("e (f p) -> (e f) p", p=P)),
        (w.fc[:, :].rearrange("p (f c) -> p f c", f=FC), F["W_fc"].rearrange("(f p) c -> p f c", p=P)),
        (w.proj[:, :, :].rearrange("p f c -> p (f c)"), F["W_proj"]),
        (w.raw_bfc[:, :, :], F["B_fc"].rearrange("(f p) r -> p f r", p=P)), (w.raw_bproj[:, :], F["B_proj"]),
        (w.a_fc[:, :], F["A_fc"]), (w.a_proj[:, :], F["A_proj"]), (w.proj_b[:, :], on_every_partition(F["b_proj"])),
        (w.raw_gate[:, :], M["gate_w"]), (w.gate_b[:, :], on_every_partition(M["gate_b"])),
        (w.b2[:, :], on_every_partition(M["b2"].rearrange("e c -> (e c)"))),
        (w.w2[:, :, :, :].rearrange("p e f c -> p e (f c)"), M["w2"].rearrange("e p h -> p e h"))]
    out += [(w.w1[:, e, 0:HID].rearrange("p (f c) -> p f c", c=C), M["w1"][e].rearrange("(f p) c -> p f c", p=P))
            for e in range(EXPERTS)]
    for a, t in w.attn.items():
        out += [(t[n][:, :, :], X[f"{a}_{n}"].rearrange("h c d -> c h d")) for n in ("wq", "wk", "wv")]
        out += [(t[n][:, :, :], X[f"{a}_{n}"].rearrange("(g p) c -> p g c", p=P)) for n in ("li1_w", "li3_w")]
        out += [(t["li2_w"][:, :], X[f"{a}_li2_w"])]
        out += [(t[n][:, :], on_every_partition(X[f"{a}_{n}"])) for n in ("li1_b", "li3_b")]
    return out + [(w.ln[n][:, :], on_every_partition(X[n])) for n in w.ln]



class Ready:

    FILLED_FIRST, RESULTS_FIRST = 2, 5

    def __init__(self, k):
        self.made, self.loaded_first, self.loaded_later = k.sem("made"), k.sem("loaded_first"), k.sem("loaded_later")
        self.gated, self.filled, self.result = k.sem("gated"), k.sem("filled"), k.sem("result")
        self.turned, self.emptied = k.sem("turned"), k.sem("emptied")


def tensor_first(pe, k, w, r):
    pe.transpose(k.num[:, 0:8], w.first_rows[:, :], k.ident[0:8, 0:8]).then_inc(r.filled, 1)
    pe.wait_ge(r.result, 3)
    pe.matmul(k.misc[:, 0:P], k.bv_b, w.raw_wp[:, :], start=True, stop=True)
    pe.matmul(k.misc[:, P:2 * P], k.bcv_b, w.raw_wp[:, :], start=True, stop=True).then_inc(r.filled, 1)


def vector_first(dve, k, w, r):
    result = Count(r.result)
    dve.wait_ge(r.filled, 1)
    result.inc(dve.tensor_copy(w.first_cols[:, :], k.num[:, 0:8]))
    dve.wait_ge(r.result, result.n)
    result.inc(dve.tensor_scalar(k.bv_b, k.ones[:, :], w.col("bv"), None, ALU.mult))
    result.inc(dve.tensor_scalar(k.bcv_b, k.ones[:, :], w.col("bcv"), None, ALU.mult))
    dve.tensor_scalar(w.scaled[:, 0:1], w.col("bq"), 8.0 ** -0.5, None, ALU.mult)
    dve.tensor_scalar(w.scaled[:, 1:2], w.col("bcq"), 8.0 ** -0.5, None, ALU.mult)
    dve.wait_ge(r.gated, 1)
    dve.tensor_scalar(w.wp[:, 0], w.raw_wp[:, :], w.gates[:, 0:1], None, ALU.mult)
    dve.wait_ge(r.filled, 2)
    result.inc(dve.tensor_tensor(k.bp_g, w.bp[:, :], k.misc[:, 0:P], ALU.add))
    dve.wait_ge(r.result, result.n)
    dve.tensor_scalar(w.o_bias1[:, :], k.bp_g, w.gates[:, 0:1], None, ALU.mult)
    result.inc(dve.tensor_scalar(w.o_bias2[:, :], k.misc[:, P:2 * P], w.gates[:, 0:1], None, ALU.mult))
    assert result.n == Ready.RESULTS_FIRST



class Prepare:

    ROW_MAX, MAX, DIAGONAL, SCALE, INVERSE, QUANTISED = 1, 2, 3, 4, 5, 15

    def __init__(self, k, w, r, later):
        self.k, self.w, self.r, self.later = k, w, r, later


def nothing(eng, m):
    pass


def tensor_prepare(pe, m):
    k, w, r, n = m.k, m.w, m.r, Ready.RESULTS_FIRST
    turned, filled = Count(r.turned), Count(r.filled)

    def turn(bank, parts, rows):
        for f, part in enumerate(parts):
            last = pe.transpose(bank[0:part.shape[1], f * rows:(f + 1) * rows], part, k.ident[0:rows, 0:rows])
        return last

    def to_scalar(parts, rows):
        if turned.n >= 4:
            pe.wait_ge(r.emptied, turned.n - 3)
        half = turned.n % 2 * 512
        turned.inc(turn(k.scores[turned.n // 2 % 2][:, half:half + 512], parts, rows))

    pe.wait_ge(r.loaded_later, m.later)
    to_scalar([w.later_rows[:, :]], 64)
    to_scalar([w.raw_bfc[:, f] for f in range(FC)], P)
    to_scalar([w.raw_bproj[:, :]], P)
    to_scalar([w.raw_gate[:, :]], EXPERTS)
    pe.wait_ge(r.result, n + m.ROW_MAX)
    filled.inc(turn(k.num, [k.amax], P))
    for e in range(EXPERTS):
        to_scalar([w.w1[:, e, f * P:(f + 1) * P] for f in range(FC)], P)
        to_scalar([w.w2[:, e, f] for f in range(FC)], P)
        if e == 1:
            pe.wait_ge(r.result, n + m.DIAGONAL)
            filled.inc(pe.matmul(k.misc[:, 0:2], k.ones[0:2, :], k.amax_d, start=True, stop=True))
    pe.wait_ge(r.result, n + m.QUANTISED)
    q = k.quant_out
    filled.inc(turn(k.turned[0], [q[:, f * P:(f + 1) * P] for f in range(FC)], P))
    filled.inc(turn(k.turned[1], [q[:, HID + f * P:HID + (f + 1) * P] for f in range(FC)], P))
    pe.wait_ge(r.emptied, turned.n)
    filled.inc(pe.matmul(k.num[:, :], w.a_fc[:, :], k.bfc_t, start=True, stop=True))
    for f in range(FC):
        last = pe.matmul(k.misc[:, f * P:(f + 1) * P], w.a_proj[:, f * P:(f + 1) * P], k.bproj_t, start=True, stop=True)
    filled.inc(last)


def scalar_prepare(act, m):
    k, w, r = m.k, m.w, m.r
    emptied = Count(r.emptied)

    def empty(out, scale=None):
        act.wait_ge(r.turned, emptied.n + 1)
        half = emptied.n % 2 * 512
        bank = k.scores[emptied.n // 2 % 2][0:out.shape[0], half:half + out.shape[1]]
        emptied.inc(act.copy(out, bank) if scale is None else act.mul(out, bank, scale))

    empty(w.later_cols[:, :])
    empty(k.bfc_t, LORA_SCALE)
    empty(k.bproj_t, LORA_SCALE)
    empty(w.gate_w[:, :])
    act.wait_ge(r.emptied, 1)
    act.copy(w.w1[:, :, HID:W1_COLS], w.expert_bias)
    for e in range(EXPERTS):
        empty(w.w1[:, e, 0:HID])
        empty(w.w2[:, e].rearrange("p f c -> p (f c)"))


def vector_prepare(dve, m):
    k, w, r = m.k, m.w, m.r
    n, filled = Ready.RESULTS_FIRST, Ready.FILLED_FIRST
    result = Count(r.result)
    result.n = n
    raws = (w.fc[:, :], w.proj[:, :, :].rearrange("p f c -> p (f c)"))
    dve.wait_ge(r.loaded_later, m.later)
    dve.tensor_reduce(k.amax[:, 0:1], raws[0], AX.X, ALU.max, apply_absolute_value=True)
    result.inc(dve.tensor_reduce(k.amax[:, 1:2], raws[1], AX.X, ALU.max, apply_absolute_value=True))
    dve.wait_ge(r.filled, filled + 1)
    result.inc(dve.tensor_reduce(k.amax_t, k.num[0:2, 0:P], AX.X, ALU.max))
    dve.wait_ge(r.result, result.n)
    result.inc(dve.tensor_scalar(k.amax_d, k.ident[0:2, 0:2], k.amax_t, None, ALU.mult))
    dve.wait_ge(r.filled, filled + 2)
    result.inc(dve.tensor_scalar(k.qscale, k.misc[:, 0:2], 1.0 / QMAX, None, ALU.mult))
    dve.wait_ge(r.result, result.n)
    result.inc(dve.reciprocal(k.qinv, k.qscale))
    assert result.n == n + m.INVERSE

    def quantise(step, j):
        half = slice(j * HID, (j + 1) * HID)
        q, rounded, raw = k.quant[:, half], k.quant_round[:, half], raws[j]
        if step == 0:
            return dve.tensor_scalar(q, raw, k.qinv[:, j:j + 1], ROUND, ALU.mult, ALU.add)
        if step == 1:
            return dve.tensor_scalar(rounded, q, ROUND, QMAX, ALU.subtract, ALU.min)
        if step == 2:
            return dve.tensor_scalar(q, rounded, -QMAX - 1.0, k.qscale[:, j:j + 1], ALU.max, ALU.mult)
        if step == 3:
            return dve.tensor_tensor(rounded, q, raw, ALU.subtract)
        return dve.tensor_tensor(k.quant_out[:, half], raw, rounded, ALU.add)

    for step in range(5):
        for j in range(2):
            dve.wait_ge(r.result, result.n - (1 if step else j))
            result.inc(quantise(step, j))
    assert result.n == n + m.QUANTISED
    dve.wait_ge(r.filled, filled + 3)
    dve.tensor_copy(k.fc_t, k.turned[0][:, :])
    dve.wait_ge(r.filled, filled + 4)
    result.inc(dve.tensor_copy(k.proj_t, k.turned[1][:, :]))
    dve.wait_ge(r.result, result.n)
    dve.wait_ge(r.filled, filled + 5)
    dve.tensor_tensor(w.fc[:, :], k.num[:, :], k.fc_t, ALU.add)
    dve.wait_ge(r.filled, filled + 6)
    result.inc(dve.tensor_tensor(k.proj_sum, k.misc[:, :], k.proj_t, ALU.add))
    dve.wait_ge(r.result, result.n)
    dve.tensor_scalar(raws[1], k.proj_sum, w.gates[:, 2:3], None, ALU.mult)
    result.inc(dve.tensor_scalar(w.proj_bg[:, :], w.proj_b[:, :], w.gates[:, 2:3], None, ALU.mult))


def gpsimd_constants(pool, k, made):
    fill, keep = makers(pool, made)
    fill(k.ident[:, :], 0.0)
    keep(k.ident[:, :], [[-1, P]], 0, 1, ALU.not_equal, 1.0)
    for t, v in ((k.identb, 0.0), (k.above, 0.0), (k.own8, 1.0), (k.ones, 1.0), (k.minus_half, -0.5), (k.eps, EPS), (k.zeros, 0.0)):
        fill(t[:, :], v)
    fill(k.own_columns[:, :, :], 1.0)
    keep(k.identb[:, :], [[-1, P]], 0, 1, ALU.not_equal, 1.0)
    keep(k.above[:, :], [[-1, P]], 0, 1, ALU.is_ge, MASKED)
    own_heads(keep, k.own8, 8)
    keep(k.own_columns[:, :, :], [[-8, 4], [1, 32]], 0, 0)
    keep(k.own_columns[:, :, :], [[8, 4], [-1, 32]], 7, 0)
    assert made.n == CONSTANTS, made.n


CONSTANTS = 16


def gpsimd_later_constants(pool, k, made):
    fill, keep = makers(pool, made)
    fill(k.own32[:, :], 1.0)
    fill(k.up_to[:, :], 1.0)
    for t in (k.own_pair8, k.own_pair32):
        fill(t[:, :, :], 1.0)
    for e in range(EXPERTS):
        fill(k.falling[:, e:e + 1], float(EXPERTS - e))
    for tile in range(TILES):
        fill(k.tile_numbers[:, tile:tile + 1], float(tile))
    keep(k.up_to[:, :], [[1, P]], 0, -1)
    own_heads(keep, k.own32, 32)
    for half in range(2):
        part = slice(64 * half, 64 * half + 64)
        keep(k.own_pair8[part], [[-16, 8], [1, P]], -8 * half, 0)
        keep(k.own_pair8[part], [[16, 8], [-1, P]], 8 * half + 7, 0)
        for j in range(2):
            four = k.own_pair32[part].rearrange("p (g j) c -> p g j c", j=2)[:, :, j]
            keep(four, [[0, 4], [1, P]], -(64 * j + 32 * half), 0)
            keep(four, [[0, 4], [-1, P]], 64 * j + 32 * half + 31, 0)
    pool.wait_ge(made.sem, made.n)


def makers(pool, made):
    def fill(t, v):
        made.inc(pool.memset(t, v))

    def keep(t, pattern, base, cm, op=ALU.is_ge, v=0.0):
        pool.wait_ge(made.sem, made.n)
        made.inc(pool.affine_select(out=t, in_=t, compare_op=op, fill=v, base=base, pattern=pattern, channel_multiplier=cm))

    return fill, keep


def own_heads(keep, own, n):
    keep(own[:, :], [[-n, P // n]], 0, 1)
    keep(own[:, :], [[n, P // n]], n - 1, -1)


def network(nc, x, ctx_512, g_xattn, g_ffn, A, F, X, M, out):
    with ExitStack() as stack:
        k = Core(nc, stack)
        w, r = Weights(k), Ready(k)
        first, later = first_loads(w, g_xattn, g_ffn, A), later_loads(w, F, X, M)
        phase, cleared = k.sem("phase"), k.sem("cleared")

        def dram(name):
            return nc.dram_tensor(name, [B, S, C], F32, kind="Internal").ap()

        s1, s2, x2, xx, xo1, xm, xo2, x3 = (dram(n) for n in ("s1", "s2", "x2", "xx", "xo1", "xm", "xo2", "x3"))

        sorted_in, sorted_out = (nc.dram_tensor(n, [TILES * P, C], F32, kind="Internal").ap() for n in ("sorted_in", "sorted_out"))
        later += [(sorted_in.rearrange("(t p n) c -> t p (n c)", p=P, n=4)[i], k.zeros[:, :]) for i in range(TILES // 4)]

        def second(a):
            t = w.attn[a]
            wide = {n: t[n][:, :, :].rearrange("c h d -> c (h d)") for n in ("wq", "wk", "wv")}
            return dict(wide, wo=t["li1_w"], q_gain=w.col(a + "_lnx_g"), q_shift=w.col(a + "_lnx_b"),
                        k_gain=w.col(a + "_lny_g"), k_shift=w.col(a + "_lny_b"), q_bias=None, k_bias=None,
                        o_bias=t["li1_b"][:, :], own=k.own32, own_pair=k.own_pair32[:, :, :])

        def first_layer(wq, wk, wv, q_bias, k_bias, o_bias):
            return dict(wq=wq, wk=wk, wv=wv, wo=w.wp, q_gain=None, q_shift=None, k_gain=None, k_shift=None, q_bias=q_bias,
                        k_bias=k_bias, o_bias=o_bias[:, :], own=k.own8, own_pair=k.own_pair8[:, :, :])

        def mlp(a, i):
            t = w.attn[a]
            return dict(gain=w.col(a + "_ln3_g"), shift=w.col(a + "_ln3_b"), w1=t["li2_w"], b1=w.hidden_bias(i), w2=t["li3_w"],
                        bias=t["li3_b"][:, :], out_gain=w.ln["ln2_g"][:, :], out_shift=w.ln["ln2_b"][:, :], gate=w.gates[:, 1:2])

        parts = [
            Attention(k, "a", "self", 8, "before", x, x, s1, None, False,
                      first_layer(w.Wq, w.Wk, w.Wv, w.scaled[:, 0:1], w.col("bk"), w.o_bias1)),
            Attention(k, "b", "cross", 8, None, x, s1, s2, ctx_512, False,
                      first_layer(w.Wcq, w.Wck, w.Wcv, w.scaled[:, 1:2], w.col("bck"), w.o_bias2)),
            Prepare(k, w, r, 16 * len(later)),
            Mlp(k, "c", s2, None, "norm", xx, x2, None, dict(
                gain=None, shift=None, w1=w.fc, b1=w.hidden_bias(0), w2=w.proj, bias=w.proj_bg[:, :],
                out_gain=w.ln["ln1_g"][:, :], out_shift=w.ln["ln1_b"][:, :])),
            Attention(k, "d", "self", 32, "after", xx, xx, xo1, None, False, second("a1")),
            Mlp(k, "e", xo1, xx, "norm", xm, None, None, mlp("a1", 1)),
            Attention(k, "f", "cross", 32, None, xm, xm, xo2, ctx_512, True, second("a2")),
            Mlp(k, "g", xo2, xm, "route", x3, None, x2, dict(mlp("a2", 2), gate_w=w.gate_w[:, :], gate_b=w.gate_b[:, :])),
            Sort(k, sorted_in),
            Tiles(k, sorted_in, sorted_out, dict(w1=w.w1[:, :, :].rearrange("p e n -> p (e n)"),
                                                 w2=w.w2[:, :, :, :].rearrange("p e f c -> p (e f c)"), b2=w.b2)),
            Gather(k, sorted_out, x3, out, dict(gate=w.gates[:, 3:4])),
        ]
        parts[0].weights_ahead, parts[0].loaded_ahead = later, r.loaded_later
        block = stack.enter_context(nc.Block())

        def phases(eng, programs, aheads={}):
            for n, part in enumerate(parts):
                if type(part) in aheads:
                    aheads[type(part)](eng, part)
                eng.drain().then_inc(phase, 1)
                eng.wait_ge(phase, 5 * (n + 1))
                programs[type(part)](eng, part)

        def sync_phases(sp, programs, aheads):
            def ahead_of(n):
                if n < len(parts) and type(parts[n]) in aheads:
                    aheads[type(parts[n])](sp, parts[n])

            ahead_of(0)
            for n, part in enumerate(parts):
                sp.drain().then_inc(phase, 1)
                sp.wait_ge(phase, 5 * (n + 1))
                if type(part) in aheads:
                    programs[type(part)](sp, part, lambda: ahead_of(n + 1))
                else:
                    programs[type(part)](sp, part)
                    ahead_of(n + 1)

        @block.sync
        def _(sp):
            sp.wait_ge(cleared, 1)
            for dst, src in first:
                sp.dma_start(dst, src).then_inc(r.loaded_first, 16)
            sync_phases(sp, {Attention: sync_attention, Mlp: sync_mlp, Prepare: nothing, Sort: nothing,
                             Tiles: sync_tiles, Gather: sync_gather},
                        {Attention: sync_attention_ahead, Mlp: sync_mlp_ahead})

        @block.gpsimd
        def _(pool):
            made = Count(r.made)
            gpsimd_constants(pool, k, made)
            pool.wait_ge(r.made, CONSTANTS)
            parts[0].constants_ahead = lambda pool: gpsimd_later_constants(pool, k, made)
            phases(pool, {Attention: gpsimd_attention, Mlp: gpsimd_mlp, Prepare: nothing, Sort: gpsimd_sort,
                          Tiles: nothing, Gather: gpsimd_gather},
                   {Attention: lambda eng, part: gpsimd_ahead(eng, part, attention_rstd),
                    Mlp: lambda eng, part: gpsimd_ahead(eng, part, mlp_rstd)})

        @block.scalar
        def _(act):
            act.wait_ge(cleared, 1)
            act.wait_ge(r.loaded_first, 16 * len(first))
            act.activation(w.gates[:, :], w.raw_gates[:, :], ACT.Tanh).then_inc(r.gated, 1)
            phases(act, {Attention: scalar_attention, Mlp: scalar_mlp, Prepare: scalar_prepare, Sort: nothing,
                         Tiles: scalar_tiles, Gather: nothing})

        @block.tensor
        def _(pe):
            pe.wait_ge(r.loaded_first, 16 * len(first))
            pe.wait_ge(r.made, CONSTANTS)
            tensor_first(pe, k, w, r)
            phases(pe, {Attention: tensor_attention, Mlp: tensor_mlp, Prepare: tensor_prepare, Sort: tensor_sort,
                        Tiles: tensor_tiles, Gather: nothing})

        @block.vector
        def _(dve):
            dve.memset(w.first_rows[:, :], 0.0)
            dve.memset(w.later_rows[:, :], 0.0).then_inc(cleared, 1)
            dve.wait_ge(r.loaded_first, 16 * len(first))
            dve.wait_ge(r.made, CONSTANTS)
            vector_first(dve, k, w, r)
            phases(dve, {Attention: vector_attention, Mlp: vector_mlp, Prepare: vector_prepare, Sort: vector_sort,
                         Tiles: vector_tiles, Gather: vector_gather},
                   {Attention: lambda eng, part: vector_ahead(eng, part, attention_norm),
                    Mlp: lambda eng, part: vector_ahead(eng, part, mlp_norm)})


OUT = (B, S, C)


def kernel(**inputs):
    import numpy as np
    import concourse.bacc as bacc
    from concourse.bass_utils import run_bass_kernel_spmd

    nc = bacc.Bacc("TRN2", target_bir_lowering=False, num_devices=1)
    arrays, aps = {}, {}
    for name, value in inputs.items():
        a = np.ascontiguousarray(value)
        arrays[f"in_{name}"] = a
        aps[name] = nc.dram_tensor(f"in_{name}", a.shape, mybir.dt.from_np(a.dtype), kind="ExternalInput").ap()
    out = nc.dram_tensor("out", OUT, F32, kind="ExternalOutput").ap()

    def group(prefix):
        return {n[len(prefix):]: ap for n, ap in aps.items() if n.startswith(prefix)}

    network(nc, aps["x"], aps["ctx_512"], aps["g_xattn"], aps["g_ffn"], group("L0_xattn_"), group("L0_ffn_"),
            group("L1_xattn_"), group("L1_ffn_"), out)
    r = run_bass_kernel_spmd(nc, [arrays], core_ids=[0])
    return r.results[0]["out"]
```
